# Optimizing a Trainium2 kernel written in Bass

```python
import numpy as np
import jax
import jax.numpy as jnp

def _softmax(x, axis=-1):
    return jax.nn.softmax(x, axis=axis)

def _gelu(x):
    return jax.nn.gelu(x, approximate=True)

def _silu(x):
    return jax.nn.silu(x)

def _sigmoid(x):
    return jax.nn.sigmoid(x)

def _layernorm(x, axis=-1, eps=1e-05):
    m = jnp.mean(x, axis=axis, keepdims=True)
    v = jnp.var(x, axis=axis, keepdims=True)
    return (x - m) / jnp.sqrt(v + eps)

def _scatter_add(tgt, idx, src, axis=0):
    return tgt.at[idx].add(src)

def _segment_sum(src, seg, n):
    return jax.ops.segment_sum(src, seg, n)
kernel_name = 'mk_adaln_d2_jaxref_r4_da1ffc'

def setup_inputs(seed: int=0):
    np.random.seed(seed)
    _w = jnp.asarray

    def _L0_attn_setup():
        import jax, jax.numpy as jnp
        import numpy as np
        H = 4
        DK = 128
        DV = 64
        LOW_RANK = 16
        GATE_NORM = 16.0
        CHUNK = 64
        EPS = 1e-05

        def _gla_chunk(q, k, v, gk):
            B, T, _, _ = q.shape
            NC, C = (T // CHUNK, CHUNK)
            scale = DK ** (-0.5)

            def chunks(a):
                return a.reshape(B, NC, C, H, a.shape[-1]).transpose(1, 0, 3, 2, 4)
            qc, kc, vc, gc = (chunks(q), chunks(k), chunks(v), chunks(gk))
            G = jnp.cumsum(gc, axis=-2)
            qg = qc * jnp.exp(G) * scale
            k_intra = kc * jnp.exp(-G)
            kg = kc * jnp.exp(G[..., -1:, :] - G)
            g_last = jnp.exp(G[..., -1, :])
            A = jnp.einsum('nbhik,nbhjk->nbhij', qg, k_intra)
            A = jnp.where(jnp.tril(jnp.ones((C, C), bool)), A, 0.0)
            o_intra = jnp.einsum('nbhij,nbhjv->nbhiv', A, vc)

            def step(S, inp):
                qg_, kg_, v_, gl_, oi_ = inp
                o = oi_ + jnp.einsum('bhck,bhkv->bhcv', qg_, S)
                S = S * gl_[..., :, None] + jnp.einsum('bhck,bhcv->bhkv', kg_, v_)
                return (S, o)
            S0 = jnp.zeros((B, H, DK, DV), q.dtype)
            _, o = jax.lax.scan(step, S0, (qg, kg, vc, g_last, o_intra))
            return o.transpose(1, 0, 3, 2, 4).reshape(B, T, H, DV)
        key = jax.random.key(seed)
        ks = jax.random.split(key, 10)
        Dm = 256
        Kd, Vd = (H * DK, H * DV)

        def lin(k, fan_in, fan_out):
            return jax.random.normal(k, (fan_in, fan_out), jnp.float32) * fan_in ** (-0.5)
        return {'x': jax.random.normal(ks[0], (4, 512, Dm), jnp.float32), 'Wq': lin(ks[1], Dm, Kd), 'Wk': lin(ks[2], Dm, Kd), 'Wv': lin(ks[3], Dm, Vd), 'Wg': lin(ks[4], Dm, Vd), 'Wgk1': lin(ks[5], Dm, LOW_RANK), 'Wgk2': lin(ks[6], LOW_RANK, Kd), 'bgk2': jnp.zeros((Kd,), jnp.float32), 'Wo': lin(ks[7], Vd, Dm), 'gnw': jnp.ones((DV,), jnp.float32)}
    _L0_attn_in = _L0_attn_setup()

    def _L0_ffn_setup():
        import jax, jax.numpy as jnp
        import numpy as np
        D_MODEL = 256
        M = 64
        INNER = 16
        key = jax.random.key(seed)
        ks = jax.random.split(key, 9)

        def init(k, shape, fan_in):
            bound = 1.0 / np.sqrt(fan_in)
            return jax.random.uniform(k, shape, jnp.float32, -bound, bound)
        x = jax.random.normal(ks[0], (16, 1024, D_MODEL), dtype=jnp.float32)
        Win = init(ks[1], (D_MODEL, M), D_MODEL)
        bin_ = init(ks[2], (M,), D_MODEL)
        W1 = init(ks[3], (M, INNER), 1)
        b1 = init(ks[4], (M, INNER), 1)
        W2 = init(ks[5], (M, INNER), INNER)
        b2 = init(ks[6], (M,), INNER)
        Wout = init(ks[7], (M, D_MODEL), M)
        bout = init(ks[8], (D_MODEL,), M)
        return {'x': x, 'Win': Win, 'bin_': bin_, 'W1': W1, 'b1': b1, 'W2': W2, 'b2': b2, 'Wout': Wout, 'bout': bout}
    _L0_ffn_in = _L0_ffn_setup()
    _L0_c = _w((lambda *s: np.random.randn(*s).astype(np.float32) * 0.05)(2, 256))
    _L0_wmod = _w((lambda *s: np.random.randn(*s).astype(np.float32) * 0.05)(256, 6 * 256) * 256 ** (-0.5))

    def _L1_attn_setup():
        import jax, jax.numpy as jnp
        import numpy as np
        D_MODEL = 256
        D_STATE = 16
        D_CONV = 4
        EXPAND = 2
        DT_RANK = 64
        D_INNER = EXPAND * D_MODEL
        B = 2
        L = 512
        key = jax.random.key(seed)
        ks = jax.random.split(key, 8)
        g = lambda i, shape, scale: jax.random.normal(ks[i], shape, dtype=jnp.float32) * scale
        return {'hidden_states': jax.random.normal(ks[0], (B, L, D_MODEL), dtype=jnp.float32), 'in_proj_w': g(1, (2 * D_INNER, D_MODEL), 0.02), 'conv_w': g(2, (D_INNER, 1, D_CONV), 0.2), 'conv_b': jnp.zeros((D_INNER,), jnp.float32), 'x_proj_w': g(3, (DT_RANK + 2 * D_STATE, D_INNER), 0.02), 'dt_head_w': g(4, (D_INNER, DT_RANK), 0.1), 'dt_head_b': g(5, (D_INNER,), 0.1), 'out_proj_w': g(6, (D_MODEL, D_INNER), 0.02), 'D': jnp.ones((D_INNER,), jnp.float32)}
    _L1_attn_in = _L1_attn_setup()

    def _L1_ffn_setup():
        import jax, jax.numpy as jnp
        import numpy as np
        NUM_EXPERTS = 8
        EXPERT_CAPACITY = 2.0
        DIM = 256
        HIDDEN_DIM = 1024
        key = jax.random.key(seed)
        k_x, k_g, k_w1, k_w2 = jax.random.split(key, 4)
        n, t, d, f, e = (8, 256, DIM, HIDDEN_DIM, NUM_EXPERTS)
        x = jax.random.normal(k_x, (n, t, d), dtype=jnp.float32)
        gate_w = jax.random.normal(k_g, (e, d), dtype=jnp.float32) * 0.02
        w1 = jax.random.normal(k_w1, (e, d, f), dtype=jnp.float32) * 0.02
        w2 = jax.random.normal(k_w2, (e, f, d), dtype=jnp.float32) * 0.02
        return {'x': x, 'gate_w': gate_w, 'w1': w1, 'w2': w2}
    _L1_ffn_in = _L1_ffn_setup()
    _L1_c = _w((lambda *s: np.random.randn(*s).astype(np.float32) * 0.05)(2, 256))
    _L1_wmod = _w((lambda *s: np.random.randn(*s).astype(np.float32) * 0.05)(256, 6 * 256) * 256 ** (-0.5))
    _d = {'L0_attn_x': _L0_attn_in['x'], 'L0_attn_Wq': _L0_attn_in['Wq'], 'L0_attn_Wk': _L0_attn_in['Wk'], 'L0_attn_Wv': _L0_attn_in['Wv'], 'L0_attn_Wg': _L0_attn_in['Wg'], 'L0_attn_Wgk1': _L0_attn_in['Wgk1'], 'L0_attn_Wgk2': _L0_attn_in['Wgk2'], 'L0_attn_bgk2': _L0_attn_in['bgk2'], 'L0_attn_Wo': _L0_attn_in['Wo'], 'L0_attn_gnw': _L0_attn_in['gnw'], 'L0_ffn_Win': _L0_ffn_in['Win'], 'L0_ffn_bin_': _L0_ffn_in['bin_'], 'L0_ffn_W1': _L0_ffn_in['W1'], 'L0_ffn_b1': _L0_ffn_in['b1'], 'L0_ffn_W2': _L0_ffn_in['W2'], 'L0_ffn_b2': _L0_ffn_in['b2'], 'L0_ffn_Wout': _L0_ffn_in['Wout'], 'L0_ffn_bout': _L0_ffn_in['bout'], 'L0_c': _L0_c, 'L0_wmod': _L0_wmod, 'L1_attn_in_proj_w': _L1_attn_in['in_proj_w'], 'L1_attn_conv_w': _L1_attn_in['conv_w'], 'L1_attn_conv_b': _L1_attn_in['conv_b'], 'L1_attn_x_proj_w': _L1_attn_in['x_proj_w'], 'L1_attn_dt_head_w': _L1_attn_in['dt_head_w'], 'L1_attn_dt_head_b': _L1_attn_in['dt_head_b'], 'L1_attn_out_proj_w': _L1_attn_in['out_proj_w'], 'L1_attn_D': _L1_attn_in['D'], 'L1_ffn_gate_w': _L1_ffn_in['gate_w'], 'L1_ffn_w1': _L1_ffn_in['w1'], 'L1_ffn_w2': _L1_ffn_in['w2'], 'L1_c': _L1_c, 'L1_wmod': _L1_wmod}
    _x0 = _d['L0_attn_x']
    _d['L0_attn_x'] = jax.random.normal(jax.random.fold_in(jax.random.key(seed), 1), (2, 2048, 256), dtype=_x0.dtype)
    del _x0
    return _d

def reference(L0_attn_x, L0_attn_Wq, L0_attn_Wk, L0_attn_Wv, L0_attn_Wg, L0_attn_Wgk1, L0_attn_Wgk2, L0_attn_bgk2, L0_attn_Wo, L0_attn_gnw, L0_ffn_Win, L0_ffn_bin_, L0_ffn_W1, L0_ffn_b1, L0_ffn_W2, L0_ffn_b2, L0_ffn_Wout, L0_ffn_bout, L0_c, L0_wmod, L1_attn_in_proj_w, L1_attn_conv_w, L1_attn_conv_b, L1_attn_x_proj_w, L1_attn_dt_head_w, L1_attn_dt_head_b, L1_attn_out_proj_w, L1_attn_D, L1_ffn_gate_w, L1_ffn_w1, L1_ffn_w2, L1_c, L1_wmod):

    def _L0_attn_ref(x, Wq, Wk, Wv, Wg, Wgk1, Wgk2, bgk2, Wo, gnw):
        import jax, jax.numpy as jnp
        import numpy as np
        H = 4
        DK = 128
        DV = 64
        LOW_RANK = 16
        GATE_NORM = 16.0
        CHUNK = 64
        EPS = 1e-05

        def _gla_chunk(q, k, v, gk):
            B, T, _, _ = q.shape
            NC, C = (T // CHUNK, CHUNK)
            scale = DK ** (-0.5)

            def chunks(a):
                return a.reshape(B, NC, C, H, a.shape[-1]).transpose(1, 0, 3, 2, 4)
            qc, kc, vc, gc = (chunks(q), chunks(k), chunks(v), chunks(gk))
            G = jnp.cumsum(gc, axis=-2)
            qg = qc * jnp.exp(G) * scale
            k_intra = kc * jnp.exp(-G)
            kg = kc * jnp.exp(G[..., -1:, :] - G)
            g_last = jnp.exp(G[..., -1, :])
            A = jnp.einsum('nbhik,nbhjk->nbhij', qg, k_intra)
            A = jnp.where(jnp.tril(jnp.ones((C, C), bool)), A, 0.0)
            o_intra = jnp.einsum('nbhij,nbhjv->nbhiv', A, vc)

            def step(S, inp):
                qg_, kg_, v_, gl_, oi_ = inp
                o = oi_ + jnp.einsum('bhck,bhkv->bhcv', qg_, S)
                S = S * gl_[..., :, None] + jnp.einsum('bhck,bhcv->bhkv', kg_, v_)
                return (S, o)
            S0 = jnp.zeros((B, H, DK, DV), q.dtype)
            _, o = jax.lax.scan(step, S0, (qg, kg, vc, g_last, o_intra))
            return o.transpose(1, 0, 3, 2, 4).reshape(B, T, H, DV)
        B, T, Dm = x.shape
        q = (x @ Wq).reshape(B, T, H, DK)
        k = (x @ Wk).reshape(B, T, H, DK)
        v = (x @ Wv).reshape(B, T, H, DV)
        gk = jax.nn.log_sigmoid(x @ Wgk1 @ Wgk2 + bgk2) / GATE_NORM
        gk = gk.reshape(B, T, H, DK)
        o = _gla_chunk(q, k, v, gk)
        g = (x @ Wg).reshape(B, T, H, DV)
        o = o * jax.lax.rsqrt(jnp.mean(o * o, axis=-1, keepdims=True) + EPS) * gnw
        o = o * (g * jax.nn.sigmoid(g))
        return o.reshape(B, T, H * DV) @ Wo

    def _L0_ffn_ref(x, Win, bin_, W1, b1, W2, b2, Wout, bout):
        import jax, jax.numpy as jnp
        import numpy as np
        D_MODEL = 256
        M = 64
        INNER = 16
        s = jnp.einsum('btd,dm->btm', x, Win) + bin_
        h = jax.nn.relu(s[..., None] * W1 + b1)
        g = jnp.einsum('btmh,mh->btm', h, W2) + b2
        out = jnp.einsum('btm,md->btd', g, Wout) + bout
        return out

    def _L1_attn_ref(hidden_states, in_proj_w, conv_w, conv_b, x_proj_w, dt_head_w, dt_head_b, out_proj_w, D):
        import jax, jax.numpy as jnp
        import numpy as np
        D_MODEL = 256
        D_STATE = 16
        D_CONV = 4
        EXPAND = 2
        DT_RANK = 64
        D_INNER = EXPAND * D_MODEL
        B = 2
        L = 512
        Bz, Lz, _ = hidden_states.shape
        xz = hidden_states @ in_proj_w.T
        x, z = jnp.split(xz, 2, axis=-1)
        xc = jnp.transpose(x, (0, 2, 1))
        xc = jax.lax.conv_general_dilated(xc, conv_w, window_strides=(1,), padding=[(D_CONV - 1, 0)], dimension_numbers=('NCH', 'OIH', 'NCH'), feature_group_count=D_INNER) + conv_b[None, :, None]
        x = jax.nn.silu(jnp.transpose(xc, (0, 2, 1)))
        x_dbl = x @ x_proj_w.T
        dt, k, q = jnp.split(x_dbl, [DT_RANK, DT_RANK + D_STATE], axis=-1)
        dt = dt @ dt_head_w.T

        def step(state, inp):
            x_t, dt_t, k_t, q_t = inp
            dtv = jax.nn.sigmoid(dt_t + dt_head_b)
            dtv = dtv / (1.0 + dtv * jnp.sum(k_t * k_t, axis=-1, keepdims=True))
            kk = k_t * k_t
            state = state * (1.0 - dtv[..., None] * kk[:, None, :]) + (x_t * dtv)[..., None] * k_t[:, None, :]
            y_t = jnp.einsum('bdn,bn->bd', state, q_t)
            return (state, y_t)
        init = jnp.zeros((Bz, D_INNER, D_STATE), hidden_states.dtype)
        xs = (jnp.transpose(x, (1, 0, 2)), jnp.transpose(dt, (1, 0, 2)), jnp.transpose(k, (1, 0, 2)), jnp.transpose(q, (1, 0, 2)))
        _, ys = jax.lax.scan(step, init, xs)
        y = jnp.transpose(ys, (1, 0, 2)) + D * x
        y = y * jax.nn.silu(z)
        out = y @ out_proj_w.T
        return out

    def _L1_ffn_ref(x, gate_w, w1, w2):
        import jax, jax.numpy as jnp
        import numpy as np
        NUM_EXPERTS = 8
        EXPERT_CAPACITY = 2.0
        DIM = 256
        HIDDEN_DIM = 1024
        n, t, d = x.shape
        e = gate_w.shape[0]
        k = int(EXPERT_CAPACITY * t / e)
        scores = jnp.einsum('ntd,ed->nte', x, gate_w)
        probs = jax.nn.softmax(scores, axis=-1)
        g, m = jax.lax.top_k(probs.transpose(0, 2, 1), k)
        batch_idx = jnp.arange(n)[:, None, None]
        xin = x[batch_idx, m]
        h = jnp.einsum('nekd,edf->nekf', xin, w1)
        h = jax.nn.gelu(h, approximate=False)
        h = jnp.einsum('nekf,efd->nekd', h, w2)
        out_tok = g[..., None] * h
        out = jnp.zeros((n, t, d), dtype=x.dtype).at[batch_idx, m].add(out_tok)
        return out
    x = L0_attn_x
    mod = (_silu(L0_c) @ L0_wmod).reshape(L0_c.shape[0], 6, 1, -1)
    sa, ca, ga, sb, cb, gb = (mod[:, 0], mod[:, 1], mod[:, 2], mod[:, 3], mod[:, 4], mod[:, 5])
    ga = (2 * (ga >= 0) - 1) * jnp.maximum(jnp.abs(ga), 0.25)
    gb = (2 * (gb >= 0) - 1) * jnp.maximum(jnp.abs(gb), 0.25)
    h = _layernorm(x, axis=-1) * (1 + ca) + sa
    x = x + ga * _L0_attn_ref(h, L0_attn_Wq, L0_attn_Wk, L0_attn_Wv, L0_attn_Wg, L0_attn_Wgk1, L0_attn_Wgk2, L0_attn_bgk2, L0_attn_Wo, L0_attn_gnw)
    h = _layernorm(x, axis=-1) * (1 + cb) + sb
    x = x + gb * _L0_ffn_ref(h, L0_ffn_Win, L0_ffn_bin_, L0_ffn_W1, L0_ffn_b1, L0_ffn_W2, L0_ffn_b2, L0_ffn_Wout, L0_ffn_bout)
    mod = (_silu(L1_c) @ L1_wmod).reshape(L1_c.shape[0], 6, 1, -1)
    sa, ca, ga, sb, cb, gb = (mod[:, 0], mod[:, 1], mod[:, 2], mod[:, 3], mod[:, 4], mod[:, 5])
    ga = (2 * (ga >= 0) - 1) * jnp.maximum(jnp.abs(ga), 0.25)
    gb = (2 * (gb >= 0) - 1) * jnp.maximum(jnp.abs(gb), 0.25)
    h = _layernorm(x, axis=-1) * (1 + ca) + sa
    x = x + ga * _L1_attn_ref(h, L1_attn_in_proj_w, L1_attn_conv_w, L1_attn_conv_b, L1_attn_x_proj_w, L1_attn_dt_head_w, L1_attn_dt_head_b, L1_attn_out_proj_w, L1_attn_D)
    h = _layernorm(x, axis=-1) * (1 + cb) + sb
    x = x + gb * _L1_ffn_ref(h, L1_ffn_gate_w, L1_ffn_w1, L1_ffn_w2)
    return x

_drawn_inputs = setup_inputs


def setup_inputs(seed=0):
    import zlib

    import numpy as np

    out = dict(_drawn_inputs(seed))
    spreads = {'L0_attn_bgk2': (0.0, 2.0),
     'L0_attn_gnw': (1.0, 0.2),
     'L1_attn_conv_b': (0.0, 0.8),
     'L1_attn_D': (1.0, 0.6)}
    factors = {'L0_attn_Wgk1': 3.568,
     'L0_attn_Wgk2': 3.501,
     'L0_ffn_Win': 3.428,
     'L0_ffn_bin_': 8.0,
     'L0_ffn_W1': 3.38,
     'L0_ffn_bout': 3.26,
     'L1_attn_in_proj_w': 8.0,
     'L1_attn_conv_w': 8.0,
     'L1_attn_x_proj_w': 8.0,
     'L1_attn_dt_head_w': 8.0,
     'L1_attn_dt_head_b': 43.782,
     'L1_attn_out_proj_w': 8.0,
     'L1_ffn_gate_w': 8.0,
     'L1_ffn_w1': 8.0,
     'L1_ffn_w2': 8.0,
     'L1_c': 7.472,
     'L1_wmod': 7.565}
    for name, (base, spread) in spreads.items():
        noise = np.random.default_rng([zlib.crc32(name.encode()), seed]).standard_normal(out[name].shape)
        drawn = base * np.exp(spread * noise) if base else spread * noise
        out[name] = jnp.asarray(drawn.astype(out[name].dtype))
    for name, factor in factors.items():
        out[name] = (out[name] * factor).astype(out[name].dtype)
    return out
```

```python
from contextlib import ExitStack

import numpy as np
import concourse.bass as bass
from concourse import mybir

F32 = mybir.dt.float32
BF16 = mybir.dt.bfloat16
U32 = mybir.dt.uint32
I32 = mybir.dt.int32
ALU = mybir.AluOpType
ACT = mybir.ActivationFunctionType
AX_X = mybir.AxisListType.X

P = 128
B, T, D = 2, 2048, 256
DC = D // P
TB = 256
NB = B * T // TB
BPB = T // TB
NT = TB // P
H, DK, DV, LR = 4, 128, 64, 16
CH = 64
NCH = TB // CH
GN = 16.0
FM, FI = 64, 16
FJ = FI // 2
DI, DS, DR, DCV = 512, 16, 64, 4
DT = DI // P
E, F = 8, 1024
K = 2 * T // E
NL = B * E
TT = T // P
SL = K // P
FT = F // P
BITS = 30
EPS = 1e-5


PER_BLOCK = dict(
    x_in=16, x_out=16, rows_out=16, x_attn=1, x_ffn=1, x_scan=1,
    turn_a=1, turn_b=1, turn_c=1, turn_d=1, hT_a=DC, hT_b=DC, hT_c=DC, hT_d=DC,
    low_rank=1, lr=1, z=2, z_read=8, z_exp=1, z_ln=1, lz_sum=1, cumsum=1, to_end=1, eG=1, emG=1, eD=1,
    v_mm=1, v_s=1, g_mm=1, sg=1, q_mm=2, k_mm=2, qg=2, kg=2, kgt_mm=2, kgt=2, att_mm=2, att=2, kv_mm=2,
    state0=1, state=NCH * H, o_mm=1, o_s=1, o_sq=1, ms_mm=1, ms_ln=1, rms=1, o_n=1, og=1, wo_mm=1,
    win_mm=1, ffn_s=1, relu=FJ, facc=FJ, wout_mm=1,
    halo=1, in_mm=4, x_cp=2, sz=2, tail=1, conv=DCV * DT, xs=1, dkq_mm=1, dkq=2, squares=1, parts=5,
    dt_mm=2, dt_sig=DT, ksum_mm=1, ksum=1, s_ksum=1, den_ln=1, den=1, dtv=1, u=1,
    k_rows=DS, q_mm2=DS // 2, q_rows=DS // 2, rate=DS, decay=DS, inp=DS, scanned=DS, saved=DS,
    read_out=DS, summed=DS, yz=1, out_mm=1, score_mm=1, scores=1)
PER_BLOCK.update({f"ln{n}_{what}": 1 for n in "abcd" for what in ("stats", "aggr", "var", "rstd", "rows")})
PER_TURN = dict(gt_mm=4 * DC, hg=4 * DC, up_mm=4 * FT, gelu=4 * FT, down_mm=4 * SL, scaled=4 * SL,
                w1_in0=16, w1_in1=16, w2_in0=16, w2_in1=16)


def shape_constants():
    p = np.arange(P)
    c = {}
    c["ident"] = np.eye(P)
    c["ones"] = np.ones((P, P))
    c["headones"] = (p[:, None] // DV == p[None, :] // DV) * 1.0
    c["before"] = (p[:, None] < p[None, :]) * 1.0
    i = np.arange(P)
    causal = (p[:, None] <= i[None, :]) & (p[:, None] // CH == i[None, :] // CH)
    c["causal"] = np.tile(causal * 1.0, (1, 4))
    c["chunkrun"] = np.tile((np.arange(H * TB) % CH != 0) * 1.0, (P, 1))
    c["tilerun"] = np.tile((np.arange(NL * TT) % TT != 0) * 1.0, (P, 1))
    r = np.arange(P)
    sel = ((r[:, None] % 32 == np.arange(32)[None, :]) & (r[:, None] < 96)) * 1.0
    c["sel"] = np.repeat(sel, P, axis=1)
    c["selk"] = np.repeat(((r % 32 < DS) & (r < 96))[:, None] * 1.0, P, axis=1)
    c["iota"] = np.tile(i, (P, 1))
    lt = np.arange(NL * TT)
    c["token"] = (lt[None, :] // TT // E) * T + (lt[None, :] % TT) * P + p[:, None]
    c["bitsf"] = np.tile(2.0 ** np.arange(BITS - 1, -1, -1), (P, 1))
    return {k: np.ascontiguousarray(v, dtype=np.float32) for k, v in c.items()}


def layout(sizes):
    at, off = {}, 0
    for name, w in sizes:
        at[name] = (off, w)
        off += w
    return at, off


CONST_SIZES = [("ident", P), ("ones", P), ("headones", P), ("before", P), ("causal", 4 * P),
               ("chunkrun", H * TB), ("tilerun", NL * TT), ("sel", 32 * P), ("selk", P), ("iota", P),
               ("token", NL * TT), ("bitsf", BITS)]
WEIGHT_SIZES = [("wq", DC * H * DK), ("wk", DC * H * DK), ("wv", DC * H * DV), ("wg", DC * H * DV),
                ("wgk1", DC * LR), ("wgk2", H * DK), ("win2", DC * P), ("inproj", DC * 2 * DI),
                ("xproj", DT * (DR + 2 * DS)), ("dthead", DI), ("gate", DC * E),
                ("bgk2", H), ("bin", 1), ("w1", FJ), ("b1", FJ), ("w2", FJ), ("b2", 1),
                ("convw", DT * DCV), ("convb", DT), ("dtb", DT), ("dskip", DT), ("gnw", 1)]
FOLD_SIZES = [("wo", DC * D), ("wout2", D), ("bout", D), ("outproj", DT * D), ("c0", DC * B), ("c1", DC * B)]
CONST_AT, CONST_W = layout(CONST_SIZES)
WEIGHT_AT, WEIGHT_W = layout(WEIGHT_SIZES)
FOLD_AT, FOLD_W = layout(FOLD_SIZES)


def build(nc, x_in, consts, weights, folds, wmod0, wmod1, w1_d, w2_d, out):
    xn_d = nc.dram_tensor("xn_rows", (B * T, D), F32, kind="Internal").ap()
    x_rows = x_in.rearrange("b t d -> (b t) d")
    out_rows = out.rearrange("b t d -> (b t) d")
    with ExitStack() as top:
        def keep(name, shape, dt=F32):
            return top.enter_context(nc.sbuf_tensor(name, shape, dt))

        names = {}

        def sem(name):
            if name not in names:
                names[name] = top.enter_context(nc.semaphore(name))
            return names[name]

        scores = keep("scores", [P, B * TT * E])
        ones_s = keep("ones_s", [P, P])
        ident_s = keep("ident_s", [P, P])
        col1 = keep("col1", [P, 6 * DC * B])
        gb1 = keep("gb1", [P, B * D])
        layers(nc, sem, x_rows, consts, weights, folds, wmod0, wmod1, out_rows, xn_d,
               scores, ones_s, ident_s, col1, gb1)
        experts(nc, sem, consts, w1_d, w2_d, out_rows, xn_d, scores, ones_s, ident_s, col1, gb1)


def layers(nc, sem, x_rows, consts, weights, folds, wmod0, wmod1, out_rows, xn_d,
           scores, ones_s, ident_s, col1, gb1):
    with ExitStack() as ctx:
        def sb(name, shape, dt=F32):
            return ctx.enter_context(nc.sbuf_tensor(name, shape, dt))

        def ps(name, shape, dt=F32):
            return ctx.enter_context(nc.psum_tensor(name, shape, dt))

        W = sb("W", [P, WEIGHT_W])

        def w(name):
            a, n = WEIGHT_AT[name]
            return W[:, a:a + n]

        def cols(name, n):
            return w(name).rearrange("p (c n) -> p c n", n=n)

        headones = sb("headones", [P, P])
        causal = sb("causal", [P, 4 * P], mybir.dt.uint8)
        chunkrun = sb("chunkrun", [P, H * TB])
        sel = sb("sel", [96, 32, P], BF16)
        selk = sb("selk", [96, P], BF16)
        epst = sb("epst", [P, 1])
        expo = sb("expo", [P, NT])
        wo_g = sb("wo_g", [P, B, DC, D])
        wout_g = sb("wout_g", [P, B, D])
        bout_g = sb("bout_g", [1, B, D])
        oproj_g = sb("oproj_g", [P, B, DT, D])
        dskip = sb("dskip", [P, DT, P])
        col0 = sb("col0", [P, 6 * DC * B])
        b1s = sb("b1s", [P, FJ])
        nbgk = sb("nbgk", [P, H])

        wq, wk = cols("wq", H * DK), cols("wk", H * DK)
        wv, wg = cols("wv", H * DV), cols("wg", H * DV)
        wgk1, wgk2 = cols("wgk1", LR), w("wgk2")
        win2, inproj = cols("win2", P), cols("inproj", 2 * DI)
        xproj, dthead, gate = cols("xproj", DR + 2 * DS), w("dthead"), cols("gate", E)

        def modcol(col, what, c, b):
            return col[:, bass.ds((what * DC + c) * B + b, 1)]

        with ExitStack() as pre:
            def tsb(name, shape, dt=F32):
                return pre.enter_context(nc.sbuf_tensor(name, shape, dt))

            cst = tsb("cst", [P, CONST_W])
            fold = tsb("fold", [P, FOLD_W])
            wmod = tsb("wmod", [P, 2, DC, 6 * D])
            silc = tsb("silc", [P, 2, DC * B])
            silr = tsb("silr", [P, 2, B, DC, P])
            gabs = tsb("gabs", [P, 4, B * D])
            gsig = tsb("gsig", [P, 4, B * D])
            gmul = tsb("gmul", [P, 3, B * D])
            wo_n = tsb("wo_n", [P, DC, D])
            pcol = pre.enter_context(nc.psum_tensor("pcol", [P, 2, 512], F32))
            prow = pre.enter_context(nc.psum_tensor("prow", [P, 4, 512], F32))

            def cs(name):
                a, n = CONST_AT[name]
                return cst[:, a:a + n]

            def fo(name):
                a, n = FOLD_AT[name]
                return fold[:, a:a + n]

            with nc.Block() as block:
                @block.sync
                def _(sp):
                    sp.dma_start(fold[:, :], folds).then_inc(sem("fold_in"), 16)
                    sp.dma_start(wmod[:, 0], wmod0.rearrange("(c p) n -> p c n", p=P)).then_inc(sem("wmod0_in"), 16)
                    sp.dma_start(cst[:, :], consts).then_inc(sem("const_in"), 16)
                    sp.dma_start(W[:, :], weights).then_inc(sem("weights_in"), 16)
                    sp.wait_ge(sem("weights_in"), 16)

                @block.scalar
                def _(act):
                    act.dma_start(wmod[:, 1], wmod1.rearrange("(c p) n -> p c n", p=P)).then_inc(sem("wmod1_in"), 16)
                    act.wait_ge(sem("fold_in"), 16)
                    for n in range(2):
                        act.activation(silc[:, n, :], fo(f"c{n}"), ACT.Silu).then_inc(sem("silc"), 1)
                    for g in range(4):
                        act.wait_ge(sem("rows"), g + 1)
                        act.activation(gabs[:, g, :], prow[:, g, :], ACT.Abs).then_inc(sem("gabs"), 1)

                @block.gpsimd
                def _(pool):
                    for name, n in (PER_BLOCK | PER_TURN).items():
                        pool.sem_inc(sem(name), n)

                @block.tensor
                def _(pe):
                    pe.wait_ge(sem("silc"), 2)
                    pe.wait_ge(sem("wmod0_in"), 16)
                    for n in range(2):
                        if n == 1:
                            pe.wait_ge(sem("wmod1_in"), 16)
                        for m in range(6 * DC):
                            for c in range(DC):
                                last = pe.matmul(pcol[:, n, m * B:(m + 1) * B], wmod[:, n, c, m * P:(m + 1) * P],
                                                 silc[:, n, c * B:(c + 1) * B], start=(c == 0), stop=(c == DC - 1))
                        last.then_inc(sem("modcols"), 1)
                    pe.wait_ge(sem("silr"), 2 * B * DC)
                    for n in range(2):
                        for g in range(2):
                            what = 2 + 3 * g
                            for b in range(B):
                                for c in range(DC):
                                    last = pe.matmul(prow[:, 2 * n + g, b * D:(b + 1) * D], silr[:, n, b, c, :],
                                                     wmod[:, n, c, what * D:(what + 1) * D],
                                                     start=(c == 0), stop=(c == DC - 1))
                            last.then_inc(sem("rows"), 1)

                @block.vector
                def _(dve):
                    dve.memset(epst[:, :], EPS)
                    dve.memset(expo[:, :], -0.5)
                    dve.wait_ge(sem("const_in"), 16)
                    dve.wait_ge(sem("silc"), 2)
                    for n in range(2):
                        for b in range(B):
                            for c in range(DC):
                                dve.tensor_scalar(silr[:, n, b, c, :], cs("ones"), silc[:, n, c * B + b:c * B + b + 1],
                                                  None, ALU.mult).then_inc(sem("silr"), 1)
                    dve.tensor_copy(headones[:, :], cs("headones"))
                    dve.tensor_copy(ones_s[:, :], cs("ones"))
                    dve.tensor_copy(ident_s[:, :], cs("ident"))
                    dve.tensor_copy(causal[:, :], cs("causal"))
                    dve.tensor_copy(chunkrun[:, :], cs("chunkrun"))
                    dve.tensor_copy(sel[:, :, :].rearrange("p a b -> p (a b)"), cs("sel")[0:96])
                    dve.tensor_copy(selk[:, :], cs("selk")[0:96])
                    for n, col in enumerate((col0, col1)):
                        dve.wait_ge(sem("modcols"), n + 1)
                        dve.tensor_copy(col[:, :], pcol[:, n, 0:6 * DC * B]).then_inc(sem("col"), 1)
                    dve.wait_ge(sem("col"), 2)
                    for col in (col0, col1):
                        for what in (1, 4):
                            v = col[:, what * DC * B:(what + 1) * DC * B]
                            dve.tensor_scalar(v, v, 1.0, None, ALU.add)
                    for g in range(4):
                        dve.wait_ge(sem("gabs"), g + 1)
                        dve.tensor_scalar(gsig[:, g, :], prow[:, g, :], 0.0, 2.0, ALU.is_ge, ALU.mult)\
                            .then_inc(sem("gsig"), 1)
                        dve.tensor_scalar(gabs[:, g, :], gabs[:, g, :], 0.25, None, ALU.max).then_inc(sem("gsig"), 1)
                        dve.wait_ge(sem("gsig"), 2 * g + 2)
                        to = gmul[:, g, :] if g < 3 else gb1[:, :]
                        dve.scalar_tensor_tensor(to, gsig[:, g, :], -1.0, gabs[:, g, :], ALU.add, ALU.mult)\
                            .then_inc(sem("gates"), 1)
                    dve.wait_ge(sem("gates"), 4)
                    dve.wait_ge(sem("weights_in"), 16)
                    dve.tensor_scalar(wo_n[:, :, :].rearrange("p c n -> p (c n)"), fo("wo"), w("gnw"), None, ALU.mult)\
                        .then_inc(sem("wo_n"), 1)
                    dve.wait_ge(sem("wo_n"), 1)
                    for b in range(B):
                        ga0, gb0, ga1 = (gmul[:, g, b * D:(b + 1) * D] for g in range(3))
                        for c in range(DC):
                            dve.tensor_tensor(wo_g[:, b, c, :], wo_n[:, c, :], ga0, ALU.mult)
                        dve.tensor_tensor(wout_g[:, b, :], fo("wout2"), gb0, ALU.mult)
                        dve.tensor_tensor(bout_g[0:1, b, :], fo("bout")[0:1], gb0[0:1], ALU.mult)
                        for k in range(DT):
                            dve.tensor_tensor(oproj_g[:, b, k, :], fo("outproj")[:, k * D:(k + 1) * D], ga1, ALU.mult)
                    for k in range(DT):
                        dve.tensor_scalar(dskip[:, k, :], cs("ident"), w("dskip")[:, k:k + 1], None, ALU.mult)
                    dve.scalar_tensor_tensor(b1s[:, :], w("w1"), w("bin"), w("b1"), ALU.mult, ALU.add)
                    dve.tensor_scalar(nbgk[:, :], w("bgk2"), -1.0, None, ALU.mult)

        xt = sb("xt", [P, 2 * NT * D])
        stat = {n: sb(f"stat_{n}", [P, NT, 6]) for n in "abcd"}
        mv = {n: sb(f"mv_{n}", [P, NT, 2]) for n in "abcd"}
        ve = {n: sb(f"ve_{n}", [P, NT]) for n in "abcd"}
        rstd = {n: sb(f"rstd_{n}", [P, NT]) for n in "abcd"}
        xn = sb("xn", [P, NT, D])
        hT = sb("hT", [P, DC, TB])
        lr = sb("lr", [LR, TB])
        lz = sb("lz", [P, H * TB])
        rz = sb("rz", [P, H * TB])
        eG = sb("eG", [P, H, TB])
        emG = sb("emG", [P, H, TB])
        eD = sb("eD", [P, H, TB])
        qg = sb("qg", [P, H, TB])
        kin = sb("kin", [P, H, TB])
        kg = sb("kg", [P, H, TB])
        v = sb("v", [P, NT, H * DV])
        vh = sb("vh", [P, NT, 2, H * DV])
        sg = sb("sg", [P, DC, TB])
        kgt = sb("kgt", [P, NT, H, DK])
        att = sb("att", [P, NT, H, P])
        S = sb("S", [P, 2 + NCH, H * DV])
        o_s = sb("o_s", [P, DC, TB])
        o_q = sb("o_q", [P, DC, TB])
        rms = sb("rms", [P, DC * TB])
        og = sb("og", [P, DC, TB])
        s_f = sb("s_f", [P, TB])
        rel = sb("rel", [P, 4, TB])
        facc = sb("facc", [P, TB])

        xnB = sb("xnB", [P, NT, D])
        hB = sb("hB", [P, DC, TB])
        xraw = sb("xraw", [P, DT, TB + DCV - 1])
        tail = sb("tail", [P, 2 * DT * (DCV - 1)])
        xs = sb("xs", [P, DT, TB])
        sz = sb("sz", [P, DT, TB])
        dtl = sb("dtl", [DR, TB])
        kx = sb("kx", [32, 2, TB])
        kr = sb("kr", [32, 2, TB])
        km = sb("km", [32, 2, TB], BF16)
        k3 = sb("k3", [96, 2, TB], BF16)
        ksum = sb("ksum", [P, TB])
        dtv = sb("dtv", [P, DT, TB])
        tmp = sb("tmp", [P, DT, TB])
        u = sb("u", [P, DT, TB])
        dec = sb("dec", [P, 2, DT, TB])
        st = sb("st", [P, 3, DT, TB])
        qb = sb("qb", [P, 2, 2 * TB])
        last = sb("last", [P, 2 * DS * DT])
        xo = sb("xo", [P, NT, D])
        xnC = sb("xnC", [P, NT, D])
        hC = hB

        pA = [ps(f"pA{i}", [P, 512]) for i in range(2)]
        pB = ps("pB", [P, 512])
        pK = [ps(f"pK{i}", [P, 512]) for i in range(2)]
        pQ = ps("pQ", [P, 512])
        pY = ps("pY", [P, DT, TB])

        def batch(it):
            return (it - 1) // BPB

        def later(it):
            return ((it - 1) % BPB + BPB - 1) // BPB

        def x_at(it, t, n=1):
            return xt[:, bass.ds((it % 2) * (NT * D) + t * D, n * D)]

        def settled(dve):
            dve.wait_ge(sem("weights_in"), 16)

        def ln_vector(dve, it, n, src, dst):
            for t in range(NT):
                i = dve.bn_stats(stat[n][:, t, :], src(t))
            i.then_inc(sem(f"ln{n}_stats"), 1)
            settled(dve)
            dve.wait_ge(sem(f"ln{n}_stats"), it + 1)
            for t in range(NT):
                i = dve.bn_aggr(mv[n][:, t, :], stat[n][:, t, :])
            i.then_inc(sem(f"ln{n}_aggr"), 1)
            dve.wait_ge(sem(f"ln{n}_aggr"), it + 1)
            dve.tensor_scalar(ve[n][:, :], mv[n][:, :, 1], EPS, None, ALU.add).then_inc(sem(f"ln{n}_var"), 1)
            dve.wait_ge(sem(f"ln{n}_rstd"), it + 1)
            for t in range(NT):
                i = dve.tensor_scalar(dst[:, t, :], src(t), mv[n][:, t, 0:1], rstd[n][:, t:t + 1],
                                      ALU.subtract, ALU.mult)
            i.then_inc(sem(f"ln{n}_rows"), 1)

        def ln_pool(pool, it, n):
            pool.wait_ge(sem(f"ln{n}_var"), it + 1)
            pool.tensor_tensor(rstd[n][:, :], ve[n][:, :], expo[:, :], ALU.pow).then_inc(sem(f"ln{n}_rstd"), 1)

        def turn(pe, it, n, rows, bank, done):
            pe.wait_ge(sem(f"ln{n}_rows"), it + 1)
            for c in range(DC):
                for t in range(NT):
                    i = pe.transpose(bank[:, c * TB + t * P:c * TB + (t + 1) * P], rows[:, t, c * P:(c + 1) * P],
                                     ident_s[:, :])
            i.then_inc(sem(done), 1)

        def modulate(act, it, b, bank, col, scale, shift, dst, ready, done):
            act.wait_ge(sem(ready), it + 1)
            for c in range(DC):
                act.activation(dst[:, c, :], bank[:, c * TB:(c + 1) * TB], ACT.Identity,
                               bias=modcol(col, shift, c, b), scale=modcol(col, scale, c, b)).then_inc(sem(done), 1)

        def A_pe(pe, it, b):
            pe.wait_ge(sem("ffn_s"), it)
            turn(pe, it, "a", xn, pA[0], "turn_a")
            pe.wait_ge(sem("x_ffn"), it)
            pe.wait_ge(sem("hT_a"), (it + 1) * DC)
            for c in range(DC):
                i = pe.matmul(pA[1][0:LR, 0:TB], wgk1[:, c, :], hT[:, c, :], start=(c == 0), stop=(c == DC - 1))
            i.then_inc(sem("low_rank"), 1)
            pe.wait_ge(sem("lr"), it + 1)
            for hp in range(2):
                for h2 in range(2):
                    h = 2 * hp + h2
                    i = pe.matmul(pA[hp][:, h2 * TB:(h2 + 1) * TB], wgk2[0:LR, h * DK:(h + 1) * DK], lr[:, :],
                                  start=True, stop=True)
                i.then_inc(sem("z"), 1)
            pe.wait_ge(sem("z_read"), it * 8 + 4)
            for t in range(NT):
                for c in range(DC):
                    i = pe.matmul(pA[0][:, t * D:(t + 1) * D], hT[:, c, t * P:(t + 1) * P], wv[:, c, :],
                                  start=(c == 0), stop=(c == DC - 1))
            i.then_inc(sem("v_mm"), 1)
            pe.wait_ge(sem("z_read"), it * 8 + 8)
            for m in range(DC):
                for c in range(DC):
                    i = pe.matmul(pA[1][:, m * TB:(m + 1) * TB], wg[:, c, m * P:(m + 1) * P], hT[:, c, :],
                                  start=(c == 0), stop=(c == DC - 1))
            i.then_inc(sem("g_mm"), 1)
            for hp in range(2):
                heads = (2 * hp, 2 * hp + 1)
                for n, (wt, ready) in enumerate(((wq, "q_mm"), (wk, "k_mm"))):
                    if hp == 0:
                        pe.wait_ge(sem("v_s") if n == 0 else sem("sg"), it + 1)
                    else:
                        pe.wait_ge(sem("att") if n == 0 else sem("state"), it * 2 + 1 if n == 0 else it * 16 + 8)
                    bank = pA[n] if hp == 0 else pA[1 - n]
                    for h2, h in enumerate(heads):
                        for c in range(DC):
                            i = pe.matmul(bank[:, h2 * TB:(h2 + 1) * TB], wt[:, c, h * DK:(h + 1) * DK], hT[:, c, :],
                                          start=(c == 0), stop=(c == DC - 1))
                    i.then_inc(sem(ready), 1)
                bank = pA[hp]
                pe.wait_ge(sem("kg"), it * 2 + hp + 1)
                pe.wait_ge(sem("qg"), it * 2 + hp + 1)
                for t in range(NT):
                    for h2, h in enumerate(heads):
                        i = pe.transpose(bank[:, (t * 2 + h2) * P:(t * 2 + h2 + 1) * P], kg[:, h, t * P:(t + 1) * P],
                                         ident_s[:, :])
                i.then_inc(sem("kgt_mm"), 1)
                bank = pA[1 - hp]
                for t in range(NT):
                    for h2, h in enumerate(heads):
                        i = pe.matmul(bank[:, (t * 2 + h2) * P:(t * 2 + h2 + 1) * P], kin[:, h, t * P:(t + 1) * P],
                                      qg[:, h, t * P:(t + 1) * P], start=True, stop=True)
                i.then_inc(sem("att_mm"), 1)
                bank = pA[hp]
                pe.wait_ge(sem("kgt"), it * 2 + hp + 1)
                for t in range(NT):
                    for h2, h in enumerate(heads):
                        i = pe.matmul(bank[:, :].rearrange("p (c h n) -> p c h n", h=2, n=DV)[:, 2 * t:2 * t + 2, h2, :],
                                      kgt[:, t, h, :], vh[:, t, :, h * DV:(h + 1) * DV], start=True, stop=True)
                i.then_inc(sem("kv_mm"), 1)
            pe.wait_ge(sem("att"), it * 2 + 2)
            pe.wait_ge(sem("state"), it * 16 + 16)
            for h in range(H):
                hp, h2 = h // 2, h % 2
                for t in range(NT):
                    o = pA[0][h2 * DV:(h2 + 1) * DV, hp * TB + t * P:hp * TB + (t + 1) * P]
                    pe.matmul(o, v[:, t, h * DV:(h + 1) * DV], att[:, t, h, :], start=True, stop=False,
                              skip_group_check=True)
                    for c in (2 * t, 2 * t + 1):
                        i = pe.matmul(o[:, (c % 2) * CH:(c % 2 + 1) * CH], S[:, 1 + c, h * DV:(h + 1) * DV],
                                      qg[:, h, c * CH:(c + 1) * CH], start=False, stop=(c % 2 == 1),
                                      skip_group_check=True)
            i.then_inc(sem("o_mm"), 1)
            pe.wait_ge(sem("o_sq"), it + 1)
            pe.matmul(pA[1][:, :], headones[:, :], o_q[:, :, :].rearrange("p c t -> p (c t)"), start=True, stop=True)\
                .then_inc(sem("ms_mm"), 1)
            pe.wait_ge(sem("og"), it + 1)
            for t in range(NT):
                for c in range(DC):
                    i = pe.matmul(pA[0][:, t * D:(t + 1) * D], og[:, c, t * P:(t + 1) * P],
                                  wo_g[:, :, :, :].rearrange("p b c n -> p (b c n)")[:, bass.ds((b * DC + c) * D, D)],
                                  start=(c == 0), stop=(c == DC - 1))
            i.then_inc(sem("wo_mm"), 1)
            turn(pe, it, "b", xn, pA[1], "turn_b")
            pe.wait_ge(sem("hT_b"), (it + 1) * DC)
            for c in range(DC):
                i = pe.matmul(pA[0][:, 0:TB], win2[:, c, :], hT[:, c, :], start=(c == 0), stop=(c == DC - 1))
            i.then_inc(sem("win_mm"), 1)
            pe.wait_ge(sem("facc"), (it + 1) * FJ)
            for t in range(NT):
                pe.matmul(pA[1][:, t * D:(t + 1) * D], ones_s[0:1, :],
                          bout_g[:, :, :].rearrange("p b n -> p (b n)")[:, bass.ds(b * D, D)], start=True, stop=False)
                i = pe.matmul(pA[1][:, t * D:(t + 1) * D], facc[:, t * P:(t + 1) * P],
                              wout_g[:, :, :].rearrange("p b n -> p (b n)")[:, bass.ds(b * D, D)],
                              start=False, stop=True)
            i.then_inc(sem("wout_mm"), 1)

        def A_act(act, it, b):
            modulate(act, it, b, pA[0], col0, 1, 0, hT, "turn_a", "hT_a")
            act.wait_ge(sem("low_rank"), it + 1)
            act.activation(lr[:, :], pA[1][0:LR, 0:TB], ACT.Copy).then_inc(sem("lr"), 1)
            for hp in range(2):
                act.wait_ge(sem("z"), it * 2 + hp + 1)
                for h2 in range(2):
                    h = 2 * hp + h2
                    z = pA[hp][:, h2 * TB:(h2 + 1) * TB]
                    act.activation(lz[:, h * TB:(h + 1) * TB], z, ACT.Abs, bias=w("bgk2")[:, h:h + 1])\
                        .then_inc(sem("z_read"), 1)
                    act.activation(rz[:, h * TB:(h + 1) * TB], z, ACT.Relu, bias=nbgk[:, h:h + 1], scale=-1.0)\
                        .then_inc(sem("z_read"), 1)
            act.wait_ge(sem("tail0"), 2)
            act.wait_ge(sem("v_mm"), it + 1)
            act.activation(v[:, :, :].rearrange("p t n -> p (t n)"), pA[0][:, :], ACT.Copy)
            for half in range(2):
                r = slice(half * CH, (half + 1) * CH)
                i = act.activation(vh[r, :, half, :], pA[0][r, :].rearrange("p (t n) -> p t n", t=NT), ACT.Copy)
            i.then_inc(sem("v_s"), 1)
            act.wait_ge(sem("z_read"), it * 8 + 8)
            act.activation(lz[:, :], lz[:, :], ACT.Exp, scale=-1.0).then_inc(sem("z_exp"), 1)
            act.wait_ge(sem("z_exp"), it + 1)
            act.activation(lz[:, :], lz[:, :], ACT.Ln, bias=ones_s[:, 0:1]).then_inc(sem("z_ln"), 1)
            act.wait_ge(sem("g_mm"), it + 1)
            act.activation(sg[:, :, :].rearrange("p c t -> p (c t)"), pA[1][:, :], ACT.Silu).then_inc(sem("sg"), 1)
            act.wait_ge(sem("cumsum"), it + 1)
            act.activation(eG[:, :, :].rearrange("p h t -> p (h t)"), lz[:, :], ACT.Exp, scale=-1.0 / GN)\
                .then_inc(sem("eG"), 1)
            act.activation(emG[:, :, :].rearrange("p h t -> p (h t)"), lz[:, :], ACT.Exp, scale=1.0 / GN)\
                .then_inc(sem("emG"), 1)
            act.wait_ge(sem("to_end"), it + 1)
            act.activation(eD[:, :, :].rearrange("p h t -> p (h t)"), rz[:, :], ACT.Exp, scale=1.0 / GN)\
                .then_inc(sem("eD"), 1)
            for hp in range(2):
                act.wait_ge(sem("kgt_mm"), it * 2 + hp + 1)
                act.activation(kgt[:, :, 2 * hp:2 * hp + 2, :],
                               pA[hp][:, :].rearrange("p (t h n) -> p t h n", t=NT, h=2), ACT.Copy)\
                    .then_inc(sem("kgt"), 1)
            act.wait_ge(sem("o_mm"), it + 1)
            act.activation(o_s[:, :, :].rearrange("p c t -> p (c t)"), pA[0][:, :], ACT.Copy).then_inc(sem("o_s"), 1)
            act.activation(o_q[:, :, :].rearrange("p c t -> p (c t)"), pA[0][:, :], ACT.Square).then_inc(sem("o_sq"), 1)
            act.wait_ge(sem("ms_mm"), it + 1)
            act.activation(rms[:, :], pA[1][:, :], ACT.Ln, bias=epst[:, :], scale=1.0 / DV).then_inc(sem("ms_ln"), 1)
            act.wait_ge(sem("ms_ln"), it + 1)
            act.activation(rms[:, :], rms[:, :], ACT.Exp, scale=-0.5).then_inc(sem("rms"), 1)
            modulate(act, it, b, pA[1], col0, 4, 3, hT, "turn_b", "hT_b")
            act.wait_ge(sem("win_mm"), it + 1)
            act.activation(s_f[:, :], pA[0][:, 0:TB], ACT.Copy).then_inc(sem("ffn_s"), 1)
            act.wait_ge(sem("ffn_s"), it + 1)
            for jj in range(FJ):
                if jj >= 4:
                    act.wait_ge(sem("facc"), it * FJ + jj - 3)
                act.activation(rel[:, jj % 4, :], s_f[:, :], ACT.Relu, bias=b1s[:, jj:jj + 1],
                               scale=w("w1")[:, jj:jj + 1]).then_inc(sem("relu"), 1)

        def A_dve(dve, it, b):
            settled(dve)
            dve.wait_ge(sem("x_in"), (it + 1) * 16)
            ln_vector(dve, it, "a", lambda t: x_at(it, t), xn)
            dve.wait_ge(sem("lz_sum"), it + 1)
            dve.tensor_tensor_scan(lz[:, :], chunkrun[:, :], lz[:, :], 0.0, ALU.mult, ALU.add)\
                .then_inc(sem("cumsum"), 1)
            dve.wait_ge(sem("state"), it * 16)
            dve.wait_ge(sem("o_mm"), it)
            Sf = S[:, :, :].rearrange("p c n -> p (c n)")
            dve.tensor_copy(S[:, 1, :], Sf[:, bass.ds(later(it) * ((1 + NCH) * H * DV), H * DV)])\
                .then_inc(sem("state0"), 1)
            dve.wait_ge(sem("state0"), it + 1)
            for hp in range(2):
                hs = slice(2 * hp, 2 * hp + 2)

                def pair(x):
                    return x[:, hs, :].rearrange("p h t -> p (h t)")

                qbank, kbank = (pA[0], pA[1]) if hp == 0 else (pA[1], pA[0])
                dve.wait_ge(sem("q_mm"), it * 2 + hp + 1)
                dve.wait_ge(sem("eG"), it + 1)
                dve.scalar_tensor_tensor(pair(qg), qbank[:, :], DK ** -0.5, pair(eG), ALU.mult, ALU.mult)\
                    .then_inc(sem("qg"), 1)
                dve.wait_ge(sem("k_mm"), it * 2 + hp + 1)
                dve.wait_ge(sem("emG"), it + 1)
                dve.tensor_tensor(pair(kin), kbank[:, :], pair(emG), ALU.mult)
                dve.wait_ge(sem("eD"), it + 1)
                dve.tensor_tensor(pair(kg), kbank[:, :], pair(eD), ALU.mult).then_inc(sem("kg"), 1)
                settled(dve)
                dve.wait_ge(sem("att_mm"), it * 2 + hp + 1)
                dve.copy_predicated(att[:, :, hs, :], causal[:, :].rearrange("p (t h n) -> p t h n", t=NT, h=2),
                                    pA[1 - hp][:, :].rearrange("p (t h n) -> p t h n", t=NT, h=2))\
                    .then_inc(sem("att"), 1)
                dve.wait_ge(sem("kv_mm"), it * 2 + hp + 1)
                for c in range(NCH):
                    for h2 in range(2):
                        h = 2 * hp + h2
                        if c > 0:
                            dve.wait_ge(sem("state"), it * 16 + hp * 8 + 2 * c + h2 - 1)
                        dve.scalar_tensor_tensor(
                            S[:, 2 + c, h * DV:(h + 1) * DV], S[:, 1 + c, h * DV:(h + 1) * DV],
                            eG[:, h, (c + 1) * CH - 1:(c + 1) * CH],
                            pA[hp][:, (c * 2 + h2) * DV:(c * 2 + h2 + 1) * DV],
                            ALU.mult, ALU.add).then_inc(sem("state"), 1)
            dve.wait_ge(sem("rms"), it + 1)
            dve.wait_ge(sem("o_s"), it + 1)
            dve.tensor_tensor(o_s[:, :, :].rearrange("p c t -> p (c t)"), o_s[:, :, :].rearrange("p c t -> p (c t)"),
                              rms[:, :], ALU.mult).then_inc(sem("o_n"), 1)
            dve.wait_ge(sem("wo_mm"), it + 1)
            dve.tensor_tensor(x_at(it, 0, NT), x_at(it, 0, NT), pA[0][:, :], ALU.add).then_inc(sem("x_attn"), 1)
            settled(dve)
            dve.wait_ge(sem("x_attn"), it + 1)
            ln_vector(dve, it, "b", lambda t: x_at(it, t), xn)
            for jj in range(FJ):
                dve.wait_ge(sem("relu"), it * FJ + jj + 1)
                w2c = w("w2")[:, jj:jj + 1]
                if jj == 0:
                    dve.wait_ge(sem("wout_mm"), it)
                    dve.tensor_scalar(facc[:, :], rel[:, 0, :], w2c, w("b2"), ALU.mult, ALU.add)\
                        .then_inc(sem("facc"), 1)
                else:
                    dve.wait_ge(sem("facc"), it * FJ + jj)
                    dve.scalar_tensor_tensor(facc[:, :], rel[:, jj % 4, :], w2c, facc[:, :], ALU.mult, ALU.add)\
                        .then_inc(sem("facc"), 1)
            dve.wait_ge(sem("wout_mm"), it + 1)
            dve.tensor_tensor(x_at(it, 0, NT), x_at(it, 0, NT), pA[1][:, :], ALU.add).then_inc(sem("x_ffn"), 1)

        def A_pool(pool, it):
            ln_pool(pool, it, "a")
            pool.wait_ge(sem("z_ln"), it + 1)
            pool.tensor_tensor(lz[:, :], lz[:, :], rz[:, :], ALU.add).then_inc(sem("lz_sum"), 1)
            pool.wait_ge(sem("cumsum"), it + 1)
            lv = lz[:, :].rearrange("p (n t) -> p n t", t=CH)
            pool.tensor_tensor(rz[:, :].rearrange("p (n t) -> p n t", t=CH), lv,
                               lv[:, :, CH - 1:CH].broadcast_to([P, H * NCH, CH]), ALU.subtract)\
                .then_inc(sem("to_end"), 1)
            pool.wait_ge(sem("o_n"), it + 1)
            pool.wait_ge(sem("sg"), it + 1)
            pool.tensor_tensor(og[:, :, :], o_s[:, :, :], sg[:, :, :], ALU.mult).then_inc(sem("og"), 1)
            ln_pool(pool, it, "b")

        def B_pe_front(pe, it, b):
            pe.wait_ge(sem("scores"), it)
            turn(pe, it, "c", xnB, pB, "turn_c")
            pe.wait_ge(sem("hT_c"), (it + 1) * DC)
            for n in range(2 * DT // 2):
                if n > 0:
                    pe.wait_ge(sem("x_cp") if n <= 2 else sem("sz"), it * 2 + (n if n <= 2 else 1))
                for m in range(2):
                    for c in range(DC):
                        col = (2 * n + m) * P
                        i = pe.matmul(pB[:, m * TB:(m + 1) * TB], inproj[:, c, col:col + P], hB[:, c, :],
                                      start=(c == 0), stop=(c == DC - 1))
                i.then_inc(sem("in_mm"), 1)
            pe.wait_ge(sem("sz"), it * 2 + 2)
            pe.wait_ge(sem("xs"), it + 1)
            for lo, n, at in ((0, DR, 0), (DR, 2 * DS, TB)):
                for k in range(DT):
                    i = pe.matmul(pB[0:n, at:at + TB], xproj[:, k, lo:lo + n], xs[:, k, :],
                                  start=(k == 0), stop=(k == DT - 1))
            i.then_inc(sem("dkq_mm"), 1)
            pe.wait_ge(sem("dkq"), it * 2 + 2)
            for n in range(DT // 2):
                if n == 1:
                    pe.wait_ge(sem("dt_sig"), it * DT + 2)
                for m in range(2):
                    k = 2 * n + m
                    i = pe.matmul(pB[:, m * TB:(m + 1) * TB], dthead[0:DR, k * P:(k + 1) * P], dtl[:, :],
                                  start=True, stop=True)
                i.then_inc(sem("dt_mm"), 1)
            pe.wait_ge(sem("dt_sig"), it * DT + DT)
            pe.wait_ge(sem("parts"), (it + 1) * 5)
            pe.matmul(pB[:, 0:TB], selk[:, :], k3[:, 1, :], start=True, stop=True).then_inc(sem("ksum_mm"), 1)

        def B_pe_spread(pe, it, n):
            if n == 0:
                pe.wait_ge(sem("parts"), (it + 1) * 5)
            if n < 2:
                pe.wait_ge(sem("inp"), it * DS)
            else:
                pe.wait_ge(sem("inp"), it * DS + n - 1)
            pe.matmul(pK[n % 2][:, 0:TB], sel[:, n, :], k3[:, 1, :], start=True, stop=True)
            pe.matmul(pK[n % 2][:, TB:2 * TB], sel[:, n, :], k3[:, 0, :], start=True, stop=True)\
                .then_inc(sem("k_rows"), 1)
            if n % 2 == 0:
                pe.wait_ge(sem("q_rows"), it * (DS // 2) + n // 2)
                pe.matmul(pQ[:, 0:TB], sel[:, DS + n, :], k3[:, 0, :], start=True, stop=True)
                pe.matmul(pQ[:, TB:2 * TB], sel[:, DS + n + 1, :], k3[:, 0, :], start=True, stop=True)\
                    .then_inc(sem("q_mm2"), 1)

        def B_pe_sum(pe, it, n):
            pe.wait_ge(sem("read_out"), it * DS + n + 1)
            for m in range(DT // 2):
                i = pe.matmul(pY[:, 2 * m:2 * m + 2, :].rearrange("p k t -> p (k t)"), ident_s[:, :],
                              st[:, n % 3, 2 * m:2 * m + 2, :].rearrange("p k t -> p (k t)"),
                              start=False, stop=(n == DS - 1), skip_group_check=True)
            i.then_inc(sem("summed"), 1)

        def B_pe_scan(pe, it, b):
            pe.wait_ge(sem("yz"), it)
            for k in range(DT):
                pe.matmul(pY[:, k, :], dskip[:, k, :], xs[:, k, :], start=(k % 2 == 0), stop=False,
                          skip_group_check=True)
            B_pe_spread(pe, it, 0)
            for n in range(DS):
                if n + 1 < DS:
                    B_pe_spread(pe, it, n + 1)
                B_pe_sum(pe, it, n)

        def B_pe_back(pe, it, b):
            pe.wait_ge(sem("yz"), it + 1)
            pe.wait_ge(sem("ksum"), it + 1)
            for t in range(NT):
                for k in range(DT):
                    i = pe.matmul(pB[:, t * D:(t + 1) * D], tmp[:, k, t * P:(t + 1) * P],
                                  oproj_g[:, :, :, :].rearrange("p b k n -> p (b k n)")[
                                      :, bass.ds((b * DT + k) * D, D)],
                                  start=(k == 0), stop=(k == DT - 1))
            i.then_inc(sem("out_mm"), 1)
            pe.wait_ge(sem("x_scan"), it + 1)
            turn(pe, it, "d", xnC, pB, "turn_d")
            pe.wait_ge(sem("hT_d"), (it + 1) * DC)
            for t in range(NT):
                for c in range(DC):
                    i = pe.matmul(pB[:, t * E:(t + 1) * E], hC[:, c, t * P:(t + 1) * P], gate[:, c, :],
                                  start=(c == 0), stop=(c == DC - 1))
            i.then_inc(sem("score_mm"), 1)

        def B_act_front(act, it, b):
            modulate(act, it, b, pB, col1, 1, 0, hB, "turn_c", "hT_c")
            act.wait_ge(sem("conv"), it * 16)
            act.wait_ge(sem("tail"), it)
            nt = DT * (DCV - 1)
            act.activation(xraw[:, :, 0:DCV - 1],
                           tail[:, bass.ds(later(it) * nt, nt)].rearrange("p (k n) -> p k n", n=DCV - 1), ACT.Copy)\
                .then_inc(sem("halo"), 1)
            for n in range(2):
                act.wait_ge(sem("in_mm"), it * 4 + n + 1)
                act.activation(xraw[:, 2 * n:2 * n + 2, DCV - 1:], pB[:, :].rearrange("p (k t) -> p k t", k=2),
                               ACT.Copy).then_inc(sem("x_cp"), 1)
            for n in range(2):
                act.wait_ge(sem("in_mm"), it * 4 + n + 3)
                act.activation(sz[:, 2 * n:2 * n + 2, :], pB[:, :].rearrange("p (k t) -> p k t", k=2),
                               ACT.Silu).then_inc(sem("sz"), 1)
            act.wait_ge(sem("x_cp"), it * 2 + 2)
            act.wait_ge(sem("halo"), it + 1)
            act.activation(tail[:, nt:2 * nt].rearrange("p (k n) -> p k n", n=DCV - 1), xraw[:, :, TB:], ACT.Copy)\
                .then_inc(sem("tail"), 1)
            act.wait_ge(sem("conv"), it * 16 + 16)
            act.activation(xs[:, :, :], xs[:, :, :], ACT.Silu).then_inc(sem("xs"), 1)
            act.wait_ge(sem("dkq_mm"), it + 1)
            act.activation(dtl[:, :], pB[0:DR, 0:TB], ACT.Copy).then_inc(sem("dkq"), 1)
            act.activation(kx[:, 0, :], pB[0:32, TB:2 * TB], ACT.Copy).then_inc(sem("dkq"), 1)
            for k in range(DT):
                act.wait_ge(sem("dt_mm"), it * 2 + k // 2 + 1)
                act.activation(dtv[:, k, :], pB[:, (k % 2) * TB:(k % 2 + 1) * TB], ACT.Sigmoid,
                               bias=w("dtb")[:, k:k + 1]).then_inc(sem("dt_sig"), 1)
            act.wait_ge(sem("ksum_mm"), it + 1)
            act.activation(ksum[:, :], pB[:, 0:TB], ACT.Copy).then_inc(sem("ksum"), 1)
            act.wait_ge(sem("s_ksum"), it + 1)
            act.activation(tmp[:, :, :], tmp[:, :, :], ACT.Ln, bias=ones_s[:, 0:1]).then_inc(sem("den_ln"), 1)
            act.wait_ge(sem("den_ln"), it + 1)
            act.activation(tmp[:, :, :], tmp[:, :, :], ACT.Exp, scale=-1.0).then_inc(sem("den"), 1)

        def B_act_q(act, it, m):
            act.wait_ge(sem("q_mm2"), it * (DS // 2) + m + 1)
            if m >= 2:
                act.wait_ge(sem("read_out"), it * DS + 2 * (m - 1))
            else:
                act.wait_ge(sem("read_out"), it * DS)
            act.activation(qb[:, m % 2, :], pQ[:, :], ACT.Copy).then_inc(sem("q_rows"), 1)

        def B_act_scan(act, it, b):
            ns = DS * DT
            for n in range(DS):
                if n % 2 == 0:
                    B_act_q(act, it, n // 2)
                act.wait_ge(sem("rate"), it * DS + n + 1)
                act.activation(dec[:, n % 2], dec[:, n % 2], ACT.Identity, bias=ones_s[:, 0:1], scale=-1.0)\
                    .then_inc(sem("decay"), 1)
                if n >= 1:
                    B_act_save(act, it, n - 1)
            B_act_save(act, it, DS - 1)

        def B_act_save(act, it, n):
            act.wait_ge(sem("scanned"), it * DS + n + 1)
            act.activation(last[:, (DS + n) * DT:(DS + n + 1) * DT], st[:, n % 3, :, TB - 1], ACT.Copy)\
                .then_inc(sem("saved"), 1)

        def B_act_back(act, it, b):
            modulate(act, it, b, pB, col1, 4, 3, hC, "turn_d", "hT_d")
            act.wait_ge(sem("score_mm"), it + 1)
            act.activation(scores[:, bass.ds((it - 1) * (NT * E), NT * E)], pB[:, 0:NT * E], ACT.Copy)\
                .then_inc(sem("scores"), 1)

        def B_dve_front(dve, it, b):
            settled(dve)
            dve.wait_ge(sem("x_ffn"), it + 1)
            ln_vector(dve, it, "c", lambda t: x_at(it, t), xnB)
            dve.wait_ge(sem("halo"), it + 1)
            for j in range(DCV):
                for k in range(DT):
                    if j == 0:
                        dve.wait_ge(sem("x_cp"), it * 2 + k // 2 + 1)
                        if k == 0:
                            dve.wait_ge(sem("summed"), it * DS)
                        dve.tensor_scalar(xs[:, k, :], xraw[:, k, 0:TB], w("convw")[:, k * DCV:k * DCV + 1],
                                          w("convb")[:, k:k + 1], ALU.mult, ALU.add).then_inc(sem("conv"), 1)
                    else:
                        dve.wait_ge(sem("conv"), it * 16 + (j - 1) * DT + k + 1)
                        dve.scalar_tensor_tensor(xs[:, k, :], xraw[:, k, j:j + TB],
                                                 w("convw")[:, k * DCV + j:k * DCV + j + 1], xs[:, k, :],
                                                 ALU.mult, ALU.add).then_inc(sem("conv"), 1)
            dve.wait_ge(sem("dkq"), it * 2 + 2)
            dve.tensor_tensor(kx[:, 1, :], kx[:, 0, :], kx[:, 0, :], ALU.mult).then_inc(sem("squares"), 1)
            dve.wait_ge(sem("squares"), it + 1)
            dve.wait_ge(sem("k_rows"), it * DS)
            dve.wait_ge(sem("q_mm2"), it * (DS // 2))
            dve.wait_ge(sem("ksum_mm"), it)
            dve.tensor_copy(k3[0:32, :, :], kx[:, :, :]).then_inc(sem("parts"), 1)
            dve.wait_ge(sem("parts"), it * 5 + 1)
            dve.tensor_tensor(kr[:, :, :], kx[:, :, :], k3[0:32, :, :], ALU.subtract).then_inc(sem("parts"), 1)
            dve.wait_ge(sem("parts"), it * 5 + 2)
            dve.tensor_copy(km[:, :, :], kr[:, :, :]).then_inc(sem("parts"), 1)
            dve.wait_ge(sem("parts"), it * 5 + 3)
            dve.tensor_copy(k3[32:64, :, :], km[:, :, :]).then_inc(sem("parts"), 1)
            dve.tensor_tensor(k3[64:96, :, :], kr[:, :, :], km[:, :, :], ALU.subtract).then_inc(sem("parts"), 1)
            dve.wait_ge(sem("ksum"), it + 1)
            dve.wait_ge(sem("dt_sig"), it * DT + DT)
            dve.wait_ge(sem("out_mm"), it)
            dve.tensor_tensor(tmp[:, :, :], dtv[:, :, :], ksum[:, :].unsqueeze(1).broadcast_to([P, DT, TB]), ALU.mult)\
                .then_inc(sem("s_ksum"), 1)

        def B_dve_inputs(dve, it, n):
            rows = pK[n % 2]
            if n == 0:
                dve.wait_ge(sem("dtv"), it + 1)
                dve.wait_ge(sem("u"), it + 1)
            dve.wait_ge(sem("k_rows"), it * DS + n + 1)
            if n >= 2:
                dve.wait_ge(sem("scanned"), it * DS + n - 1)
            dve.tensor_tensor(dec[:, n % 2], dtv[:, :, :], rows[:, 0:TB].unsqueeze(1).broadcast_to([P, DT, TB]),
                              ALU.mult).then_inc(sem("rate"), 1)
            dve.wait_ge(sem("summed"), it * DS + n - 2)
            dve.tensor_tensor(st[:, n % 3], u[:, :, :], rows[:, TB:2 * TB].unsqueeze(1).broadcast_to([P, DT, TB]),
                              ALU.mult).then_inc(sem("inp"), 1)

        def B_dve_scan(dve, it, b):
            ns = DS * DT
            dve.wait_ge(sem("saved"), it * DS)
            B_dve_inputs(dve, it, 0)
            for n in range(DS):
                if n + 1 < DS:
                    B_dve_inputs(dve, it, n + 1)
                dve.wait_ge(sem("decay"), it * DS + n + 1)
                dve.wait_ge(sem("inp"), it * DS + n + 1)
                for k in range(DT):
                    i = dve.tensor_tensor_scan(st[:, n % 3, k, :], dec[:, n % 2, k, :], st[:, n % 3, k, :],
                                               last[:, bass.ds(later(it) * ns + n * DT + k, 1)],
                                               ALU.mult, ALU.add)
                i.then_inc(sem("scanned"), 1)

        def B_dve_back(dve, it, b):
            dve.wait_ge(sem("summed"), (it + 1) * DS)
            dve.wait_ge(sem("dtv"), it + 1)
            dve.tensor_tensor(tmp[:, :, :], pY[:, :, :], sz[:, :, :], ALU.mult).then_inc(sem("yz"), 1)
            dve.wait_ge(sem("out_mm"), it + 1)
            dve.wait_ge(sem("x_out"), it * 16)
            dve.tensor_tensor(xo[:, :, :].rearrange("p t n -> p (t n)"), x_at(it, 0, NT), pB[:, :], ALU.add)\
                .then_inc(sem("x_scan"), 1)
            settled(dve)
            dve.wait_ge(sem("x_scan"), it + 1)
            dve.wait_ge(sem("rows_out"), it * 16)
            ln_vector(dve, it, "d", lambda t: xo[:, t, :], xnC)

        def B_pool(pool, it, b):
            ln_pool(pool, it, "c")
            pool.wait_ge(sem("den"), it + 1)
            pool.tensor_tensor(dtv[:, :, :], dtv[:, :, :], tmp[:, :, :], ALU.mult).then_inc(sem("dtv"), 1)
            pool.wait_ge(sem("dtv"), it + 1)
            pool.wait_ge(sem("inp"), it * DS)
            pool.tensor_tensor(u[:, :, :], xs[:, :, :], dtv[:, :, :], ALU.mult).then_inc(sem("u"), 1)
            for n in range(DS):
                pool.wait_ge(sem("saved"), it * DS + n + 1)
                pool.wait_ge(sem("q_rows"), it * (DS // 2) + n // 2 + 1)
                q = qb[:, (n // 2) % 2, (n % 2) * TB:(n % 2 + 1) * TB]
                pool.tensor_tensor(st[:, n % 3], st[:, n % 3], q.unsqueeze(1).broadcast_to([P, DT, TB]), ALU.mult)\
                    .then_inc(sem("read_out"), 1)
            ln_pool(pool, it, "d")

        with nc.Block() as block:
            @block.sync
            def _(sp):
                def load(it):
                    sp.dma_start(xt[:, bass.ds((it % 2) * (NT * D), NT * D)].rearrange("p (t n) -> p t n", n=D),
                                 x_rows[bass.ds((it - 1) * TB, TB), :].rearrange("(t p) n -> p t n", p=P))\
                        .then_inc(sem("x_in"), 16)

                def store(it):
                    sp.wait_ge(sem("x_scan"), it + 1)
                    sp.dma_start(out_rows[bass.ds((it - 1) * TB, TB), :].rearrange("(t p) n -> p t n", p=P), xo[:, :, :])\
                        .then_inc(sem("x_out"), 16)
                    sp.wait_ge(sem("lnd_rows"), it + 1)
                    sp.dma_start(xn_d[bass.ds((it - 1) * TB, TB), :].rearrange("(t p) n -> p t n", p=P), xnC[:, :, :])\
                        .then_inc(sem("rows_out"), 16)

                load(1)
                with sp.Fori(1, NB) as it:
                    sp.wait_ge(sem("x_scan"), it)
                    sp.wait_ge(sem("x_in"), (it + 1) * 16)
                    load(it + 1)
                    store(it)
                store(NB)
                sp.wait_ge(sem("x_out"), (NB + 1) * 16)
                sp.wait_ge(sem("rows_out"), (NB + 1) * 16)

            @block.tensor
            def _(pe):
                with pe.Fori(1, NB + 1) as it:
                    b = pe.snap(batch(it))
                    if True:
                        A_pe(pe, it, b)
                        B_pe_front(pe, it, b)
                        B_pe_scan(pe, it, b)
                        B_pe_back(pe, it, b)

            @block.scalar
            def _(act):
                with act.Fori(1, NB + 1) as it:
                    b = act.snap(batch(it))
                    A_act(act, it, b)
                    B_act_front(act, it, b)
                    B_act_scan(act, it, b)
                    B_act_back(act, it, b)

            @block.vector
            def _(dve):
                dve.memset(att[:, :, :, :], 0.0)
                dve.memset(vh[:, :, :, :], 0.0)
                dve.memset(S[:, 0, :], 0.0)
                dve.memset(tail[:, 0:DT * (DCV - 1)], 0.0).then_inc(sem("tail0"), 1)
                dve.memset(last[:, 0:DS * DT], 0.0).then_inc(sem("tail0"), 1)
                dve.wait_ge(sem("tail0"), 2)
                with dve.Fori(1, NB + 1) as it:
                    b = None
                    A_dve(dve, it, b)
                    B_dve_front(dve, it, b)
                    B_dve_scan(dve, it, b)
                    B_dve_back(dve, it, b)

            @block.gpsimd
            def _(pool):
                with pool.Fori(1, NB + 1) as it:
                    A_pool(pool, it)
                    B_pool(pool, it, None)


def experts(nc, sem, consts, w1_d, w2_d, out_rows, xn_d, scores, ones_s, ident_s, col1, gb1):
    with ExitStack() as ctx:
        def sb(name, shape, dt=F32):
            return ctx.enter_context(nc.sbuf_tensor(name, shape, dt))

        def ps(name, shape, dt=F32):
            return ctx.enter_context(nc.psum_tensor(name, shape, dt))

        def chain(eng, instruction, s):
            count[s] = count.get(s, 0) + 1
            instruction.then_inc(sem(s), 1)
            eng.wait_ge(sem(s), count[s])

        count = {}
        LT = NL * TT
        before = sb("before", [P, P])
        tilerun = sb("tilerun", [P, LT])
        iota = sb("iota", [P, P])
        token = sb("token", [P, LT])
        bitsf = sb("bitsf", [P, BITS])
        bitsu = sb("bitsu", [P, BITS], U32)
        red = sb("red", [P, B * TT])
        prob = sb("prob", [P, B * TT, E])
        pl = sb("pl", [P, LT])
        thr = sb("thr", [P, NL], U32)
        cand = sb("cand", [P, NL], U32)
        hit = sb("hit", [P, LT])
        cnt = sb("cnt", [P, NL])
        step = sb("step", [P, NL], U32)
        eq = sb("eq", [P, LT])
        tot = sb("tot", [P, LT])
        run = sb("run", [P, LT])
        pos = sb("pos", [P, LT])
        need = sb("need", [P, NL])
        posi = sb("posi", [P, LT], I32)
        loi = sb("loi", [P, LT], I32)
        lo = sb("lo", [P, LT])
        hi = sb("hi", [P, LT])
        what = sb("what", [P, NL, TT, 2 * SL])
        onehot = sb("onehot", [P, 2, TT, P])
        slots = sb("slots", [P, NL, 2 * SL])
        ids = sb("ids", [P, NL, SL], U32)
        w1s = sb("w1s", [P, 2, DC, F])
        w2s = sb("w2s", [P, 2, FT, D])
        xg = sb("xg", [P, 2, SL, D])
        hg = sb("hg", [P, DC, K])
        h1 = sb("h1", [P, FT, K])
        ys = sb("ys", [P, 2, SL, D])
        pc = ps("pc", [P, 2, 512])
        pt = ps("pt", [P, 2, 512])
        ph = ps("ph", [P, 2, 512])
        po = ps("po", [P, 2, 512])

        def lists(x):
            return x.rearrange("p (l t) -> p l t", t=TT)

        def spread(x):
            return x.unsqueeze(2).broadcast_to([P, NL, TT])

        ITEMS = NL // 4

        with nc.Block() as block:
            @block.sync
            def _(sp):
                def load(e, slot):
                    sp.dma_start(w1s[:, slot], w1_d[bass.ds(e, 1)].rearrange("e (c p) f -> p (e c) f", p=P))\
                        .then_inc(sem(f"w1_in{slot}"), 16)
                    sp.dma_start(w2s[:, slot], w2_d[bass.ds(e, 1)].rearrange("e (c p) f -> p (e c) f", p=P))\
                        .then_inc(sem(f"w2_in{slot}"), 16)

                for name, dst in (("before", before), ("tilerun", tilerun), ("iota", iota), ("token", token),
                                  ("bitsf", bitsf)):
                    a, n = CONST_AT[name]
                    sp.dma_start(dst[:, :], consts[:, a:a + n]).then_inc(sem("const2_in"), 16)
                load(0, 0)
                load(1, 1)
                with sp.Fori(1, ITEMS) as i:
                    for slot in range(2):
                        sp.wait_ge(sem("down_mm"), i * 4 * SL + (slot + 1) * 2 * SL)
                        load(2 * i + slot, slot)

            @block.vector
            def _(dve):
                def do(instruction):
                    chain(dve, instruction, "sel_step")

                sc = scores[:, :].rearrange("p (t e) -> p t e", e=E)
                do(dve.tensor_reduce(red[:, :], sc, AX_X, ALU.max))
                do(dve.tensor_tensor(sc, sc, red[:, :].unsqueeze(2).broadcast_to([P, B * TT, E]), ALU.subtract))
                dve.wait_ge(sem("const2_in"), 80)
                do(dve.tensor_copy(bitsu[:, :], bitsf[:, :]))
                do(dve.memset(thr[:, :], 0))
                dve.wait_ge(sem("prob_exp"), 1)
                do(dve.tensor_reduce(red[:, :], prob[:, :, :], AX_X, ALU.add))
                do(dve.reciprocal(red[:, :], red[:, :]))
                for b in range(B):
                    i = dve.tensor_tensor(
                        lists(pl[:, :])[:, b * E:(b + 1) * E, :],
                        prob[:, b * TT:(b + 1) * TT, :].rearrange("p t e -> p e t"),
                        red[:, b * TT:(b + 1) * TT].unsqueeze(1).broadcast_to([P, E, TT]), ALU.mult)
                do(i)
                with dve.Fori(0, BITS) as i:
                    dve.tensor_tensor(cand[:, :], thr[:, :], bitsu[:, bass.ds(i, 1)].broadcast_to([P, NL]),
                                      ALU.bitwise_or).then_inc(sem("t_cand"), 1)
                    dve.wait_ge(sem("t_cand"), i + 1)
                    dve.tensor_tensor(lists(hit[:, :]), lists(pl[:, :]), spread(cand[:, :].bitcast(F32)), ALU.is_ge)\
                        .then_inc(sem("t_hit"), 1)
                    dve.wait_ge(sem("t_hit"), i + 1)
                    dve.tensor_reduce(cnt[:, :], lists(hit[:, :]), AX_X, ALU.add).then_inc(sem("t_cnt"), 1)
                    dve.wait_ge(sem("t_all"), i + 1)
                    dve.tensor_scalar(step[:, :], pc[:, 0, 0:NL], float(K), bitsf[:, bass.ds(i, 1)],
                                      ALU.is_ge, ALU.mult).then_inc(sem("t_step"), 1)
                    dve.wait_ge(sem("t_step"), i + 1)
                    dve.tensor_tensor(thr[:, :], thr[:, :], step[:, :], ALU.bitwise_or).then_inc(sem("t_thr"), 1)
                    dve.wait_ge(sem("t_thr"), i + 1)
                tf = spread(thr[:, :].bitcast(F32))
                do(dve.tensor_tensor(lists(hit[:, :]), lists(pl[:, :]), tf, ALU.is_gt))
                do(dve.tensor_tensor(lists(eq[:, :]), lists(pl[:, :]), tf, ALU.is_equal))
                dve.tensor_reduce(cnt[:, :], lists(hit[:, :]), AX_X, ALU.add).then_inc(sem("above"), 1)

                def ranks(src_ready, dst):
                    dve.wait_ge(sem("prefix"), src_ready)
                    do(dve.tensor_copy(tot[:, :], pc[:, 1, LT:2 * LT]))
                    do(dve.tensor_tensor_scan(run[:, :], tilerun[:, :], tot[:, :], 0.0, ALU.mult, ALU.add))
                    do(dve.tensor_tensor(run[:, :], run[:, :], tot[:, :], ALU.subtract))
                    do(dve.tensor_tensor(dst[:, :], run[:, :], pc[:, 1, 0:LT], ALU.add))

                dve.wait_ge(sem("t_all"), BITS + 1)
                do(dve.tensor_scalar(need[:, :], pc[:, 0, 0:NL], -1.0, float(K), ALU.mult, ALU.add))
                ranks(1, pos)
                do(dve.tensor_tensor(lists(pos[:, :]), lists(pos[:, :]), spread(need[:, :]), ALU.is_lt))
                do(dve.tensor_tensor(eq[:, :], eq[:, :], pos[:, :], ALU.mult))
                do(dve.tensor_tensor(hit[:, :], hit[:, :], eq[:, :], ALU.add))
                dve.sem_inc(sem("marked"), 1)
                ranks(2, pos)
                do(dve.scalar_tensor_tensor(pos[:, :], pos[:, :], 1.0, hit[:, :], ALU.add, ALU.mult))
                do(dve.tensor_scalar(posi[:, :], pos[:, :], -1.0, None, ALU.add))
                do(dve.tensor_scalar(loi[:, :], posi[:, :], P - 1, None, ALU.bitwise_and))
                do(dve.tensor_copy(lo[:, :], loi[:, :]))
                do(dve.tensor_scalar(loi[:, :], posi[:, :], 7, None, ALU.arith_shift_right))
                do(dve.tensor_copy(hi[:, :], loi[:, :]))
                for c in range(SL):
                    dve.scalar_tensor_tensor(what[:, :, :, c].rearrange("p l t -> p (l t)"), hi[:, :], float(c),
                                             token[:, :], ALU.is_equal, ALU.mult)
                    i = dve.scalar_tensor_tensor(what[:, :, :, SL + c].rearrange("p l t -> p (l t)"), hi[:, :],
                                                 float(c), pl[:, :], ALU.is_equal, ALU.mult)
                i.then_inc(sem("what"), 1)
                for li in range(NL):
                    if li >= 2:
                        dve.wait_ge(sem("slot_mm"), li - 1)
                    dve.tensor_tensor(onehot[:, li % 2], iota[:, :].unsqueeze(1).broadcast_to([P, TT, P]),
                                      lists(lo[:, :])[:, li, :].unsqueeze(2).broadcast_to([P, TT, P]), ALU.is_equal)\
                        .then_inc(sem("onehot"), 1)
                dve.wait_ge(sem("slot_mm"), NL)
                dve.tensor_copy(slots[:, :, :].rearrange("p l c -> p (l c)"), pt[:, 0, 0:NL * 2 * SL])\
                    .then_inc(sem("slots"), 1)
                dve.wait_ge(sem("slots"), 1)
                dve.tensor_copy(ids[:, :, :], slots[:, :, 0:SL]).then_inc(sem("ids"), 1)

                sf = slots[:, :, :].rearrange("p l c -> p (l c)")
                with dve.Fori(1, ITEMS + 1) as i:
                    for n in range(4):
                        e2, b = n // 2, n % 2
                        for c in range(SL):
                            dve.wait_ge(sem("down_mm"), i * 4 * SL + n * SL + c + 1)
                            if c == 0:
                                dve.wait_ge(sem("ys_free"), (i - 1) * 4 + n + 1)
                            dve.scalar_tensor_tensor(
                                ys[:, b, c, :], po[:, c % 2, 0:D],
                                sf[:, bass.ds((b * E + e2) * 2 * SL + SL + c + (i - 1) * (2 * 2 * SL), 1)],
                                gb1[:, b * D:(b + 1) * D], ALU.mult, ALU.mult).then_inc(sem("scaled"), 1)

            @block.scalar
            def _(act):
                act.wait_ge(sem("sel_step"), 2)
                act.activation(prob[:, :, :].rearrange("p t e -> p (t e)"), scores[:, :], ACT.Exp)\
                    .then_inc(sem("prob_exp"), 1)
                with act.Fori(1, ITEMS + 1) as i:
                    for n in range(4):
                        b = n % 2
                        for c in range(DC):
                            act.wait_ge(sem("gt_mm"), i * 8 + n * 2 + c + 1)
                            sc, sh = ((what * DC + c) * B + b for what in (4, 3))
                            act.activation(hg[:, c, :], pt[:, c, :], ACT.Identity, bias=col1[:, sh:sh + 1],
                                           scale=col1[:, sc:sc + 1]).then_inc(sem("hg"), 1)
                        for f in range(FT):
                            act.wait_ge(sem("up_mm"), i * 4 * FT + n * FT + f + 1)
                            if f == 0:
                                act.wait_ge(sem("down_mm"), i * 4 * SL + n * SL)
                            act.activation(h1[:, f, :], ph[:, f % 2, :], ACT.Gelu).then_inc(sem("gelu"), 1)

            @block.tensor
            def _(pe):
                with pe.Fori(0, BITS) as i:
                    pe.wait_ge(sem("t_cnt"), i + 1)
                    pe.matmul(pc[:, 0, 0:NL], ones_s[:, :], cnt[:, :], start=True, stop=True).then_inc(sem("t_all"), 1)
                pe.wait_ge(sem("above"), 1)
                pe.wait_ge(sem("t_step"), BITS)
                pe.matmul(pc[:, 0, 0:NL], ones_s[:, :], cnt[:, :], start=True, stop=True).then_inc(sem("t_all"), 1)
                for n, marks in enumerate((eq, hit)):
                    if n == 1:
                        pe.wait_ge(sem("marked"), 1)
                    pe.matmul(pc[:, 1, 0:LT], before[:, :], marks[:, :], start=True, stop=True)
                    pe.matmul(pc[:, 1, LT:2 * LT], ones_s[:, :], marks[:, :], start=True, stop=True)\
                        .then_inc(sem("prefix"), 1)
                pe.wait_ge(sem("what"), 1)
                for li in range(NL):
                    pe.wait_ge(sem("onehot"), li + 1)
                    for t in range(TT):
                        m = pe.matmul(pt[:, 0, li * 2 * SL:(li + 1) * 2 * SL], onehot[:, li % 2, t, :],
                                      what[:, li, t, :], start=(t == 0), stop=(t == TT - 1))
                    m.then_inc(sem("slot_mm"), 1)
                pe.wait_ge(sem("slots"), 1)
                with pe.Fori(1, ITEMS + 1) as i:
                    for n in range(4):
                        e2, b = n // 2, n % 2
                        pe.wait_ge(sem(f"rows_in{b}"), ((i - 1) * 2 + e2 + 1) * SL * 16)
                        pe.wait_ge(sem("hg"), i * 8 + n * 2)
                        for c in range(DC):
                            for s in range(SL):
                                m = pe.transpose(pt[:, c, s * P:(s + 1) * P], xg[:, n % 2, s, c * P:(c + 1) * P],
                                                 ident_s[:, :])
                            m.then_inc(sem("gt_mm"), 1)
                        pe.wait_ge(sem("hg"), i * 8 + n * 2 + 2)
                        if b == 0:
                            pe.wait_ge(sem(f"w1_in{e2}"), (i + 1) * 16)
                            pe.wait_ge(sem(f"w2_in{e2}"), (i + 1) * 16)
                        for f in range(FT):
                            pe.wait_ge(sem("gelu"), i * 4 * FT + n * FT + f - 1)
                            for c in range(DC):
                                m = pe.matmul(ph[:, f % 2, :], w1s[:, e2, c, f * P:(f + 1) * P], hg[:, c, :],
                                              start=(c == 0), stop=(c == DC - 1))
                            m.then_inc(sem("up_mm"), 1)
                        pe.wait_ge(sem("gelu"), i * 4 * FT + (n + 1) * FT)
                        for s in range(SL):
                            k = n * SL + s
                            pe.wait_ge(sem("scaled"), i * 4 * SL + k - 1)
                            for f in range(FT):
                                m = pe.matmul(po[:, s % 2, 0:D], h1[:, f, s * P:(s + 1) * P], w2s[:, e2, f, :],
                                              start=(f == 0), stop=(f == FT - 1))
                            m.then_inc(sem("down_mm"), 1)

            @block.gpsimd
            def _(pool):
                pool.wait_ge(sem("ids"), 1)

                def gather(n):
                    e, b = n // 2, n % 2
                    for s in range(SL):
                        pool.indirect_dma_start(
                            xg[:, b, s, :], None, xn_d[:, :],
                            bass.IndirectOffsetOnAxis(ap=ids[:, b * E + e, s:s + 1], axis=0))\
                            .then_inc(sem(f"rows_in{b}"), 16)

                def scatter(n):
                    e, b = n // 2, n % 2
                    pool.wait_ge(sem("scaled"), PER_TURN["scaled"] + (n + 1) * SL)
                    for s in range(SL):
                        pool.indirect_dma_start(
                            out_rows, bass.IndirectOffsetOnAxis(ap=ids[:, b * E + e, s:s + 1], axis=0),
                            ys[:, b, s, :], None, compute_op=ALU.add).then_inc(sem(f"added{b}"), 16)

                gather(0)
                gather(1)
                for n in range(NL):
                    if n >= 2:
                        pool.wait_ge(sem(f"added{n % 2}"), n // 2 * SL * 16)
                    pool.sem_inc(sem("ys_free"), 1)
                    if n + 2 < NL:
                        pool.wait_ge(sem("gt_mm"), PER_TURN["gt_mm"] + (n + 1) * DC)
                        gather(n + 2)
                    scatter(n)
                for b in range(B):
                    pool.wait_ge(sem(f"added{b}"), E * SL * 16)


def rows_of_chunks(a):
    n = a.shape[1]
    c = -(-a.shape[0] // P)
    full = np.zeros((c * P, n), np.float32)
    full[:a.shape[0]] = a
    return full.reshape(c, P, n).transpose(1, 0, 2).reshape(P, c * n)


def kernel(**inputs):
    import concourse.bacc as _bacc
    from concourse.bass_utils import run_bass_kernel_spmd as _run

    a = {k: np.asarray(v) for k, v in inputs.items()}
    col = lambda x: x.reshape(-1, P).T
    two = lambda x: np.concatenate([x, x], axis=-1)

    def pair(x):
        return np.concatenate([x[:, 0::2], x[:, 1::2]], axis=0)

    wt = {
        "wq": rows_of_chunks(a["L0_attn_Wq"]), "wk": rows_of_chunks(a["L0_attn_Wk"]),
        "wv": rows_of_chunks(a["L0_attn_Wv"]), "wg": rows_of_chunks(a["L0_attn_Wg"]),
        "wgk1": rows_of_chunks(a["L0_attn_Wgk1"]), "wgk2": rows_of_chunks(a["L0_attn_Wgk2"]),
        "win2": rows_of_chunks(two(a["L0_ffn_Win"])), "inproj": rows_of_chunks(a["L1_attn_in_proj_w"].T),
        "xproj": rows_of_chunks(a["L1_attn_x_proj_w"].T), "dthead": rows_of_chunks(a["L1_attn_dt_head_w"].T),
        "gate": rows_of_chunks(a["L1_ffn_gate_w"].T), "bgk2": col(a["L0_attn_bgk2"]),
        "bin": two(a["L0_ffn_bin_"])[:, None], "w1": pair(a["L0_ffn_W1"]), "b1": pair(a["L0_ffn_b1"]),
        "w2": pair(a["L0_ffn_W2"]),
        "b2": np.concatenate([a["L0_ffn_b2"], np.zeros(FM, np.float32)])[:, None],
        "convw": a["L1_attn_conv_w"].reshape(DT, P, DCV).transpose(1, 0, 2).reshape(P, DT * DCV),
        "convb": col(a["L1_attn_conv_b"]), "dtb": col(a["L1_attn_dt_head_b"]), "dskip": col(a["L1_attn_D"]),
        "gnw": two(a["L0_attn_gnw"])[:, None],
    }
    fd = {
        "wo": rows_of_chunks(a["L0_attn_Wo"]),
        "wout2": np.concatenate([a["L0_ffn_Wout"], a["L0_ffn_Wout"]], axis=0),
        "bout": rows_of_chunks(a["L0_ffn_bout"][None, :]),
        "outproj": rows_of_chunks(a["L1_attn_out_proj_w"].T),
        "c0": rows_of_chunks(a["L0_c"].T), "c1": rows_of_chunks(a["L1_c"].T),
    }
    cs = shape_constants()
    packed = lambda sizes, parts: np.ascontiguousarray(np.concatenate([parts[n] for n, _ in sizes], axis=1))
    arrays = {
        "x_in": a["L0_attn_x"], "consts": packed(CONST_SIZES, cs), "weights": packed(WEIGHT_SIZES, wt),
        "folds": packed(FOLD_SIZES, fd), "wmod0": a["L0_wmod"], "wmod1": a["L1_wmod"],
        "w1_d": a["L1_ffn_w1"], "w2_d": a["L1_ffn_w2"],
    }
    nc = _bacc.Bacc("TRN2", target_bir_lowering=False, num_devices=1)
    args = [nc.dram_tensor(n, v.shape, mybir.dt.from_np(v.dtype), kind="ExternalInput").ap() for n, v in arrays.items()]
    args.append(nc.dram_tensor("y_out", (B, T, D), F32, kind="ExternalOutput").ap())
    build(nc, *args)
    r = _run(nc, [arrays], core_ids=[0])
    return r.results[0]["y_out"]
```

```python
from contextlib import ExitStack

import numpy as np
import concourse.bass as bass
from concourse import mybir

F32 = mybir.dt.float32
BF16 = mybir.dt.bfloat16
U32 = mybir.dt.uint32
I32 = mybir.dt.int32
ALU = mybir.AluOpType
ACT = mybir.ActivationFunctionType
AX_X = mybir.AxisListType.X

P = 128
B, T, D = 2, 2048, 256
DC = D // P
TB = 256
NB = B * T // TB
BPB = T // TB
NT = TB // P
H, DK, DV, LR = 4, 128, 64, 16
CH = 64
NCH = TB // CH
GN = 16.0
FM, FI = 64, 16
FJ = FI // 2
DI, DS, DR, DCV = 512, 16, 64, 4
DT = DI // P
E, F = 8, 1024
K = 2 * T // E
NL = B * E
TT = T // P
SL = K // P
FT = F // P
BITS = 30
EPS = 1e-5
XBUF = 4


PER_BLOCK = dict(
    x_in=16, x_out=16, rows_out=16, x_attn=1, x_ffn=1, x_scan=1,
    turn_a=1, turn_b=1, turn_c=1, turn_d=1, hT_a=DC, hT_b=DC, hT_c=DC, hT_d=DC,
    low_rank=1, lr=1, z=2, z_read=8, z_exp=1, z_ln=1, lz_sum=1, cumsum=1, to_end=1, eG=1, emG=1, eD=1,
    v_mm=1, v_s=1, g_mm=1, sg=1, q_mm=2, k_mm=2, qg=2, kg=2, kgt_mm=2, kgt=2, att_mm=2, att=2, kv_mm=2,
    state0=1, state=NCH * H, o_mm=1, o_s=1, o_sq=1, ms_mm=1, ms_ln=1, rms=1, o_n=1, og=1, wo_mm=1,
    win_mm=1, ffn_s=1, relu=FJ, facc=FJ, wout_mm=1,
    halo=1, in_mm=4, x_cp=2, sz=2, tail=1, conv=DCV * DT, xs=1, dkq_mm=1, dkq=2, squares=1, parts=5,
    dt_mm=2, dt_sig=DT, ksum_mm=1, ksum=1, s_ksum=1, den_ln=1, den=1, dtv=1, u=1,
    k_rows=DS, q_mm2=DS // 2, q_rows=DS // 2, rate=DS, decay=DS, inp=DS, scanned=DS, saved=DS,
    read_out=DS, summed=DS, yz=1, opened=1, glast=1, out_mm=1, score_mm=1, scores=1)
PER_BLOCK.update({f"ln{n}_{what}": 1 for n in "abcd" for what in ("stats", "rstd", "rows")})
PER_BLOCK.update({f"ln{n}_var": 2 for n in "abcd"})
PER_TURN = dict(gt_mm=4 * DC, hg=4 * DC, up_mm=4 * FT, gelu=4 * FT, down_mm=4 * SL, scaled=4 * SL,
                w1_in0=16, w1_in1=16, w2_in0=16, w2_in1=16)


def shape_constants():
    p = np.arange(P)
    c = {}
    c["ident"] = np.eye(P)
    c["ones"] = np.ones((P, P))
    c["headones"] = (p[:, None] // DV == p[None, :] // DV) * 1.0
    c["before"] = (p[:, None] < p[None, :]) * 1.0
    i = np.arange(P)
    causal = (p[:, None] <= i[None, :]) & (p[:, None] // CH == i[None, :] // CH)
    c["causal"] = np.tile(causal * 1.0, (1, 4))
    c["chunkrun"] = np.tile((np.arange(H * TB) % CH != 0) * 1.0, (P, 1))
    c["tilerun"] = np.tile((np.arange(NL * TT) % TT != 0) * 1.0, (P, 1))
    r = np.arange(P)
    sel = ((r[:, None] % 32 == np.arange(32)[None, :]) & (r[:, None] < 96)) * 1.0
    c["sel"] = np.repeat(sel, P, axis=1)
    c["selk"] = np.repeat(((r % 32 < DS) & (r < 96))[:, None] * 1.0, P, axis=1)
    c["iota"] = np.tile(i, (P, 1))
    lt = np.arange(NL * TT)
    c["token"] = (lt[None, :] // TT // E) * T + (lt[None, :] % TT) * P + p[:, None]
    c["bitsf"] = np.tile(2.0 ** np.arange(BITS - 1, -1, -1), (P, 1))
    return {k: np.ascontiguousarray(v, dtype=np.float32) for k, v in c.items()}


def layout(sizes):
    at, off = {}, 0
    for name, w in sizes:
        at[name] = (off, w)
        off += w
    return at, off


CONST_SIZES = [("ident", P), ("ones", P), ("headones", P), ("before", P), ("causal", 4 * P),
               ("chunkrun", H * TB), ("tilerun", NL * TT), ("sel", 32 * P), ("selk", P), ("iota", P),
               ("token", NL * TT), ("bitsf", BITS)]
WEIGHT_SIZES = [("wq", DC * H * DK), ("wk", DC * H * DK), ("wv", DC * H * DV), ("wg", DC * H * DV),
                ("wgk1", DC * LR), ("wgk2", H * DK), ("win2", DC * P), ("inproj", DC * 2 * DI),
                ("xproj", DT * (DR + 2 * DS)), ("dthead", DI), ("gate", DC * E),
                ("bgk2", H), ("bin", 1), ("w1", FJ), ("b1", FJ), ("w2", FJ), ("b2", 1),
                ("convw", DT * DCV), ("convb", DT), ("dtb", DT), ("dskip", DT), ("gnw", 1)]
FOLD_SIZES = [("wo", DC * D), ("wout2", D), ("bout", D), ("outproj", DT * D), ("c0", DC * B), ("c1", DC * B)]
CONST_AT, CONST_W = layout(CONST_SIZES)
WEIGHT_AT, WEIGHT_W = layout(WEIGHT_SIZES)
FOLD_AT, FOLD_W = layout(FOLD_SIZES)


def build(nc, x_in, consts, weights, folds, wmod0, wmod1, w1_d, w2_d, out):
    xn_d = nc.dram_tensor("xn_rows", (B * T, D), F32, kind="Internal").ap()
    x_rows = x_in.rearrange("b t d -> (b t) d")
    out_rows = out.rearrange("b t d -> (b t) d")
    with ExitStack() as top:
        def keep(name, shape, dt=F32):
            return top.enter_context(nc.sbuf_tensor(name, shape, dt))

        names = {}

        def sem(name):
            if name not in names:
                names[name] = top.enter_context(nc.semaphore(name))
            return names[name]

        scores = keep("scores", [P, B * TT * E])
        ones_s = keep("ones_s", [P, P])
        ident_s = keep("ident_s", [P, P])
        col1 = keep("col1", [P, 6 * DC * B])
        gb1 = keep("gb1", [P, B * D])
        layers(nc, sem, x_rows, consts, weights, folds, wmod0, wmod1, out_rows, xn_d,
               scores, ones_s, ident_s, col1, gb1)
        experts(nc, sem, consts, w1_d, w2_d, out_rows, xn_d, scores, ones_s, ident_s, col1, gb1)


def layers(nc, sem, x_rows, consts, weights, folds, wmod0, wmod1, out_rows, xn_d,
           scores, ones_s, ident_s, col1, gb1):
    with ExitStack() as ctx:
        def sb(name, shape, dt=F32):
            return ctx.enter_context(nc.sbuf_tensor(name, shape, dt))

        def ps(name, shape, dt=F32):
            return ctx.enter_context(nc.psum_tensor(name, shape, dt))

        W = sb("W", [P, WEIGHT_W])

        def w(name):
            a, n = WEIGHT_AT[name]
            return W[:, a:a + n]

        def cols(name, n):
            return w(name).rearrange("p (c n) -> p c n", n=n)

        headones = sb("headones", [P, P])
        causal = sb("causal", [P, 4 * P], mybir.dt.uint8)
        chunkrun = sb("chunkrun", [P, H * TB])
        sel = sb("sel", [96, 32, P], BF16)
        selk = sb("selk", [96, P], BF16)
        epst = sb("epst", [P, 1])
        expo = sb("expo", [P, NT])
        wo_g = sb("wo_g", [P, B, DC, D])
        wout_g = sb("wout_g", [P, B, D])
        bout_g = sb("bout_g", [1, B, D])
        oproj_g = sb("oproj_g", [P, B, DT, D])
        dskip = sb("dskip", [P, DT, P])
        col0 = sb("col0", [P, 6 * DC * B])
        b1s = sb("b1s", [P, FJ])
        nbgk = sb("nbgk", [P, H])

        wq, wk = cols("wq", H * DK), cols("wk", H * DK)
        wv, wg = cols("wv", H * DV), cols("wg", H * DV)
        wgk1, wgk2 = cols("wgk1", LR), w("wgk2")
        win2, inproj = cols("win2", P), cols("inproj", 2 * DI)
        xproj, dthead, gate = cols("xproj", DR + 2 * DS), w("dthead"), cols("gate", E)

        def modcol(col, what, c, b):
            return col[:, bass.ds((what * DC + c) * B + b, 1)]

        with ExitStack() as pre:
            def tsb(name, shape, dt=F32):
                return pre.enter_context(nc.sbuf_tensor(name, shape, dt))

            cst = tsb("cst", [P, CONST_W])
            fold = tsb("fold", [P, FOLD_W])
            wmod = tsb("wmod", [P, 2, DC, 6 * D])
            silc = tsb("silc", [P, 2, DC * B])
            silr = tsb("silr", [P, 2, B, DC, P])
            gabs = tsb("gabs", [P, 4, B * D])
            gsig = tsb("gsig", [P, 4, B * D])
            gmul = tsb("gmul", [P, 3, B * D])
            wo_n = tsb("wo_n", [P, DC, D])
            pcol = pre.enter_context(nc.psum_tensor("pcol", [P, 2, 512], F32))
            prow = pre.enter_context(nc.psum_tensor("prow", [P, 4, 512], F32))

            def cs(name):
                a, n = CONST_AT[name]
                return cst[:, a:a + n]

            def fo(name):
                a, n = FOLD_AT[name]
                return fold[:, a:a + n]

            with nc.Block() as block:
                @block.sync
                def _(sp):
                    sp.dma_start(fold[:, :], folds).then_inc(sem("fold_in"), 16)
                    sp.dma_start(wmod[:, 0], wmod0.rearrange("(c p) n -> p c n", p=P)).then_inc(sem("wmod0_in"), 16)
                    sp.dma_start(cst[:, :], consts).then_inc(sem("const_in"), 16)
                    sp.dma_start(W[:, :], weights).then_inc(sem("weights_in"), 16)
                    sp.wait_ge(sem("weights_in"), 16)

                @block.scalar
                def _(act):
                    act.dma_start(wmod[:, 1], wmod1.rearrange("(c p) n -> p c n", p=P)).then_inc(sem("wmod1_in"), 16)
                    act.wait_ge(sem("fold_in"), 16)
                    for n in range(2):
                        act.activation(silc[:, n, :], fo(f"c{n}"), ACT.Silu).then_inc(sem("silc"), 1)
                    for g in range(4):
                        act.wait_ge(sem("rows"), g + 1)
                        act.activation(gabs[:, g, :], prow[:, g, :], ACT.Abs).then_inc(sem("gabs"), 1)

                @block.gpsimd
                def _(pool):
                    for name, n in (PER_BLOCK | PER_TURN).items():
                        pool.sem_inc(sem(name), n)

                @block.tensor
                def _(pe):
                    pe.wait_ge(sem("silc"), 2)
                    pe.wait_ge(sem("wmod0_in"), 16)
                    for n in range(2):
                        if n == 1:
                            pe.wait_ge(sem("wmod1_in"), 16)
                        for m in range(6 * DC):
                            for c in range(DC):
                                last = pe.matmul(pcol[:, n, m * B:(m + 1) * B], wmod[:, n, c, m * P:(m + 1) * P],
                                                 silc[:, n, c * B:(c + 1) * B], start=(c == 0), stop=(c == DC - 1))
                        last.then_inc(sem("modcols"), 1)
                    pe.wait_ge(sem("silr"), 2 * B * DC)
                    for n in range(2):
                        for g in range(2):
                            what = 2 + 3 * g
                            for b in range(B):
                                for c in range(DC):
                                    last = pe.matmul(prow[:, 2 * n + g, b * D:(b + 1) * D], silr[:, n, b, c, :],
                                                     wmod[:, n, c, what * D:(what + 1) * D],
                                                     start=(c == 0), stop=(c == DC - 1))
                            last.then_inc(sem("rows"), 1)

                @block.vector
                def _(dve):
                    dve.memset(epst[:, :], EPS)
                    dve.memset(expo[:, :], -0.5)
                    dve.wait_ge(sem("const_in"), 16)
                    dve.wait_ge(sem("silc"), 2)
                    for n in range(2):
                        for b in range(B):
                            for c in range(DC):
                                dve.tensor_scalar(silr[:, n, b, c, :], cs("ones"), silc[:, n, c * B + b:c * B + b + 1],
                                                  None, ALU.mult).then_inc(sem("silr"), 1)
                    dve.tensor_copy(headones[:, :], cs("headones"))
                    dve.tensor_copy(ones_s[:, :], cs("ones"))
                    dve.tensor_copy(ident_s[:, :], cs("ident"))
                    dve.tensor_copy(causal[:, :], cs("causal"))
                    dve.tensor_copy(chunkrun[:, :], cs("chunkrun"))
                    dve.tensor_copy(sel[:, :, :].rearrange("p a b -> p (a b)"), cs("sel")[0:96])
                    dve.tensor_copy(selk[:, :], cs("selk")[0:96])
                    for n, col in enumerate((col0, col1)):
                        dve.wait_ge(sem("modcols"), n + 1)
                        dve.tensor_copy(col[:, :], pcol[:, n, 0:6 * DC * B]).then_inc(sem("col"), 1)
                    dve.wait_ge(sem("col"), 2)
                    for col in (col0, col1):
                        for what in (1, 4):
                            v = col[:, what * DC * B:(what + 1) * DC * B]
                            dve.tensor_scalar(v, v, 1.0, None, ALU.add)
                    for g in range(4):
                        dve.wait_ge(sem("gabs"), g + 1)
                        dve.tensor_scalar(gsig[:, g, :], prow[:, g, :], 0.0, 2.0, ALU.is_ge, ALU.mult)\
                            .then_inc(sem("gsig"), 1)
                        dve.tensor_scalar(gabs[:, g, :], gabs[:, g, :], 0.25, None, ALU.max).then_inc(sem("gsig"), 1)
                        dve.wait_ge(sem("gsig"), 2 * g + 2)
                        to = gmul[:, g, :] if g < 3 else gb1[:, :]
                        dve.scalar_tensor_tensor(to, gsig[:, g, :], -1.0, gabs[:, g, :], ALU.add, ALU.mult)\
                            .then_inc(sem("gates"), 1)
                    dve.wait_ge(sem("gates"), 4)
                    dve.wait_ge(sem("weights_in"), 16)
                    dve.tensor_scalar(wo_n[:, :, :].rearrange("p c n -> p (c n)"), fo("wo"), w("gnw"), None, ALU.mult)\
                        .then_inc(sem("wo_n"), 1)
                    dve.wait_ge(sem("wo_n"), 1)
                    for b in range(B):
                        ga0, gb0, ga1 = (gmul[:, g, b * D:(b + 1) * D] for g in range(3))
                        for c in range(DC):
                            dve.tensor_tensor(wo_g[:, b, c, :], wo_n[:, c, :], ga0, ALU.mult)
                        dve.tensor_tensor(wout_g[:, b, :], fo("wout2"), gb0, ALU.mult)
                        dve.tensor_tensor(bout_g[0:1, b, :], fo("bout")[0:1], gb0[0:1], ALU.mult)
                        for k in range(DT):
                            dve.tensor_tensor(oproj_g[:, b, k, :], fo("outproj")[:, k * D:(k + 1) * D], ga1, ALU.mult)
                    for k in range(DT):
                        dve.tensor_scalar(dskip[:, k, :], cs("ident"), w("dskip")[:, k:k + 1], None, ALU.mult)
                    dve.scalar_tensor_tensor(b1s[:, :], w("w1"), w("bin"), w("b1"), ALU.mult, ALU.add)
                    dve.tensor_scalar(nbgk[:, :], w("bgk2"), -1.0, None, ALU.mult)

        xt = sb("xt", [P, XBUF * NT * D])
        stat = {n: sb(f"stat_{n}", [P, NT, 6]) for n in "abcd"}
        mv = {n: sb(f"mv_{n}", [P, NT, 2]) for n in "abcd"}
        ve = {n: sb(f"ve_{n}", [P, NT]) for n in "abcd"}
        rstd = {n: sb(f"rstd_{n}", [P, NT]) for n in "abcd"}
        xnA = sb("xnA", [P, NT, D])
        hA = sb("hA", [P, DC, TB])
        lr = sb("lr", [LR, TB])
        lz = sb("lz", [P, H * TB])
        rz = sb("rz", [P, H * TB])
        qg = sb("qg", [P, H, TB])
        kin = sb("kin", [P, H, TB])
        kg = sb("kg", [P, H, TB])
        glast = sb("glast", [P, H, NCH])
        v = sb("v", [P, NT, H * DV])
        vh = sb("vh", [P, NT, 2, H * DV])
        sg = sb("sg", [P, DC * TB])
        kgt = sb("kgt", [P, NT, H, DK])
        att = sb("att", [P, NT, H, P])
        S = sb("S", [P, 2 + NCH, H * DV])
        o_s, o_q = lz[:, 0:DC * TB], lz[:, DC * TB:2 * DC * TB]
        rms, og = rz[:, 0:DC * TB], rz[:, DC * TB:2 * DC * TB]
        s_f = sb("s_f", [P, TB])
        rel = sb("rel", [P, 4, TB])
        facc = sb("facc", [P, TB])
        xnB = sb("xnB", [P, NT, D])
        hB = sb("hB", [P, DC, TB])
        xraw = sb("xraw", [P, DT, TB + DCV - 1])
        tail = sb("tail", [P, 2 * DT * (DCV - 1)])
        xs = sb("xs", [P, DT, TB])
        sz = sb("sz", [P, 2 * DT * TB])
        dtl = sb("dtl", [DR, TB])
        kx = sb("kx", [32, 2, TB])
        kr = sb("kr", [32, 2, TB])
        km = sb("km", [32, 2, TB], BF16)
        k3 = sb("k3", [96, 2 * 2 * TB], BF16)
        ksum = sb("ksum", [P, TB])
        dtv = sb("dtv", [P, 2 * DT * TB])
        tmp = sb("tmp", [P, DT, TB])
        u = sb("u", [P, 2 * DT * TB])
        dec = sb("dec", [P, 2, DT, TB])
        st = sb("st", [P, 3, DT, TB])
        qb = sb("qb", [P, 2, 2 * TB])
        last = sb("last", [P, 2 * DS * DT])
        xo = sb("xo", [P, NT, D])
        xnC = sb("xnC", [P, NT, D])

        pA = [ps(f"pA{i}", [P, 512]) for i in range(2)]
        pB = ps("pB", [P, 512])
        pK = [ps(f"pK{i}", [P, 512]) for i in range(2)]
        pQ = ps("pQ", [P, 512])
        pY = ps("pY", [P, DT, TB])

        def after(eng, name, value):
            if not (isinstance(value, int) and value <= 0):
                eng.wait_ge(sem(name), value)

        def batch(it):
            return (it - 1) // BPB

        def later(it):
            return ((it - 1) % BPB + BPB - 1) // BPB

        def x_at(it, t, n=1):
            return xt[:, bass.ds((it % XBUF) * (NT * D) + t * D, n * D)]

        def turn2(buf, it, n):
            return buf[:, bass.ds((it % 2) * n, n)]

        def flat(x):
            return x.rearrange("p a b -> p (a b)")

        def wide(x):
            return x.rearrange("p (k t) -> p k t", k=DT)

        def settled(dve):
            dve.wait_ge(sem("weights_in"), 16)

        def ln_stats(dve, it, n, src):
            for t in range(NT):
                i = dve.bn_stats(stat[n][:, t, :], src(t))
            i.then_inc(sem(f"ln{n}_stats"), 1)
            settled(dve)
            dve.wait_ge(sem(f"ln{n}_stats"), it + 1)
            for t in range(NT):
                i = dve.bn_aggr(mv[n][:, t, :], stat[n][:, t, :])
            i.then_inc(sem(f"ln{n}_var"), 1)
            dve.wait_ge(sem(f"ln{n}_var"), it * 2 + 1)
            dve.tensor_scalar(ve[n][:, :], mv[n][:, :, 1], EPS, None, ALU.add).then_inc(sem(f"ln{n}_var"), 1)

        def ln_rows(dve, it, n, src, dst):
            dve.wait_ge(sem(f"ln{n}_rstd"), it + 1)
            for t in range(NT):
                i = dve.tensor_scalar(dst[:, t, :], src(t), mv[n][:, t, 0:1], rstd[n][:, t:t + 1],
                                      ALU.subtract, ALU.mult)
            i.then_inc(sem(f"ln{n}_rows"), 1)

        def ln_pool(pool, it, n):
            pool.wait_ge(sem(f"ln{n}_var"), it * 2 + 2)
            pool.tensor_tensor(rstd[n][:, :], ve[n][:, :], expo[:, :], ALU.pow).then_inc(sem(f"ln{n}_rstd"), 1)

        def turn(pe, it, n, rows, bank):
            pe.wait_ge(sem(f"ln{n}_rows"), it + 1)
            for c in range(DC):
                for t in range(NT):
                    i = pe.transpose(bank[:, c * TB + t * P:c * TB + (t + 1) * P], rows[:, t, c * P:(c + 1) * P],
                                     ident_s[:, :])
            i.then_inc(sem(f"turn_{n}"), 1)

        def modulate(act, it, n, bank, col, scale, shift, dst):
            act.wait_ge(sem(f"turn_{n}"), it + 1)
            for c in range(DC):
                act.activation(dst[:, c, :], bank[:, c * TB:(c + 1) * TB], ACT.Identity,
                               bias=modcol(col, shift, c, batch(it)), scale=modcol(col, scale, c, batch(it)))\
                    .then_inc(sem(f"hT_{n}"), 1)

        def attn_pe(pe, it, n):
            if n == 1:
                after(pe, "x_attn", it)
                turn(pe, it, "a", xnA, pA[0])
            if n == 2:
                after(pe, "ms_ln", it)
                pe.wait_ge(sem("hT_a"), (it + 1) * DC)
                for c in range(DC):
                    i = pe.matmul(pA[1][0:LR, 0:TB], wgk1[:, c, :], hA[:, c, :], start=(c == 0), stop=(c == DC - 1))
                i.then_inc(sem("low_rank"), 1)
            if n == 3:
                pe.wait_ge(sem("lr"), it + 1)
                for h in range(H):
                    i = pe.matmul(pA[h // 2][:, (h % 2) * TB:(h % 2 + 1) * TB], wgk2[0:LR, h * DK:(h + 1) * DK],
                                  lr[:, :], start=True, stop=True)
                    if h % 2:
                        i.then_inc(sem("z"), 1)
            if n == 4:
                pe.wait_ge(sem("z_read"), it * 8 + 4)
                for t in range(NT):
                    for c in range(DC):
                        i = pe.matmul(pA[0][:, t * D:(t + 1) * D], hA[:, c, t * P:(t + 1) * P], wv[:, c, :],
                                      start=(c == 0), stop=(c == DC - 1))
                i.then_inc(sem("v_mm"), 1)
                pe.wait_ge(sem("z_read"), it * 8 + 8)
                for m in range(DC):
                    for c in range(DC):
                        i = pe.matmul(pA[1][:, m * TB:(m + 1) * TB], wg[:, c, m * P:(m + 1) * P], hA[:, c, :],
                                      start=(c == 0), stop=(c == DC - 1))
                i.then_inc(sem("g_mm"), 1)
            if n == 6:
                pe.wait_ge(sem("v_s"), it + 1)
                project(pe, wq, pA[0], 0, "q_mm")
                pe.wait_ge(sem("sg"), it + 1)
                project(pe, wk, pA[1], 0, "k_mm")
            if n in (8, 11):
                hp = (n - 8) // 3
                pe.wait_ge(sem("kg"), it * 2 + hp + 1)
                for t in range(NT):
                    for h2 in range(2):
                        i = pe.transpose(pA[hp][:, (t * 2 + h2) * P:(t * 2 + h2 + 1) * P],
                                         kg[:, 2 * hp + h2, t * P:(t + 1) * P], ident_s[:, :])
                i.then_inc(sem("kgt_mm"), 1)
                for t in range(NT):
                    for h2 in range(2):
                        h = 2 * hp + h2
                        i = pe.matmul(pA[1 - hp][:, (t * 2 + h2) * P:(t * 2 + h2 + 1) * P],
                                      kin[:, h, t * P:(t + 1) * P], qg[:, h, t * P:(t + 1) * P],
                                      start=True, stop=True)
                i.then_inc(sem("att_mm"), 1)
            if n in (9, 12):
                hp = (n - 9) // 3
                pe.wait_ge(sem("kgt"), it * 2 + hp + 1)
                for t in range(NT):
                    for h2 in range(2):
                        h = 2 * hp + h2
                        i = pe.matmul(pA[hp][:, :].rearrange("p (c h n) -> p c h n", h=2, n=DV)[:, 2 * t:2 * t + 2, h2, :],
                                      kgt[:, t, h, :], vh[:, t, :, h * DV:(h + 1) * DV], start=True, stop=True)
                i.then_inc(sem("kv_mm"), 1)
            if n == 9:
                pe.wait_ge(sem("att"), it * 2 + 1)
                project(pe, wq, pA[1], 1, "q_mm")
            if n == 10:
                pe.wait_ge(sem("state"), it * 16 + 8)
                project(pe, wk, pA[0], 1, "k_mm")
            if n == 13:
                pe.wait_ge(sem("att"), it * 2 + 2)
                pe.wait_ge(sem("state"), it * 16 + 16)
                for h in range(H):
                    hp, h2 = h // 2, h % 2
                    for t in range(NT):
                        o = pA[0][h2 * DV:(h2 + 1) * DV, hp * TB + t * P:hp * TB + (t + 1) * P]
                        pe.matmul(o, v[:, t, h * DV:(h + 1) * DV], att[:, t, h, :], start=True, stop=False,
                                  skip_group_check=True)
                        for c in (2 * t, 2 * t + 1):
                            i = pe.matmul(o[:, (c % 2) * CH:(c % 2 + 1) * CH], S[:, 1 + c, h * DV:(h + 1) * DV],
                                          qg[:, h, c * CH:(c + 1) * CH], start=False, stop=(c % 2 == 1),
                                          skip_group_check=True)
                i.then_inc(sem("o_mm"), 1)
            if n == 14:
                pe.wait_ge(sem("o_sq"), it + 1)
                pe.matmul(pA[1][:, :], headones[:, :], o_q, start=True, stop=True).then_inc(sem("ms_mm"), 1)
            if n == 15:
                pe.wait_ge(sem("og"), it + 1)
                wof = wo_g[:, :, :, :].rearrange("p b c n -> p (b c n)")
                for t in range(NT):
                    for c in range(DC):
                        i = pe.matmul(pA[0][:, t * D:(t + 1) * D], og[:, c * TB + t * P:c * TB + (t + 1) * P],
                                      wof[:, bass.ds((batch(it) * DC + c) * D, D)],
                                      start=(c == 0), stop=(c == DC - 1))
                i.then_inc(sem("wo_mm"), 1)

        def project(pe, wt, bank, hp, done):
            for h2 in range(2):
                h = 2 * hp + h2
                for c in range(DC):
                    i = pe.matmul(bank[:, h2 * TB:(h2 + 1) * TB], wt[:, c, h * DK:(h + 1) * DK], hA[:, c, :],
                                  start=(c == 0), stop=(c == DC - 1))
            i.then_inc(sem(done), 1)

        def attn_act(act, it, n):
            if n == 1:
                after(act, "k_mm", it * 2)
                modulate(act, it, "a", pA[0], col0, 1, 0, hA)
            if n == 2:
                act.wait_ge(sem("low_rank"), it + 1)
                act.activation(lr[:, :], pA[1][0:LR, 0:TB], ACT.Copy).then_inc(sem("lr"), 1)
            if n == 3:
                after(act, "wo_mm", it)
                for h in range(H):
                    if h % 2 == 0:
                        act.wait_ge(sem("z"), it * 2 + h // 2 + 1)
                    z = pA[h // 2][:, (h % 2) * TB:(h % 2 + 1) * TB]
                    act.activation(lz[:, h * TB:(h + 1) * TB], z, ACT.Abs, bias=w("bgk2")[:, h:h + 1])\
                        .then_inc(sem("z_read"), 1)
                    act.activation(rz[:, h * TB:(h + 1) * TB], z, ACT.Relu, bias=nbgk[:, h:h + 1], scale=-1.0)\
                        .then_inc(sem("z_read"), 1)
            if n == 4:
                act.wait_ge(sem("v_mm"), it + 1)
                act.activation(v[:, :, :].rearrange("p t n -> p (t n)"), pA[0][:, :], ACT.Copy)
                for half in range(2):
                    r = slice(half * CH, (half + 1) * CH)
                    i = act.activation(vh[r, :, half, :], pA[0][r, :].rearrange("p (t n) -> p t n", t=NT), ACT.Copy)
                i.then_inc(sem("v_s"), 1)
            if n == 5:
                act.wait_ge(sem("z_read"), it * 8 + 8)
                act.activation(lz[:, :], lz[:, :], ACT.Exp, scale=-1.0).then_inc(sem("z_exp"), 1)
                act.wait_ge(sem("z_exp"), it + 1)
                act.activation(lz[:, :], lz[:, :], ACT.Ln, bias=ones_s[:, 0:1]).then_inc(sem("z_ln"), 1)
                act.wait_ge(sem("g_mm"), it + 1)
                act.activation(sg[:, :], pA[1][:, :], ACT.Silu).then_inc(sem("sg"), 1)
            if n == 7:
                act.wait_ge(sem("cumsum"), it + 1)
                act.activation(flat(qg[:, :, :]), lz[:, :], ACT.Exp, scale=-1.0 / GN).then_inc(sem("eG"), 1)
                act.activation(flat(kin[:, :, :]), lz[:, :], ACT.Exp, scale=1.0 / GN).then_inc(sem("emG"), 1)
                act.wait_ge(sem("to_end"), it + 1)
                act.activation(flat(kg[:, :, :]), rz[:, :], ACT.Exp, scale=1.0 / GN).then_inc(sem("eD"), 1)
            if n in (8, 11):
                hp = (n - 8) // 3
                act.wait_ge(sem("kgt_mm"), it * 2 + hp + 1)
                act.activation(kgt[:, :, 2 * hp:2 * hp + 2, :],
                               pA[hp][:, :].rearrange("p (t h n) -> p t h n", t=NT, h=2), ACT.Copy)\
                    .then_inc(sem("kgt"), 1)
            if n == 13:
                act.wait_ge(sem("o_mm"), it + 1)
                act.activation(o_s, pA[0][:, :], ACT.Copy).then_inc(sem("o_s"), 1)
                act.activation(o_q, pA[0][:, :], ACT.Square).then_inc(sem("o_sq"), 1)
            if n == 14:
                act.wait_ge(sem("ms_mm"), it + 1)
                act.activation(rms, pA[1][:, :], ACT.Ln, bias=epst[:, :], scale=1.0 / DV).then_inc(sem("ms_ln"), 1)
                act.wait_ge(sem("ms_ln"), it + 1)
                act.activation(rms, rms, ACT.Exp, scale=-0.5).then_inc(sem("rms"), 1)

        def attn_dve(dve, it, n):
            def pair(x, hp):
                return x[:, 2 * hp:2 * hp + 2, :].rearrange("p h t -> p (h t)")

            def queries(hp, bank):
                dve.wait_ge(sem("q_mm"), it * 2 + hp + 1)
                dve.scalar_tensor_tensor(pair(qg, hp), bank[:, :], DK ** -0.5, pair(qg, hp), ALU.mult, ALU.mult)\
                    .then_inc(sem("qg"), 1)

            def keys(hp, bank):
                dve.wait_ge(sem("k_mm"), it * 2 + hp + 1)
                dve.tensor_tensor(pair(kin, hp), bank[:, :], pair(kin, hp), ALU.mult)
                dve.tensor_tensor(pair(kg, hp), bank[:, :], pair(kg, hp), ALU.mult).then_inc(sem("kg"), 1)

            def states(hp):
                dve.wait_ge(sem("kv_mm"), it * 2 + hp + 1)
                for c in range(NCH):
                    for h2 in range(2):
                        h = 2 * hp + h2
                        if c > 0:
                            dve.wait_ge(sem("state"), it * 16 + hp * 8 + 2 * c + h2 - 1)
                        dve.scalar_tensor_tensor(
                            S[:, 2 + c, h * DV:(h + 1) * DV], S[:, 1 + c, h * DV:(h + 1) * DV], glast[:, h, c:c + 1],
                            pA[hp][:, (c * 2 + h2) * DV:(c * 2 + h2 + 1) * DV],
                            ALU.mult, ALU.add).then_inc(sem("state"), 1)

            if n == 0:
                settled(dve)
                dve.wait_ge(sem("x_in"), (it + 1) * 16)
                ln_stats(dve, it, "a", lambda t: x_at(it, t))
            if n == 1:
                after(dve, "turn_a", it)
                ln_rows(dve, it, "a", lambda t: x_at(it, t), xnA)
            if n == 6:
                dve.wait_ge(sem("lz_sum"), it + 1)
                dve.tensor_tensor_scan(lz[:, :], chunkrun[:, :], lz[:, :], 0.0, ALU.mult, ALU.add)\
                    .then_inc(sem("cumsum"), 1)
                dve.wait_ge(sem("state"), it * 16)
                dve.wait_ge(sem("o_mm"), it)
                dve.tensor_copy(S[:, 1, :], flat(S[:, :, :])[:, bass.ds(later(it) * ((1 + NCH) * H * DV), H * DV)])\
                    .then_inc(sem("state0"), 1)
            if n == 8:
                dve.wait_ge(sem("eG"), it + 1)
                dve.tensor_copy(glast[:, :, :], qg[:, :, :].rearrange("p h (c t) -> p h c t", t=CH)[:, :, :, CH - 1])\
                    .then_inc(sem("glast"), 1)
                dve.wait_ge(sem("glast"), it + 1)
                queries(0, pA[0])
                dve.wait_ge(sem("eD"), it + 1)
                keys(0, pA[1])
            if n in (9, 12):
                hp = (n - 9) // 3
                settled(dve)
                dve.wait_ge(sem("att_mm"), it * 2 + hp + 1)
                dve.copy_predicated(att[:, :, 2 * hp:2 * hp + 2, :],
                                    causal[:, :].rearrange("p (t h n) -> p t h n", t=NT, h=2),
                                    pA[1 - hp][:, :].rearrange("p (t h n) -> p t h n", t=NT, h=2))\
                    .then_inc(sem("att"), 1)
            if n == 10:
                states(0)
                queries(1, pA[1])
            if n == 11:
                keys(1, pA[0])
            if n == 13:
                states(1)
            if n == 15:
                dve.wait_ge(sem("rms"), it + 1)
                dve.wait_ge(sem("o_s"), it + 1)
                dve.tensor_tensor(o_s, o_s, rms, ALU.mult).then_inc(sem("o_n"), 1)

        def attn_pool(pool, it, n):
            if n == 0:
                ln_pool(pool, it, "a")
            if n == 5:
                pool.wait_ge(sem("z_ln"), it + 1)
                pool.tensor_tensor(lz[:, :], lz[:, :], rz[:, :], ALU.add).then_inc(sem("lz_sum"), 1)
            if n == 7:
                pool.wait_ge(sem("cumsum"), it + 1)
                lv = lz[:, :].rearrange("p (n t) -> p n t", t=CH)
                pool.tensor_tensor(rz[:, :].rearrange("p (n t) -> p n t", t=CH), lv,
                                   lv[:, :, CH - 1:CH].broadcast_to([P, H * NCH, CH]), ALU.subtract)\
                    .then_inc(sem("to_end"), 1)
            if n == 15:
                pool.wait_ge(sem("o_n"), it + 1)
                pool.wait_ge(sem("sg"), it + 1)
                pool.tensor_tensor(og, o_s, sg[:, :], ALU.mult).then_inc(sem("og"), 1)

        def front_pe(pe, it, n, back):
            if n == 1:
                after(pe, "ksum", it)
                turn(pe, it, "b", xnB, pB)
            if n == 2:
                pe.wait_ge(sem("hT_b"), (it + 1) * DC)
                for c in range(DC):
                    i = pe.matmul(pB[:, 0:TB], win2[:, c, :], hB[:, c, :], start=(c == 0), stop=(c == DC - 1))
                i.then_inc(sem("win_mm"), 1)
            if n == 4:
                pe.wait_ge(sem("facc"), (it + 1) * FJ)
                pe.wait_ge(sem("ffn_s"), it + 1)
                if back is not None:
                    pe.wait_ge(sem("x_scan"), back + 1)
                bof, wof = flat(bout_g[:, :, :]), flat(wout_g[:, :, :])
                for t in range(NT):
                    pe.matmul(pB[:, t * D:(t + 1) * D], ones_s[0:1, :], bof[:, bass.ds(batch(it) * D, D)],
                              start=True, stop=False)
                    i = pe.matmul(pB[:, t * D:(t + 1) * D], facc[:, t * P:(t + 1) * P],
                                  wof[:, bass.ds(batch(it) * D, D)], start=False, stop=True)
                i.then_inc(sem("wout_mm"), 1)
            if n == 5:
                turn(pe, it, "c", xnB, pB)
            if n in (6, 7):
                for m in (2 * (n - 6), 2 * (n - 6) + 1):
                    pe.wait_ge(*((sem("hT_c"), (it + 1) * DC), (sem("x_cp"), it * 2 + 1), (sem("x_cp"), it * 2 + 2),
                                 (sem("sz"), it * 2 + 1))[m])
                    for k in range(2):
                        for c in range(DC):
                            col = (2 * m + k) * P
                            i = pe.matmul(pB[:, k * TB:(k + 1) * TB], inproj[:, c, col:col + P], hB[:, c, :],
                                          start=(c == 0), stop=(c == DC - 1))
                    i.then_inc(sem("in_mm"), 1)
            if n == 9:
                pe.wait_ge(sem("sz"), it * 2 + 2)
                if back is not None:
                    pe.wait_ge(sem("scores"), back + 1)
                pe.wait_ge(sem("xs"), it + 1)
                for lo, m, at in ((0, DR, 0), (DR, 2 * DS, TB)):
                    for k in range(DT):
                        i = pe.matmul(pB[0:m, at:at + TB], xproj[:, k, lo:lo + m], xs[:, k, :],
                                      start=(k == 0), stop=(k == DT - 1))
                i.then_inc(sem("dkq_mm"), 1)
            if n in (10, 11):
                m = n - 10
                pe.wait_ge(sem("dkq"), it * 2 + 2)
                if m == 1:
                    pe.wait_ge(sem("dt_sig"), it * DT + 2)
                for k in range(2):
                    i = pe.matmul(pB[:, k * TB:(k + 1) * TB], dthead[0:DR, (2 * m + k) * P:(2 * m + k + 1) * P],
                                  dtl[:, :], start=True, stop=True)
                i.then_inc(sem("dt_mm"), 1)
            if n == 11:
                pe.wait_ge(sem("dt_sig"), it * DT + DT)
                pe.wait_ge(sem("parts"), (it + 1) * 5)
                pe.matmul(pB[:, 0:TB], selk[:, :], k3[:, bass.ds((it % 2) * 2 * TB + TB, TB)],
                          start=True, stop=True).then_inc(sem("ksum_mm"), 1)

        def front_act(act, it, n):
            nt = DT * (DCV - 1)
            if n == 1:
                after(act, "score_mm", it - 2)
                modulate(act, it, "b", pB, col0, 4, 3, hB)
            if n == 2:
                act.wait_ge(sem("win_mm"), it + 1)
                act.activation(s_f[:, :], pB[:, 0:TB], ACT.Copy).then_inc(sem("ffn_s"), 1)
                act.wait_ge(sem("ffn_s"), it + 1)
            if n in (2, 3):
                for j in range(4 * (n - 2), 4 * (n - 2) + 4):
                    act.wait_ge(sem("facc"), it * FJ + j - 3)
                    act.activation(rel[:, j % 4, :], s_f[:, :], ACT.Relu, bias=b1s[:, j:j + 1],
                                   scale=w("w1")[:, j:j + 1]).then_inc(sem("relu"), 1)
            if n == 5:
                act.wait_ge(sem("win_mm"), it + 1)
                modulate(act, it, "c", pB, col1, 1, 0, hB)
            if n == 6:
                act.wait_ge(sem("conv"), it * 16)
                act.wait_ge(sem("tail"), it)
                act.activation(xraw[:, :, 0:DCV - 1],
                               tail[:, bass.ds(later(it) * nt, nt)].rearrange("p (k n) -> p k n", n=DCV - 1),
                               ACT.Copy).then_inc(sem("halo"), 1)
                for m in range(2):
                    act.wait_ge(sem("in_mm"), it * 4 + m + 1)
                    act.activation(xraw[:, 2 * m:2 * m + 2, DCV - 1:], pB[:, :].rearrange("p (k t) -> p k t", k=2),
                                   ACT.Copy).then_inc(sem("x_cp"), 1)
            if n == 7:
                after(act, "yz", it - 1)
                for m in range(2):
                    act.wait_ge(sem("in_mm"), it * 4 + m + 3)
                    act.activation(sz[:, bass.ds((it % 2) * (DT * TB) + m * 2 * TB, 2 * TB)], pB[:, :], ACT.Silu)\
                        .then_inc(sem("sz"), 1)
                act.wait_ge(sem("x_cp"), it * 2 + 2)
                act.wait_ge(sem("halo"), it + 1)
                act.activation(tail[:, nt:2 * nt].rearrange("p (k n) -> p k n", n=DCV - 1), xraw[:, :, TB:],
                               ACT.Copy).then_inc(sem("tail"), 1)
            if n == 8:
                act.wait_ge(sem("conv"), it * 16 + 16)
                act.activation(xs[:, :, :], xs[:, :, :], ACT.Silu).then_inc(sem("xs"), 1)
            if n == 9:
                act.wait_ge(sem("dkq_mm"), it + 1)
                act.activation(dtl[:, :], pB[0:DR, 0:TB], ACT.Copy).then_inc(sem("dkq"), 1)
                act.activation(kx[:, 0, :], pB[0:32, TB:2 * TB], ACT.Copy).then_inc(sem("dkq"), 1)
            if n in (10, 11):
                if n == 10:
                    after(act, "inp", (it - 1) * DS)
                act.wait_ge(sem("dt_mm"), it * 2 + n - 10 + 1)
                for k in (2 * (n - 10), 2 * (n - 10) + 1):
                    act.activation(dtv[:, bass.ds(((it % 2) * DT + k) * TB, TB)],
                                   pB[:, (k % 2) * TB:(k % 2 + 1) * TB], ACT.Sigmoid,
                                   bias=w("dtb")[:, k:k + 1]).then_inc(sem("dt_sig"), 1)
            if n == 11:
                act.wait_ge(sem("ksum_mm"), it + 1)
                act.activation(ksum[:, :], pB[:, 0:TB], ACT.Copy).then_inc(sem("ksum"), 1)
            if n == 13:
                act.wait_ge(sem("s_ksum"), it + 1)
                act.activation(tmp[:, :, :], tmp[:, :, :], ACT.Ln, bias=ones_s[:, 0:1]).then_inc(sem("den_ln"), 1)
                act.wait_ge(sem("den_ln"), it + 1)
                act.activation(tmp[:, :, :], tmp[:, :, :], ACT.Exp, scale=-1.0).then_inc(sem("den"), 1)

        def front_dve(dve, it, n, back):
            x_of = lambda t: x_at(it, t)
            if n == 0:
                dve.wait_ge(sem("wo_mm"), it + 1)
                dve.tensor_tensor(x_at(it, 0, NT), x_at(it, 0, NT), pA[0][:, :], ALU.add).then_inc(sem("x_attn"), 1)
                settled(dve)
                dve.wait_ge(sem("x_attn"), it + 1)
                ln_stats(dve, it, "b", x_of)
            if n == 1:
                after(dve, "turn_c", it)
                ln_rows(dve, it, "b", x_of, xnB)
            if n in (3, 4):
                for j in range(4 * (n - 3), 4 * (n - 3) + 4):
                    dve.wait_ge(sem("relu"), it * FJ + j + 1)
                    w2c = w("w2")[:, j:j + 1]
                    if j == 0:
                        dve.wait_ge(sem("wout_mm"), it)
                        dve.tensor_scalar(facc[:, :], rel[:, 0, :], w2c, w("b2"), ALU.mult, ALU.add)\
                            .then_inc(sem("facc"), 1)
                    else:
                        dve.wait_ge(sem("facc"), it * FJ + j)
                        dve.scalar_tensor_tensor(facc[:, :], rel[:, j % 4, :], w2c, facc[:, :], ALU.mult, ALU.add)\
                            .then_inc(sem("facc"), 1)
            if n == 5:
                dve.wait_ge(sem("wout_mm"), it + 1)
                dve.tensor_tensor(x_at(it, 0, NT), x_at(it, 0, NT), pB[:, :], ALU.add).then_inc(sem("x_ffn"), 1)
                settled(dve)
                dve.wait_ge(sem("x_ffn"), it + 1)
                ln_stats(dve, it, "c", x_of)
                dve.wait_ge(sem("turn_b"), it + 1)
                ln_rows(dve, it, "c", x_of, xnB)
            if n in (7, 8):
                ks = (0, 1) if n == 7 else (2, 3)
                if n == 7:
                    dve.wait_ge(sem("halo"), it + 1)
                    dve.wait_ge(sem("opened"), it)
                    dve.wait_ge(sem("u"), it)
                for j in range(DCV):
                    for k in ks:
                        done = it * 16 + (n - 7) * 8 + 2 * j + k % 2
                        if j == 0:
                            dve.wait_ge(sem("x_cp"), it * 2 + k // 2 + 1)
                            dve.tensor_scalar(xs[:, k, :], xraw[:, k, 0:TB], w("convw")[:, k * DCV:k * DCV + 1],
                                              w("convb")[:, k:k + 1], ALU.mult, ALU.add).then_inc(sem("conv"), 1)
                        else:
                            dve.wait_ge(sem("conv"), done - 1)
                            dve.scalar_tensor_tensor(xs[:, k, :], xraw[:, k, j:j + TB],
                                                     w("convw")[:, k * DCV + j:k * DCV + j + 1], xs[:, k, :],
                                                     ALU.mult, ALU.add).then_inc(sem("conv"), 1)
            if n == 10:
                dve.wait_ge(sem("dkq"), it * 2 + 2)
                dve.tensor_tensor(kx[:, 1, :], kx[:, 0, :], kx[:, 0, :], ALU.mult).then_inc(sem("squares"), 1)
                after(dve, "k_rows", (it - 1) * DS)
                after(dve, "q_mm2", (it - 1) * (DS // 2))
                dve.wait_ge(sem("squares"), it + 1)
                half = lambda r: k3[r, bass.ds((it % 2) * 2 * TB, 2 * TB)]
                dve.tensor_copy(half(slice(0, 32)), flat(kx[:, :, :])).then_inc(sem("parts"), 1)
                dve.wait_ge(sem("parts"), it * 5 + 1)
                dve.tensor_tensor(flat(kr[:, :, :]), flat(kx[:, :, :]), half(slice(0, 32)), ALU.subtract)\
                    .then_inc(sem("parts"), 1)
                dve.wait_ge(sem("parts"), it * 5 + 2)
                dve.tensor_copy(km[:, :, :], kr[:, :, :]).then_inc(sem("parts"), 1)
                dve.wait_ge(sem("parts"), it * 5 + 3)
                dve.tensor_copy(half(slice(32, 64)), flat(km[:, :, :])).then_inc(sem("parts"), 1)
                dve.tensor_tensor(half(slice(64, 96)), flat(kr[:, :, :]), flat(km[:, :, :]), ALU.subtract)\
                    .then_inc(sem("parts"), 1)
            if n == 12:
                dve.wait_ge(sem("ksum"), it + 1)
                if back is not None:
                    dve.wait_ge(sem("out_mm"), back + 1)
                dve.tensor_tensor(tmp[:, :, :], wide(turn2(dtv, it, DT * TB)),
                                  ksum[:, :].unsqueeze(1).broadcast_to([P, DT, TB]), ALU.mult)\
                    .then_inc(sem("s_ksum"), 1)

        def front_pool(pool, it, n):
            if n == 0:
                ln_pool(pool, it, "b")
            if n == 5:
                ln_pool(pool, it, "c")
            if n == 13:
                pool.wait_ge(sem("den"), it + 1)
                d = turn2(dtv, it, DT * TB)
                pool.tensor_tensor(d, d, flat(tmp[:, :, :]), ALU.mult).then_inc(sem("dtv"), 1)
            if n == 14:
                pool.wait_ge(sem("dtv"), it + 1)
                pool.tensor_tensor(turn2(u, it, DT * TB), flat(xs[:, :, :]), turn2(dtv, it, DT * TB), ALU.mult)\
                    .then_inc(sem("u"), 1)

        def spread(pe, it, n):
            if n == 0:
                pe.wait_ge(sem("parts"), (it + 1) * 5)
            pe.wait_ge(sem("inp"), it * DS + n - 1)
            base = (it % 2) * 2 * TB
            pe.matmul(pK[n % 2][:, 0:TB], sel[:, n, :], k3[:, bass.ds(base + TB, TB)], start=True, stop=True)
            pe.matmul(pK[n % 2][:, TB:2 * TB], sel[:, n, :], k3[:, bass.ds(base, TB)], start=True, stop=True)\
                .then_inc(sem("k_rows"), 1)
            if n % 2 == 0:
                pe.wait_ge(sem("q_rows"), it * (DS // 2) + n // 2)
                pe.matmul(pQ[:, 0:TB], sel[:, DS + n, :], k3[:, bass.ds(base, TB)], start=True, stop=True)
                pe.matmul(pQ[:, TB:2 * TB], sel[:, DS + n + 1, :], k3[:, bass.ds(base, TB)], start=True, stop=True)\
                    .then_inc(sem("q_mm2"), 1)

        def scan_sum(pe, it, n):
            pe.wait_ge(sem("read_out"), it * DS + n + 1)
            for m in range(DT // 2):
                i = pe.matmul(pY[:, 2 * m:2 * m + 2, :].rearrange("p k t -> p (k t)"), ident_s[:, :],
                              st[:, n % 3, 2 * m:2 * m + 2, :].rearrange("p k t -> p (k t)"),
                              start=False, stop=(n == DS - 1), skip_group_check=True)
            i.then_inc(sem("summed"), 1)

        def scan_pe_early(pe, it, n):
            if n == 0:
                spread(pe, it, 0)
                spread(pe, it, 1)
            if n + 2 < DS:
                spread(pe, it, n + 2)

        def scan_pe(pe, it, n):
            if n == 0:
                pe.wait_ge(sem("xs"), it + 1)
                pe.wait_ge(sem("yz"), it)
                for k in range(DT):
                    i = pe.matmul(pY[:, k, :], dskip[:, k, :], xs[:, k, :], start=(k % 2 == 0), stop=False,
                                  skip_group_check=True)
                i.then_inc(sem("opened"), 1)
            else:
                scan_sum(pe, it, n - 1)
            if n == DS - 1:
                scan_sum(pe, it, n)

        def q_rows(act, it, m):
            act.wait_ge(sem("q_mm2"), it * (DS // 2) + m + 1)
            act.wait_ge(sem("read_out"), it * DS + 2 * (m - 1))
            act.activation(qb[:, m % 2, :], pQ[:, :], ACT.Copy).then_inc(sem("q_rows"), 1)

        def decay(act, it, n):
            act.wait_ge(sem("rate"), it * DS + n + 1)
            act.activation(dec[:, n % 2], dec[:, n % 2], ACT.Identity, bias=ones_s[:, 0:1], scale=-1.0)\
                .then_inc(sem("decay"), 1)

        def scan_act(act, it, n):
            if n == 0:
                q_rows(act, it, 0)
                decay(act, it, 0)
            if n + 1 < DS:
                decay(act, it, n + 1)
            if n % 2 == 1 and n + 1 < DS:
                q_rows(act, it, (n + 1) // 2)

        def scan_inputs(dve, it, n):
            rows = pK[n % 2]
            if n == 0:
                dve.wait_ge(sem("dtv"), it + 1)
                dve.wait_ge(sem("u"), it + 1)
            dve.wait_ge(sem("k_rows"), it * DS + n + 1)
            dve.wait_ge(sem("scanned"), it * DS + n - 1)
            dve.tensor_tensor(dec[:, n % 2], wide(turn2(dtv, it, DT * TB)),
                              rows[:, 0:TB].unsqueeze(1).broadcast_to([P, DT, TB]), ALU.mult)\
                .then_inc(sem("rate"), 1)
            dve.wait_ge(sem("summed"), it * DS + n - 2)
            dve.tensor_tensor(st[:, n % 3], wide(turn2(u, it, DT * TB)),
                              rows[:, TB:2 * TB].unsqueeze(1).broadcast_to([P, DT, TB]), ALU.mult)\
                .then_inc(sem("inp"), 1)

        def scan_dve(dve, it, n):
            ns = DS * DT
            if n == 0:
                scan_inputs(dve, it, 0)
            if n + 1 < DS:
                scan_inputs(dve, it, n + 1)
            dve.wait_ge(sem("decay"), it * DS + n + 1)
            dve.wait_ge(sem("inp"), it * DS + n + 1)
            if n == 0:
                dve.wait_ge(sem("saved"), it * DS)
            for k in range(DT):
                i = dve.tensor_tensor_scan(st[:, n % 3, k, :], dec[:, n % 2, k, :], st[:, n % 3, k, :],
                                           last[:, bass.ds(later(it) * ns + n * DT + k, 1)], ALU.mult, ALU.add)
            i.then_inc(sem("scanned"), 1)
            dve.wait_ge(sem("scanned"), it * DS + n + 1)
            dve.tensor_copy(last[:, (DS + n) * DT:(DS + n + 1) * DT], st[:, n % 3, :, TB - 1])\
                .then_inc(sem("saved"), 1)

        def scan_pool(pool, it, n):
            pool.wait_ge(sem("saved"), it * DS + n + 1)
            pool.wait_ge(sem("q_rows"), it * (DS // 2) + n // 2 + 1)
            q = qb[:, (n // 2) % 2, (n % 2) * TB:(n % 2 + 1) * TB]
            pool.tensor_tensor(st[:, n % 3], st[:, n % 3], q.unsqueeze(1).broadcast_to([P, DT, TB]), ALU.mult)\
                .then_inc(sem("read_out"), 1)

        def back_pe(pe, it, n, front):
            if n == 3:
                if front is not None:
                    pe.wait_ge(sem("ffn_s"), front + 1)
                else:
                    pe.wait_ge(sem("ksum"), NB + 1)
                pe.wait_ge(sem("yz"), it + 1)
                opf = oproj_g[:, :, :, :].rearrange("p b k n -> p (b k n)")
                for t in range(NT):
                    for k in range(DT):
                        i = pe.matmul(pB[:, t * D:(t + 1) * D], tmp[:, k, t * P:(t + 1) * P],
                                      opf[:, bass.ds((batch(it) * DT + k) * D, D)],
                                      start=(k == 0), stop=(k == DT - 1))
                i.then_inc(sem("out_mm"), 1)
            if n == 8:
                if front is not None:
                    pe.wait_ge(sem("sz"), front * 2 + 2)
                turn(pe, it, "d", xnC, pB)
                pe.wait_ge(sem("hT_d"), (it + 1) * DC)
                for t in range(NT):
                    for c in range(DC):
                        i = pe.matmul(pB[:, t * E:(t + 1) * E], hB[:, c, t * P:(t + 1) * P], gate[:, c, :],
                                      start=(c == 0), stop=(c == DC - 1))
                i.then_inc(sem("score_mm"), 1)

        def back_act(act, it, n, front):
            if n == 8:
                if front is not None:
                    act.wait_ge(sem("in_mm"), front * 4 + 4)
                modulate(act, it, "d", pB, col1, 4, 3, hB)
                act.wait_ge(sem("score_mm"), it + 1)
                act.activation(scores[:, bass.ds((it - 1) * (NT * E), NT * E)], pB[:, 0:NT * E], ACT.Copy)\
                    .then_inc(sem("scores"), 1)

        def back_dve(dve, it, n):
            if n == 0:
                dve.wait_ge(sem("summed"), (it + 1) * DS)
                dve.tensor_tensor(tmp[:, :, :], pY[:, :, :], wide(turn2(sz, it, DT * TB)), ALU.mult)\
                    .then_inc(sem("yz"), 1)
            if n == 4:
                dve.wait_ge(sem("out_mm"), it + 1)
                dve.wait_ge(sem("x_out"), it * 16)
                dve.tensor_tensor(flat(xo[:, :, :]), x_at(it, 0, NT), pB[:, :], ALU.add).then_inc(sem("x_scan"), 1)
                settled(dve)
                dve.wait_ge(sem("x_scan"), it + 1)
                ln_stats(dve, it, "d", lambda t: xo[:, t, :])
            if n == 5:
                dve.wait_ge(sem("rows_out"), it * 16)
                after(dve, "turn_d", it)
                ln_rows(dve, it, "d", lambda t: xo[:, t, :], xnC)

        def blocks_of(i, stages):
            return [i + d if s in stages else None for s, d in (("A", 2), ("F", 1), ("S", 0), ("C", -1))]

        def turn_pe(pe, i, stages):
            a, f, s, c = blocks_of(i, stages)
            for n in range(DS):
                if s is not None:
                    scan_pe_early(pe, s, n)
                if a is not None:
                    attn_pe(pe, a, n)
                if f is not None and n != 8:
                    front_pe(pe, f, n, c)
                if s is not None:
                    scan_pe(pe, s, n)
                if c is not None:
                    back_pe(pe, c, n, f)

        def turn_act(act, i, stages):
            a, f, s, c = blocks_of(i, stages)
            for n in range(DS):
                if s is not None:
                    scan_act(act, s, n)
                if f is not None:
                    front_act(act, f, n)
                if a is not None:
                    attn_act(act, a, n)
                if c is not None:
                    back_act(act, c, n, f)

        def turn_dve(dve, i, stages):
            a, f, s, c = blocks_of(i, stages)
            for n in range(DS):
                if c is not None and n > 0:
                    back_dve(dve, c, n)
                if f is not None and n > 0:
                    front_dve(dve, f, n, c)
                if s is not None:
                    scan_dve(dve, s, n)
                if c is not None and n == 0:
                    back_dve(dve, c, n)
                if f is not None and n == 0:
                    front_dve(dve, f, n, c)
                if a is not None:
                    attn_dve(dve, a, n)

        def turn_pool(pool, i, stages):
            a, f, s, c = blocks_of(i, stages)
            for n in range(DS):
                if c is not None and n == 4:
                    ln_pool(pool, c, "d")
                if f is not None and n > 0:
                    front_pool(pool, f, n)
                if s is not None:
                    scan_pool(pool, s, n)
                if f is not None and n == 0:
                    front_pool(pool, f, n)
                if a is not None:
                    attn_pool(pool, a, n)

        def pipeline(eng, a_turn):
            a_turn(eng, -1, "A")
            a_turn(eng, 0, "AF")
            a_turn(eng, 1, "AFS")
            with eng.Fori(2, NB - 1) as i:
                a_turn(eng, i, "AFSC")
            a_turn(eng, NB - 1, "FSC")
            a_turn(eng, NB, "SC")
            a_turn(eng, NB + 1, "C")

        with nc.Block() as block:
            @block.sync
            def _(sp):
                def load(it):
                    sp.dma_start(x_at(it, 0, NT).rearrange("p (t n) -> p t n", n=D),
                                 x_rows[bass.ds((it - 1) * TB, TB), :].rearrange("(t p) n -> p t n", p=P))\
                        .then_inc(sem("x_in"), 16)

                def store(it):
                    sp.wait_ge(sem("x_scan"), it + 1)
                    sp.dma_start(out_rows[bass.ds((it - 1) * TB, TB), :].rearrange("(t p) n -> p t n", p=P),
                                 xo[:, :, :]).then_inc(sem("x_out"), 16)
                    sp.wait_ge(sem("lnd_rows"), it + 1)
                    sp.dma_start(xn_d[bass.ds((it - 1) * TB, TB), :].rearrange("(t p) n -> p t n", p=P),
                                 xnC[:, :, :]).then_inc(sem("rows_out"), 16)

                load(1)
                for it in (2, 3):
                    sp.wait_ge(sem("x_in"), it * 16)
                    load(it)
                with sp.Fori(1, NB - XBUF + 2) as it:
                    sp.wait_ge(sem("x_in"), (it + XBUF - 1) * 16)
                    load(it + XBUF - 1)
                    store(it)
                for it in range(NB - XBUF + 2, NB + 1):
                    store(it)
                sp.wait_ge(sem("x_out"), (NB + 1) * 16)
                sp.wait_ge(sem("rows_out"), (NB + 1) * 16)

            @block.tensor
            def _(pe):
                pipeline(pe, turn_pe)

            @block.scalar
            def _(act):
                act.wait_ge(sem("tail0"), 2)
                pipeline(act, turn_act)

            @block.vector
            def _(dve):
                dve.memset(att[:, :, :, :], 0.0)
                dve.memset(vh[:, :, :, :], 0.0)
                dve.memset(S[:, 0, :], 0.0)
                dve.memset(tail[:, 0:DT * (DCV - 1)], 0.0).then_inc(sem("tail0"), 1)
                dve.memset(last[:, 0:DS * DT], 0.0).then_inc(sem("tail0"), 1)
                dve.wait_ge(sem("tail0"), 2)
                pipeline(dve, turn_dve)

            @block.gpsimd
            def _(pool):
                pipeline(pool, turn_pool)


def experts(nc, sem, consts, w1_d, w2_d, out_rows, xn_d, scores, ones_s, ident_s, col1, gb1):
    with ExitStack() as ctx:
        def sb(name, shape, dt=F32):
            return ctx.enter_context(nc.sbuf_tensor(name, shape, dt))

        def ps(name, shape, dt=F32):
            return ctx.enter_context(nc.psum_tensor(name, shape, dt))

        def chain(eng, instruction, s):
            count[s] = count.get(s, 0) + 1
            instruction.then_inc(sem(s), 1)
            eng.wait_ge(sem(s), count[s])

        count = {}
        LT = NL * TT
        before = sb("before", [P, P])
        tilerun = sb("tilerun", [P, LT])
        iota = sb("iota", [P, P])
        token = sb("token", [P, LT])
        bitsf = sb("bitsf", [P, BITS])
        bitsu = sb("bitsu", [P, BITS], U32)
        red = sb("red", [P, B * TT])
        prob = sb("prob", [P, B * TT, E])
        pl = sb("pl", [P, LT])
        thr = sb("thr", [P, NL], U32)
        cand = sb("cand", [P, NL], U32)
        hit = sb("hit", [P, LT])
        cnt = sb("cnt", [P, NL])
        step = sb("step", [P, NL], U32)
        eq = sb("eq", [P, LT])
        tot = sb("tot", [P, LT])
        run = sb("run", [P, LT])
        pos = sb("pos", [P, LT])
        need = sb("need", [P, NL])
        posi = sb("posi", [P, LT], I32)
        loi = sb("loi", [P, LT], I32)
        lo = sb("lo", [P, LT])
        hi = sb("hi", [P, LT])
        what = sb("what", [P, NL, TT, 2 * SL])
        onehot = sb("onehot", [P, 2, TT, P])
        slots = sb("slots", [P, NL, 2 * SL])
        ids = sb("ids", [P, NL, SL], U32)
        w1s = sb("w1s", [P, 2, DC, F])
        w2s = sb("w2s", [P, 2, FT, D])
        xg = sb("xg", [P, 2, SL, D])
        hg = sb("hg", [P, DC, K])
        h1 = sb("h1", [P, FT, K])
        ys = sb("ys", [P, 2, SL, D])
        pc = ps("pc", [P, 2, 512])
        pt = ps("pt", [P, 2, 512])
        ph = ps("ph", [P, 2, 512])
        po = ps("po", [P, 2, 512])

        def lists(x):
            return x.rearrange("p (l t) -> p l t", t=TT)

        def spread(x):
            return x.unsqueeze(2).broadcast_to([P, NL, TT])

        ITEMS = NL // 4

        with nc.Block() as block:
            @block.sync
            def _(sp):
                def load(e, slot):
                    sp.dma_start(w1s[:, slot], w1_d[bass.ds(e, 1)].rearrange("e (c p) f -> p (e c) f", p=P))\
                        .then_inc(sem(f"w1_in{slot}"), 16)
                    sp.dma_start(w2s[:, slot], w2_d[bass.ds(e, 1)].rearrange("e (c p) f -> p (e c) f", p=P))\
                        .then_inc(sem(f"w2_in{slot}"), 16)

                for name, dst in (("before", before), ("tilerun", tilerun), ("iota", iota), ("token", token),
                                  ("bitsf", bitsf)):
                    a, n = CONST_AT[name]
                    sp.dma_start(dst[:, :], consts[:, a:a + n]).then_inc(sem("const2_in"), 16)
                load(0, 0)
                load(1, 1)
                with sp.Fori(1, ITEMS) as i:
                    for slot in range(2):
                        sp.wait_ge(sem("down_mm"), i * 4 * SL + (slot + 1) * 2 * SL)
                        load(2 * i + slot, slot)

            @block.vector
            def _(dve):
                def do(instruction):
                    chain(dve, instruction, "sel_step")

                sc = scores[:, :].rearrange("p (t e) -> p t e", e=E)
                do(dve.tensor_reduce(red[:, :], sc, AX_X, ALU.max))
                do(dve.tensor_tensor(sc, sc, red[:, :].unsqueeze(2).broadcast_to([P, B * TT, E]), ALU.subtract))
                dve.wait_ge(sem("const2_in"), 80)
                do(dve.tensor_copy(bitsu[:, :], bitsf[:, :]))
                do(dve.memset(thr[:, :], 0))
                dve.wait_ge(sem("prob_exp"), 1)
                do(dve.tensor_reduce(red[:, :], prob[:, :, :], AX_X, ALU.add))
                do(dve.reciprocal(red[:, :], red[:, :]))
                for b in range(B):
                    i = dve.tensor_tensor(
                        lists(pl[:, :])[:, b * E:(b + 1) * E, :],
                        prob[:, b * TT:(b + 1) * TT, :].rearrange("p t e -> p e t"),
                        red[:, b * TT:(b + 1) * TT].unsqueeze(1).broadcast_to([P, E, TT]), ALU.mult)
                do(i)
                with dve.Fori(0, BITS) as i:
                    dve.tensor_tensor(cand[:, :], thr[:, :], bitsu[:, bass.ds(i, 1)].broadcast_to([P, NL]),
                                      ALU.bitwise_or).then_inc(sem("t_cand"), 1)
                    dve.wait_ge(sem("t_cand"), i + 1)
                    dve.tensor_tensor(lists(hit[:, :]), lists(pl[:, :]), spread(cand[:, :].bitcast(F32)), ALU.is_ge)\
                        .then_inc(sem("t_hit"), 1)
                    dve.wait_ge(sem("t_hit"), i + 1)
                    dve.tensor_reduce(cnt[:, :], lists(hit[:, :]), AX_X, ALU.add).then_inc(sem("t_cnt"), 1)
                    dve.wait_ge(sem("t_all"), i + 1)
                    dve.tensor_scalar(step[:, :], pc[:, 0, 0:NL], float(K), bitsf[:, bass.ds(i, 1)],
                                      ALU.is_ge, ALU.mult).then_inc(sem("t_step"), 1)
                    dve.wait_ge(sem("t_step"), i + 1)
                    dve.tensor_tensor(thr[:, :], thr[:, :], step[:, :], ALU.bitwise_or).then_inc(sem("t_thr"), 1)
                    dve.wait_ge(sem("t_thr"), i + 1)
                tf = spread(thr[:, :].bitcast(F32))
                do(dve.tensor_tensor(lists(hit[:, :]), lists(pl[:, :]), tf, ALU.is_gt))
                do(dve.tensor_tensor(lists(eq[:, :]), lists(pl[:, :]), tf, ALU.is_equal))
                dve.tensor_reduce(cnt[:, :], lists(hit[:, :]), AX_X, ALU.add).then_inc(sem("above"), 1)

                def ranks(src_ready, dst):
                    dve.wait_ge(sem("prefix"), src_ready)
                    do(dve.tensor_copy(tot[:, :], pc[:, 1, LT:2 * LT]))
                    do(dve.tensor_tensor_scan(run[:, :], tilerun[:, :], tot[:, :], 0.0, ALU.mult, ALU.add))
                    do(dve.tensor_tensor(run[:, :], run[:, :], tot[:, :], ALU.subtract))
                    do(dve.tensor_tensor(dst[:, :], run[:, :], pc[:, 1, 0:LT], ALU.add))

                dve.wait_ge(sem("t_all"), BITS + 1)
                do(dve.tensor_scalar(need[:, :], pc[:, 0, 0:NL], -1.0, float(K), ALU.mult, ALU.add))
                ranks(1, pos)
                do(dve.tensor_tensor(lists(pos[:, :]), lists(pos[:, :]), spread(need[:, :]), ALU.is_lt))
                do(dve.tensor_tensor(eq[:, :], eq[:, :], pos[:, :], ALU.mult))
                do(dve.tensor_tensor(hit[:, :], hit[:, :], eq[:, :], ALU.add))
                dve.sem_inc(sem("marked"), 1)
                ranks(2, pos)
                do(dve.scalar_tensor_tensor(pos[:, :], pos[:, :], 1.0, hit[:, :], ALU.add, ALU.mult))
                do(dve.tensor_scalar(posi[:, :], pos[:, :], -1.0, None, ALU.add))
                do(dve.tensor_scalar(loi[:, :], posi[:, :], P - 1, None, ALU.bitwise_and))
                do(dve.tensor_copy(lo[:, :], loi[:, :]))
                do(dve.tensor_scalar(loi[:, :], posi[:, :], 7, None, ALU.arith_shift_right))
                do(dve.tensor_copy(hi[:, :], loi[:, :]))
                for c in range(SL):
                    dve.scalar_tensor_tensor(what[:, :, :, c].rearrange("p l t -> p (l t)"), hi[:, :], float(c),
                                             token[:, :], ALU.is_equal, ALU.mult)
                    i = dve.scalar_tensor_tensor(what[:, :, :, SL + c].rearrange("p l t -> p (l t)"), hi[:, :],
                                                 float(c), pl[:, :], ALU.is_equal, ALU.mult)
                i.then_inc(sem("what"), 1)
                for li in range(NL):
                    if li >= 2:
                        dve.wait_ge(sem("slot_mm"), li - 1)
                    dve.tensor_tensor(onehot[:, li % 2], iota[:, :].unsqueeze(1).broadcast_to([P, TT, P]),
                                      lists(lo[:, :])[:, li, :].unsqueeze(2).broadcast_to([P, TT, P]), ALU.is_equal)\
                        .then_inc(sem("onehot"), 1)
                dve.wait_ge(sem("slot_mm"), NL)
                dve.tensor_copy(slots[:, :, :].rearrange("p l c -> p (l c)"), pt[:, 0, 0:NL * 2 * SL])\
                    .then_inc(sem("slots"), 1)
                dve.wait_ge(sem("slots"), 1)
                dve.tensor_copy(ids[:, :, :], slots[:, :, 0:SL]).then_inc(sem("ids"), 1)

                sf = slots[:, :, :].rearrange("p l c -> p (l c)")
                with dve.Fori(1, ITEMS + 1) as i:
                    for n in range(4):
                        e2, b = n // 2, n % 2
                        for c in range(SL):
                            dve.wait_ge(sem("down_mm"), i * 4 * SL + n * SL + c + 1)
                            if c == 0:
                                dve.wait_ge(sem("ys_free"), (i - 1) * 4 + n + 1)
                            dve.scalar_tensor_tensor(
                                ys[:, b, c, :], po[:, c % 2, 0:D],
                                sf[:, bass.ds((b * E + e2) * 2 * SL + SL + c + (i - 1) * (2 * 2 * SL), 1)],
                                gb1[:, b * D:(b + 1) * D], ALU.mult, ALU.mult).then_inc(sem("scaled"), 1)

            @block.scalar
            def _(act):
                act.wait_ge(sem("sel_step"), 2)
                act.activation(prob[:, :, :].rearrange("p t e -> p (t e)"), scores[:, :], ACT.Exp)\
                    .then_inc(sem("prob_exp"), 1)
                with act.Fori(1, ITEMS + 1) as i:
                    for n in range(4):
                        b = n % 2
                        for c in range(DC):
                            act.wait_ge(sem("gt_mm"), i * 8 + n * 2 + c + 1)
                            sc, sh = ((what * DC + c) * B + b for what in (4, 3))
                            act.activation(hg[:, c, :], pt[:, c, :], ACT.Identity, bias=col1[:, sh:sh + 1],
                                           scale=col1[:, sc:sc + 1]).then_inc(sem("hg"), 1)
                        for f in range(FT):
                            act.wait_ge(sem("up_mm"), i * 4 * FT + n * FT + f + 1)
                            if f == 0:
                                act.wait_ge(sem("down_mm"), i * 4 * SL + n * SL)
                            act.activation(h1[:, f, :], ph[:, f % 2, :], ACT.Gelu).then_inc(sem("gelu"), 1)

            @block.tensor
            def _(pe):
                with pe.Fori(0, BITS) as i:
                    pe.wait_ge(sem("t_cnt"), i + 1)
                    pe.matmul(pc[:, 0, 0:NL], ones_s[:, :], cnt[:, :], start=True, stop=True).then_inc(sem("t_all"), 1)
                pe.wait_ge(sem("above"), 1)
                pe.wait_ge(sem("t_step"), BITS)
                pe.matmul(pc[:, 0, 0:NL], ones_s[:, :], cnt[:, :], start=True, stop=True).then_inc(sem("t_all"), 1)
                for n, marks in enumerate((eq, hit)):
                    if n == 1:
                        pe.wait_ge(sem("marked"), 1)
                    pe.matmul(pc[:, 1, 0:LT], before[:, :], marks[:, :], start=True, stop=True)
                    pe.matmul(pc[:, 1, LT:2 * LT], ones_s[:, :], marks[:, :], start=True, stop=True)\
                        .then_inc(sem("prefix"), 1)
                pe.wait_ge(sem("what"), 1)
                for li in range(NL):
                    pe.wait_ge(sem("onehot"), li + 1)
                    for t in range(TT):
                        m = pe.matmul(pt[:, 0, li * 2 * SL:(li + 1) * 2 * SL], onehot[:, li % 2, t, :],
                                      what[:, li, t, :], start=(t == 0), stop=(t == TT - 1))
                    m.then_inc(sem("slot_mm"), 1)
                pe.wait_ge(sem("slots"), 1)
                with pe.Fori(1, ITEMS + 1) as i:
                    for n in range(4):
                        e2, b = n // 2, n % 2
                        pe.wait_ge(sem(f"rows_in{b}"), ((i - 1) * 2 + e2 + 1) * SL * 16)
                        pe.wait_ge(sem("hg"), i * 8 + n * 2)
                        for c in range(DC):
                            for s in range(SL):
                                m = pe.transpose(pt[:, c, s * P:(s + 1) * P], xg[:, n % 2, s, c * P:(c + 1) * P],
                                                 ident_s[:, :])
                            m.then_inc(sem("gt_mm"), 1)
                        pe.wait_ge(sem("hg"), i * 8 + n * 2 + 2)
                        if b == 0:
                            pe.wait_ge(sem(f"w1_in{e2}"), (i + 1) * 16)
                            pe.wait_ge(sem(f"w2_in{e2}"), (i + 1) * 16)
                        for f in range(FT):
                            pe.wait_ge(sem("gelu"), i * 4 * FT + n * FT + f - 1)
                            for c in range(DC):
                                m = pe.matmul(ph[:, f % 2, :], w1s[:, e2, c, f * P:(f + 1) * P], hg[:, c, :],
                                              start=(c == 0), stop=(c == DC - 1))
                            m.then_inc(sem("up_mm"), 1)
                        pe.wait_ge(sem("gelu"), i * 4 * FT + (n + 1) * FT)
                        for s in range(SL):
                            k = n * SL + s
                            pe.wait_ge(sem("scaled"), i * 4 * SL + k - 1)
                            for f in range(FT):
                                m = pe.matmul(po[:, s % 2, 0:D], h1[:, f, s * P:(s + 1) * P], w2s[:, e2, f, :],
                                              start=(f == 0), stop=(f == FT - 1))
                            m.then_inc(sem("down_mm"), 1)

            @block.gpsimd
            def _(pool):
                pool.wait_ge(sem("ids"), 1)

                def gather(n):
                    e, b = n // 2, n % 2
                    for s in range(SL):
                        pool.indirect_dma_start(
                            xg[:, b, s, :], None, xn_d[:, :],
                            bass.IndirectOffsetOnAxis(ap=ids[:, b * E + e, s:s + 1], axis=0))\
                            .then_inc(sem(f"rows_in{b}"), 16)

                def scatter(n):
                    e, b = n // 2, n % 2
                    pool.wait_ge(sem("scaled"), PER_TURN["scaled"] + (n + 1) * SL)
                    for s in range(SL):
                        pool.indirect_dma_start(
                            out_rows, bass.IndirectOffsetOnAxis(ap=ids[:, b * E + e, s:s + 1], axis=0),
                            ys[:, b, s, :], None, compute_op=ALU.add).then_inc(sem(f"added{b}"), 16)

                gather(0)
                gather(1)
                for n in range(NL):
                    if n >= 2:
                        pool.wait_ge(sem(f"added{n % 2}"), n // 2 * SL * 16)
                    pool.sem_inc(sem("ys_free"), 1)
                    if n + 2 < NL:
                        pool.wait_ge(sem("gt_mm"), PER_TURN["gt_mm"] + (n + 1) * DC)
                        gather(n + 2)
                    scatter(n)
                for b in range(B):
                    pool.wait_ge(sem(f"added{b}"), E * SL * 16)


def rows_of_chunks(a):
    n = a.shape[1]
    c = -(-a.shape[0] // P)
    full = np.zeros((c * P, n), np.float32)
    full[:a.shape[0]] = a
    return full.reshape(c, P, n).transpose(1, 0, 2).reshape(P, c * n)


def kernel(**inputs):
    import concourse.bacc as _bacc
    from concourse.bass_utils import run_bass_kernel_spmd as _run

    a = {k: np.asarray(v) for k, v in inputs.items()}
    col = lambda x: x.reshape(-1, P).T
    two = lambda x: np.concatenate([x, x], axis=-1)

    def pair(x):
        return np.concatenate([x[:, 0::2], x[:, 1::2]], axis=0)

    wt = {
        "wq": rows_of_chunks(a["L0_attn_Wq"]), "wk": rows_of_chunks(a["L0_attn_Wk"]),
        "wv": rows_of_chunks(a["L0_attn_Wv"]), "wg": rows_of_chunks(a["L0_attn_Wg"]),
        "wgk1": rows_of_chunks(a["L0_attn_Wgk1"]), "wgk2": rows_of_chunks(a["L0_attn_Wgk2"]),
        "win2": rows_of_chunks(two(a["L0_ffn_Win"])), "inproj": rows_of_chunks(a["L1_attn_in_proj_w"].T),
        "xproj": rows_of_chunks(a["L1_attn_x_proj_w"].T), "dthead": rows_of_chunks(a["L1_attn_dt_head_w"].T),
        "gate": rows_of_chunks(a["L1_ffn_gate_w"].T), "bgk2": col(a["L0_attn_bgk2"]),
        "bin": two(a["L0_ffn_bin_"])[:, None], "w1": pair(a["L0_ffn_W1"]), "b1": pair(a["L0_ffn_b1"]),
        "w2": pair(a["L0_ffn_W2"]),
        "b2": np.concatenate([a["L0_ffn_b2"], np.zeros(FM, np.float32)])[:, None],
        "convw": a["L1_attn_conv_w"].reshape(DT, P, DCV).transpose(1, 0, 2).reshape(P, DT * DCV),
        "convb": col(a["L1_attn_conv_b"]), "dtb": col(a["L1_attn_dt_head_b"]), "dskip": col(a["L1_attn_D"]),
        "gnw": two(a["L0_attn_gnw"])[:, None],
    }
    fd = {
        "wo": rows_of_chunks(a["L0_attn_Wo"]),
        "wout2": np.concatenate([a["L0_ffn_Wout"], a["L0_ffn_Wout"]], axis=0),
        "bout": rows_of_chunks(a["L0_ffn_bout"][None, :]),
        "outproj": rows_of_chunks(a["L1_attn_out_proj_w"].T),
        "c0": rows_of_chunks(a["L0_c"].T), "c1": rows_of_chunks(a["L1_c"].T),
    }
    cs = shape_constants()
    packed = lambda sizes, parts: np.ascontiguousarray(np.concatenate([parts[n] for n, _ in sizes], axis=1))
    arrays = {
        "x_in": a["L0_attn_x"], "consts": packed(CONST_SIZES, cs), "weights": packed(WEIGHT_SIZES, wt),
        "folds": packed(FOLD_SIZES, fd), "wmod0": a["L0_wmod"], "wmod1": a["L1_wmod"],
        "w1_d": a["L1_ffn_w1"], "w2_d": a["L1_ffn_w2"],
    }
    nc = _bacc.Bacc("TRN2", target_bir_lowering=False, num_devices=1)
    args = [nc.dram_tensor(n, v.shape, mybir.dt.from_np(v.dtype), kind="ExternalInput").ap() for n, v in arrays.items()]
    args.append(nc.dram_tensor("y_out", (B, T, D), F32, kind="ExternalOutput").ap())
    build(nc, *args)
    r = _run(nc, [arrays], core_ids=[0])
    return r.results[0]["y_out"]
```

```python
from contextlib import ExitStack

import numpy as np
import concourse.bass as bass
from concourse import mybir

F32 = mybir.dt.float32
BF16 = mybir.dt.bfloat16
U32 = mybir.dt.uint32
I32 = mybir.dt.int32
F32R = mybir.dt.float32r
ALU = mybir.AluOpType
ACT = mybir.ActivationFunctionType
AX_X = mybir.AxisListType.X

P = 128
B, T, D = 2, 2048, 256
DC = D // P
TB = 256
NB = B * T // TB
BPB = T // TB
NT = TB // P
H, DK, DV, LR = 4, 128, 64, 16
CH = 64
NCH = TB // CH
GN = 16.0
FM, FI = 64, 16
FJ = FI // 2
DI, DS, DR, DCV = 512, 16, 64, 4
DT = DI // P
E, F = 8, 1024
K = 2 * T // E
NL = B * E
TT = T // P
SEG = P // NL
SW = T // SEG
ST = SW // P
SL = K // P
FT = F // P
UPPER = -4096
BITS = 30
EPS = 1e-5
XBUF = 4


PER_BLOCK = dict(
    x_in=16, x_out=16, rows_out=16, x_attn=1, x_ffn=1, x_scan=1,
    turn_a=1, turn_b=1, turn_c=1, turn_d=1, hT_a=DC, hT_b=DC, hT_c=DC, hT_d=DC,
    low_rank=1, lr=1, z=2, z_read=8, z_exp=1, z_ln=1, lz_sum=1, cumsum=1, to_end=1, eG=1, emG=1, eD=1,
    v_mm=1, v_s=1, g_mm=1, sg=1, q_mm=2, k_mm=2, qg=2, kg=2, kgt_mm=2, kgt=2, att_mm0=1, att_mm1=1, att=2, kv_mm=2,
    state0=1, state=NCH * H, o_mm=1, o_s=1, o_sq=1, ms_mm=1, ms_ln=1, rms=1, o_n=1, og=1, wo_mm=1,
    win_mm=1, ffn_s=1, relu=FJ, facc=FJ, wout_mm=1,
    halo=1, in_mm=4, x_cp=2, sz=2, tail=1, conv=DCV * DT, xs=1, dkq_mm=1, dkq=2, parts=4,
    dt_mm=2, dt_sig=DT, ksum_mm=1, ksum=1, s_ksum=1, den_ln=1, den=1, dtv=1, u=1,
    k_rows=DS, q_mm2=DS // 2, q_rows=DS // 2, rate=DS, decay=DS, inp=DS, scanned=DS, saved=DS,
    carried=DS, read_out=DS, paired=DS // 2, summed=DS // 2, yz=1, opened=1, glast=1, out_mm=1, score_mm=1, scores=1)
PER_BLOCK.update({f"ln{n}_{what}": 1 for n in "abcd" for what in ("stats", "rstd", "rows")})
PER_BLOCK.update({f"ln{n}_var": 2 for n in "abcd"})
PER_TURN = dict(gt_mm=4 * DC, hg=4 * DC, hg_split=4 * DC, up_mm=4 * FT, gelu=4 * FT, h1_split=4 * FT,
                down_mm=4 * SL, scaled=4 * SL)


def shape_constants():
    p = np.arange(P)
    c = {}
    c["ident"] = np.eye(P)
    c["ones"] = np.ones((P, P))
    c["headones"] = (p[:, None] // DV == p[None, :] // DV) * 1.0
    c["samelist"] = (p[:, None] // SEG == p[None, :] // SEG) * 1.0
    c["segbefore"] = ((p[:, None] // SEG == p[None, :] // SEG) & (p[:, None] < p[None, :])) * 1.0
    i = np.arange(P)
    causal = (p[:, None] <= i[None, :]) & (p[:, None] // CH == i[None, :] // CH)
    c["causal"] = np.tile(causal * 1.0, (1, 4))
    c["chunkrun"] = np.tile((np.arange(H * TB) % CH != 0) * 1.0, (P, 1))
    r = np.arange(P)
    sel = ((r[:, None] % 32 == np.arange(32)[None, :]) & (r[:, None] < 96)) * 1.0
    c["sel"] = np.repeat(sel, P, axis=1)
    c["selk"] = np.repeat(((r % 32 < DS) & (r < 96))[:, None] * 1.0, P, axis=1)
    c["iota"] = np.tile(i, (P, 1))
    lt = np.arange(NL * TT)
    token = (lt[None, :] // TT % B) * T + (lt[None, :] % TT) * P + p[:, None]
    c["token"] = np.concatenate([token // 64 * 64, token % 64], axis=1)
    bits = (np.arange(3)[None, :] + 1) * 4.0 ** (BITS // 2 - 1 - np.arange(BITS // 2)[:, None])
    c["bitsf"] = np.tile(bits.reshape(-1), (P, 1))
    return {k: np.ascontiguousarray(v, dtype=np.float32) for k, v in c.items()}


def layout(sizes):
    at, off = {}, 0
    for name, w in sizes:
        at[name] = (off, w)
        off += w
    return at, off


CONST_SIZES = [("ident", P), ("ones", P), ("headones", P), ("samelist", P), ("segbefore", P),
               ("causal", 4 * P), ("chunkrun", H * TB), ("sel", 32 * P), ("selk", P), ("iota", P),
               ("token", 2 * NL * TT), ("bitsf", 3 * (BITS // 2))]
WEIGHT_SIZES = [("wq", DC * H * DK), ("wk", DC * H * DK), ("wv", DC * H * DV), ("wg", DC * H * DV),
                ("wgk1", DC * LR), ("wgk2", H * DK), ("win2", DC * P), ("inproj", DC * 2 * DI),
                ("xproj", DT * (DR + 2 * DS)), ("dthead", DI), ("gate", DC * E),
                ("bgk2", H), ("bin", 1), ("w1", FJ), ("b1", FJ), ("w2", FJ), ("b2", 1),
                ("convw", DT * DCV), ("convb", DT), ("dtb", DT), ("dskip", DT), ("gnw", 1)]
FOLD_SIZES = [("wo", DC * D), ("wout2", D), ("bout", D), ("outproj", DT * D), ("c0", DC * B), ("c1", DC * B)]
CONST_AT, CONST_W = layout(CONST_SIZES)
WEIGHT_AT, WEIGHT_W = layout(WEIGHT_SIZES)
FOLD_AT, FOLD_W = layout(FOLD_SIZES)


def build(nc, x_in, consts, weights, folds, wmod0, wmod1, w1_d, w2_d, out):
    xn_d = nc.dram_tensor("xn_rows", (B * T, D), F32, kind="Internal").ap()
    x_rows = x_in.rearrange("b t d -> (b t) d")
    out_rows = out.rearrange("b t d -> (b t) d")
    with ExitStack() as top:
        def keep(name, shape, dt=F32):
            return top.enter_context(nc.sbuf_tensor(name, shape, dt))

        names = {}

        def sem(name):
            if name not in names:
                names[name] = top.enter_context(nc.semaphore(name))
            return names[name]

        scores = keep("scores", [P, B * TT * E])
        ones_s = keep("ones_s", [P, P])
        ident_s = keep("ident_s", [P, P])
        col1 = keep("col1", [P, 6 * DC * B])
        gb1 = keep("gb1", [P, B * D])
        layers(nc, sem, x_rows, consts, weights, folds, wmod0, wmod1, out_rows, xn_d,
               scores, ones_s, ident_s, col1, gb1)
        experts(nc, sem, consts, w1_d, w2_d, out_rows, xn_d, scores, ones_s, ident_s, col1, gb1)


def layers(nc, sem, x_rows, consts, weights, folds, wmod0, wmod1, out_rows, xn_d,
           scores, ones_s, ident_s, col1, gb1):
    with ExitStack() as ctx:
        def sb(name, shape, dt=F32):
            return ctx.enter_context(nc.sbuf_tensor(name, shape, dt))

        def ps(name, shape, dt=F32):
            return ctx.enter_context(nc.psum_tensor(name, shape, dt))

        W = sb("W", [P, WEIGHT_W])

        def w(name):
            a, n = WEIGHT_AT[name]
            return W[:, a:a + n]

        def cols(name, n):
            return w(name).rearrange("p (c n) -> p c n", n=n)

        headones = sb("headones", [P, P])
        causal = sb("causal", [P, 4 * P], mybir.dt.uint8)
        chunkrun = sb("chunkrun", [P, H * TB])
        sel = sb("sel", [96, 32, P], BF16)
        selk = sb("selk", [96, P], BF16)
        epst = sb("epst", [P, 1])
        expo = sb("expo", [P, NT])
        wo_g = sb("wo_g", [P, B, DC, D])
        wout_g = sb("wout_g", [P, B, D])
        bout_g = sb("bout_g", [1, B, D])
        oproj_g = sb("oproj_g", [P, B, DT, D])
        dskip = sb("dskip", [P, DT, P])
        col0 = sb("col0", [P, 6 * DC * B])
        b1s = sb("b1s", [P, FJ])
        nbgk = sb("nbgk", [P, H])

        wq, wk = cols("wq", H * DK), cols("wk", H * DK)
        wv, wg = cols("wv", H * DV), cols("wg", H * DV)
        wgk1, wgk2 = cols("wgk1", LR), w("wgk2")
        win2, inproj = cols("win2", P), cols("inproj", 2 * DI)
        xproj, dthead, gate = cols("xproj", DR + 2 * DS), w("dthead"), cols("gate", E)

        def modcol(col, what, c, b):
            return col[:, bass.ds((what * DC + c) * B + b, 1)]

        with ExitStack() as pre:
            def tsb(name, shape, dt=F32):
                return pre.enter_context(nc.sbuf_tensor(name, shape, dt))

            cst = tsb("cst", [P, CONST_W])
            fold = tsb("fold", [P, FOLD_W])
            wmod = tsb("wmod", [P, 2, DC, 6 * D])
            silc = tsb("silc", [P, 2, DC * B])
            silr = tsb("silr", [P, 2, B, DC, P])
            gabs = tsb("gabs", [P, 4, B * D])
            gsig = tsb("gsig", [P, 4, B * D])
            gmul = tsb("gmul", [P, 3, B * D])
            wo_n = tsb("wo_n", [P, DC, D])
            pcol = pre.enter_context(nc.psum_tensor("pcol", [P, 2, 512], F32))
            prow = pre.enter_context(nc.psum_tensor("prow", [P, 4, 512], F32))

            def cs(name):
                a, n = CONST_AT[name]
                return cst[:, a:a + n]

            def fo(name):
                a, n = FOLD_AT[name]
                return fold[:, a:a + n]

            with nc.Block() as block:
                @block.sync
                def _(sp):
                    sp.dma_start(fold[:, :], folds).then_inc(sem("fold_in"), 16)
                    sp.dma_start(wmod[:, 0], wmod0.rearrange("(c p) n -> p c n", p=P)).then_inc(sem("wmod0_in"), 16)
                    sp.dma_start(cst[:, :], consts).then_inc(sem("const_in"), 16)
                    sp.dma_start(W[:, :], weights).then_inc(sem("weights_in"), 16)
                    sp.wait_ge(sem("weights_in"), 16)

                @block.scalar
                def _(act):
                    act.dma_start(wmod[:, 1], wmod1.rearrange("(c p) n -> p c n", p=P)).then_inc(sem("wmod1_in"), 16)
                    act.wait_ge(sem("fold_in"), 16)
                    for n in range(2):
                        act.activation(silc[:, n, :], fo(f"c{n}"), ACT.Silu).then_inc(sem("silc"), 1)
                    for g in range(4):
                        act.wait_ge(sem("rows"), g + 1)
                        act.activation(gabs[:, g, :], prow[:, g, :], ACT.Abs).then_inc(sem("gabs"), 1)

                @block.gpsimd
                def _(pool):
                    for name, n in (PER_BLOCK | PER_TURN).items():
                        pool.sem_inc(sem(name), n)

                @block.tensor
                def _(pe):
                    pe.wait_ge(sem("silc"), 2)
                    pe.wait_ge(sem("wmod0_in"), 16)
                    for n in range(2):
                        if n == 1:
                            pe.wait_ge(sem("wmod1_in"), 16)
                        for m in range(6 * DC):
                            for c in range(DC):
                                last = pe.matmul(pcol[:, n, m * B:(m + 1) * B], wmod[:, n, c, m * P:(m + 1) * P],
                                                 silc[:, n, c * B:(c + 1) * B], start=(c == 0), stop=(c == DC - 1))
                        last.then_inc(sem("modcols"), 1)
                    pe.wait_ge(sem("silr"), 2 * B * DC)
                    for n in range(2):
                        for g in range(2):
                            what = 2 + 3 * g
                            for b in range(B):
                                for c in range(DC):
                                    last = pe.matmul(prow[:, 2 * n + g, b * D:(b + 1) * D], silr[:, n, b, c, :],
                                                     wmod[:, n, c, what * D:(what + 1) * D],
                                                     start=(c == 0), stop=(c == DC - 1))
                            last.then_inc(sem("rows"), 1)

                @block.vector
                def _(dve):
                    dve.memset(epst[:, :], EPS)
                    dve.memset(expo[:, :], -0.5)
                    dve.wait_ge(sem("const_in"), 16)
                    dve.wait_ge(sem("silc"), 2)
                    for n in range(2):
                        for b in range(B):
                            for c in range(DC):
                                dve.tensor_scalar(silr[:, n, b, c, :], cs("ones"), silc[:, n, c * B + b:c * B + b + 1],
                                                  None, ALU.mult).then_inc(sem("silr"), 1)
                    dve.tensor_copy(headones[:, :], cs("headones"))
                    dve.tensor_copy(ones_s[:, :], cs("ones"))
                    dve.tensor_copy(ident_s[:, :], cs("ident"))
                    dve.tensor_copy(causal[:, :], cs("causal"))
                    dve.tensor_copy(chunkrun[:, :], cs("chunkrun"))
                    dve.tensor_copy(sel[:, :, :].rearrange("p a b -> p (a b)"), cs("sel")[0:96])
                    dve.tensor_copy(selk[:, :], cs("selk")[0:96])
                    for n, col in enumerate((col0, col1)):
                        dve.wait_ge(sem("modcols"), n + 1)
                        dve.tensor_copy(col[:, :], pcol[:, n, 0:6 * DC * B]).then_inc(sem("prep_step"), 1)
                    dve.wait_ge(sem("prep_step"), 2)
                    for col in (col0, col1):
                        for what in (1, 4):
                            v = col[:, what * DC * B:(what + 1) * DC * B]
                            dve.tensor_scalar(v, v, 1.0, None, ALU.add)
                    for g in range(4):
                        dve.wait_ge(sem("gabs"), g + 1)
                        dve.tensor_scalar(gsig[:, g, :], prow[:, g, :], 0.0, 2.0, ALU.is_ge, ALU.mult)\
                            .then_inc(sem("prep_step"), 1)
                        dve.tensor_scalar(gabs[:, g, :], gabs[:, g, :], 0.25, None, ALU.max).then_inc(sem("prep_step"), 1)
                        dve.wait_ge(sem("prep_step"), 2 + 3 * g + 2)
                        to = gmul[:, g, :] if g < 3 else gb1[:, :]
                        dve.scalar_tensor_tensor(to, gsig[:, g, :], -1.0, gabs[:, g, :], ALU.add, ALU.mult)\
                            .then_inc(sem("prep_step"), 1)
                    dve.wait_ge(sem("prep_step"), 2 + 3 * 4)
                    dve.wait_ge(sem("weights_in"), 16)
                    dve.tensor_scalar(wo_n[:, :, :].rearrange("p c n -> p (c n)"), fo("wo"), w("gnw"), None, ALU.mult)\
                        .then_inc(sem("prep_step"), 1)
                    dve.wait_ge(sem("prep_step"), 2 + 3 * 4 + 1)
                    for b in range(B):
                        ga0, gb0, ga1 = (gmul[:, g, b * D:(b + 1) * D] for g in range(3))
                        for c in range(DC):
                            dve.tensor_tensor(wo_g[:, b, c, :], wo_n[:, c, :], ga0, ALU.mult)
                        dve.tensor_tensor(wout_g[:, b, :], fo("wout2"), gb0, ALU.mult)
                        dve.tensor_tensor(bout_g[0:1, b, :], fo("bout")[0:1], gb0[0:1], ALU.mult)
                        for k in range(DT):
                            dve.tensor_tensor(oproj_g[:, b, k, :], fo("outproj")[:, k * D:(k + 1) * D], ga1, ALU.mult)
                    for k in range(DT):
                        dve.tensor_scalar(dskip[:, k, :], cs("ident"), w("dskip")[:, k:k + 1], None, ALU.mult)
                    dve.scalar_tensor_tensor(b1s[:, :], w("w1"), w("bin"), w("b1"), ALU.mult, ALU.add)
                    dve.tensor_scalar(nbgk[:, :], w("bgk2"), -1.0, None, ALU.mult)

        xt = sb("xt", [P, XBUF * NT * D])
        stat = {n: sb(f"stat_{n}", [P, NT, 6]) for n in "abcd"}
        mv = {n: sb(f"mv_{n}", [P, NT, 2]) for n in "abcd"}
        ve = {n: sb(f"ve_{n}", [P, NT]) for n in "abcd"}
        rstd = {n: sb(f"rstd_{n}", [P, NT]) for n in "abcd"}
        xnA = sb("xnA", [P, NT, D])
        hA = sb("hA", [P, DC, TB])
        lr = sb("lr", [LR, TB])
        lz = sb("lz", [P, H * TB])
        rz = sb("rz", [P, H * TB])
        qg = sb("qg", [P, H, TB])
        kin = sb("kin", [P, H, TB])
        kg = sb("kg", [P, H, TB])
        glast = sb("glast", [P, H, NCH])
        v = sb("v", [P, NT, H * DV])
        vh = sb("vh", [P, NT, 2, H * DV])
        sg = sb("sg", [P, DC * TB])
        kgt = sb("kgt", [P, NT, H, DK])
        att = sb("att", [P, NT, H, P])
        S = sb("S", [P, 2 + NCH, H * DV])
        o_s, o_q = lz[:, 0:DC * TB], lz[:, DC * TB:2 * DC * TB]
        rms, og = rz[:, 0:DC * TB], rz[:, DC * TB:2 * DC * TB]
        s_f = sb("s_f", [P, TB])
        rel = sb("rel", [P, 4, TB])
        facc = sb("facc", [P, TB])
        xnB = sb("xnB", [P, NT, D])
        hB = sb("hB", [P, DC, TB])
        xraw = sb("xraw", [P, DT, TB + DCV - 1])
        tail = sb("tail", [P, 2 * DT * (DCV - 1)])
        xs = sb("xs", [P, DT, TB])
        sz = sb("sz", [P, 2 * DT * TB])
        dtl = sb("dtl", [DR, TB])
        kx = sb("kx", [32, 2, TB])
        kr = sb("kr", [32, 2, TB])
        km = sb("km", [32, 2, TB], BF16)
        k3 = sb("k3", [96, 2 * 2 * TB], BF16)
        ksum = sb("ksum", [P, TB])
        dtv = sb("dtv", [P, 2 * DT * TB])
        tmp = sb("tmp", [P, DT, TB])
        u = sb("u", [P, 2 * DT * TB])
        dec = sb("dec", [P, 2, DT, 1 + TB])
        st = sb("st", [P, 4, DT, 1 + TB])
        qb = sb("qb", [P, 2, 2 * TB])
        last = sb("last", [P, 2 * DS * DT])
        xo = sb("xo", [P, NT, D])
        xnC = sb("xnC", [P, NT, D])

        pA = [ps(f"pA{i}", [P, 512]) for i in range(2)]
        pB = ps("pB", [P, 512])
        pK = [ps(f"pK{i}", [P, 512]) for i in range(2)]
        pQ = ps("pQ", [P, 512])
        pY = ps("pY", [P, DT, TB])

        def after(eng, name, value):
            if not (isinstance(value, int) and value <= 0):
                eng.wait_ge(sem(name), value)

        def batch(it):
            return (it - 1) // BPB

        def later(it):
            return ((it - 1) % BPB + BPB - 1) // BPB

        def x_at(it, t, n=1):
            return xt[:, bass.ds((it % XBUF) * (NT * D) + t * D, n * D)]

        def turn2(buf, it, n):
            return buf[:, bass.ds((it % 2) * n, n)]

        def flat(x):
            return x.rearrange("p a b -> p (a b)")

        def wide(x):
            return x.rearrange("p (k t) -> p k t", k=DT)

        def settled(eng):
            eng.wait_ge(sem("weights_in"), 16)

        def ln_stats(dve, it, n, src):
            for t in range(NT):
                i = dve.bn_stats(stat[n][:, t, :], src(t))
            i.then_inc(sem(f"ln{n}_stats"), 1)
            settled(dve)
            dve.wait_ge(sem(f"ln{n}_stats"), it + 1)
            for t in range(NT):
                i = dve.bn_aggr(mv[n][:, t, :], stat[n][:, t, :])
            i.then_inc(sem(f"ln{n}_var"), 1)
            dve.wait_ge(sem(f"ln{n}_var"), it * 2 + 1)
            dve.tensor_scalar(ve[n][:, :], mv[n][:, :, 1], EPS, None, ALU.add).then_inc(sem(f"ln{n}_var"), 1)

        def ln_rows(dve, it, n, src, dst):
            dve.wait_ge(sem(f"ln{n}_rstd"), it + 1)
            for t in range(NT):
                i = dve.tensor_scalar(dst[:, t, :], src(t), mv[n][:, t, 0:1], rstd[n][:, t:t + 1],
                                      ALU.subtract, ALU.mult)
            i.then_inc(sem(f"ln{n}_rows"), 1)

        def ln_pool(pool, it, n):
            pool.wait_ge(sem(f"ln{n}_var"), it * 2 + 2)
            pool.tensor_tensor(rstd[n][:, :], ve[n][:, :], expo[:, :], ALU.pow).then_inc(sem(f"ln{n}_rstd"), 1)

        def turn(pe, it, n, rows, bank):
            pe.wait_ge(sem(f"ln{n}_rows"), it + 1)
            for c in range(DC):
                for t in range(NT):
                    i = pe.transpose(bank[:, c * TB + t * P:c * TB + (t + 1) * P], rows[:, t, c * P:(c + 1) * P],
                                     ident_s[:, :])
            i.then_inc(sem(f"turn_{n}"), 1)

        def modulate(act, it, n, bank, col, scale, shift, dst):
            act.wait_ge(sem(f"turn_{n}"), it + 1)
            for c in range(DC):
                act.activation(dst[:, c, :], bank[:, c * TB:(c + 1) * TB], ACT.Identity,
                               bias=modcol(col, shift, c, batch(it)), scale=modcol(col, scale, c, batch(it)))\
                    .then_inc(sem(f"hT_{n}"), 1)

        def attn_pe(pe, it, n):
            def scores_of(hp):
                pe.wait_ge(sem("kg"), it * 2 + hp + 1)
                for t in range(NT):
                    for h2 in range(2):
                        i = pe.transpose(pA[hp][:, (t * 2 + h2) * P:(t * 2 + h2 + 1) * P],
                                         kg[:, 2 * hp + h2, t * P:(t + 1) * P], ident_s[:, :])
                i.then_inc(sem("kgt_mm"), 1)
                for t in range(NT):
                    for h2 in range(2):
                        h = 2 * hp + h2
                        i = pe.matmul(pA[1 - hp][:, (t * 2 + h2) * P:(t * 2 + h2 + 1) * P],
                                      kin[:, h, t * P:(t + 1) * P], qg[:, h, t * P:(t + 1) * P],
                                      start=True, stop=True)
                i.then_inc(sem(f"att_mm{hp}"), 1)

            def added_of(hp):
                pe.wait_ge(sem("kgt"), it * 2 + hp + 1)
                for t in range(NT):
                    for h2 in range(2):
                        h = 2 * hp + h2
                        i = pe.matmul(pA[hp][:, :].rearrange("p (c h n) -> p c h n", h=2, n=DV)[:, 2 * t:2 * t + 2, h2, :],
                                      kgt[:, t, h, :], vh[:, t, :, h * DV:(h + 1) * DV], start=True, stop=True)
                i.then_inc(sem("kv_mm"), 1)

            if n == 2:
                after(pe, "x_attn", it)
                turn(pe, it, "a", xnA, pA[0])
            if n == 2:
                after(pe, "ms_ln", it)
                pe.wait_ge(sem("hT_a"), (it + 1) * DC)
                for c in range(DC):
                    i = pe.matmul(pA[1][0:LR, 0:TB], wgk1[:, c, :], hA[:, c, :], start=(c == 0), stop=(c == DC - 1))
                i.then_inc(sem("low_rank"), 1)
            if n == 5:
                pe.wait_ge(sem("lr"), it + 1)
                for h in range(H):
                    i = pe.matmul(pA[h // 2][:, (h % 2) * TB:(h % 2 + 1) * TB], wgk2[0:LR, h * DK:(h + 1) * DK],
                                  lr[:, :], start=True, stop=True)
                    if h % 2:
                        i.then_inc(sem("z"), 1)
            if n == 7:
                pe.wait_ge(sem("z_read"), it * 8 + 4)
                for t in range(NT):
                    for c in range(DC):
                        i = pe.matmul(pA[0][:, t * D:(t + 1) * D], hA[:, c, t * P:(t + 1) * P], wv[:, c, :],
                                      start=(c == 0), stop=(c == DC - 1))
                i.then_inc(sem("v_mm"), 1)
            if n == 8:
                pe.wait_ge(sem("z_read"), it * 8 + 8)
                for m in range(DC):
                    for c in range(DC):
                        i = pe.matmul(pA[1][:, m * TB:(m + 1) * TB], wg[:, c, m * P:(m + 1) * P], hA[:, c, :],
                                      start=(c == 0), stop=(c == DC - 1))
                i.then_inc(sem("g_mm"), 1)
            if n == 9:
                pe.wait_ge(sem("v_s"), it + 1)
                project(pe, wq, pA[0], 0, "q_mm")
            if n == 10:
                pe.wait_ge(sem("sg"), it + 1)
                project(pe, wk, pA[1], 0, "k_mm")
            if n == 17:
                scores_of(0)
            if n == 19:
                added_of(0)
            if n == 19:
                pe.wait_ge(sem("att"), it * 2 + 1)
                project(pe, wq, pA[1], 1, "q_mm")
            if n == 21:
                pe.wait_ge(sem("state"), it * 16 + 8)
                project(pe, wk, pA[0], 1, "k_mm")
            if n == 22:
                scores_of(1)
            if n == 24:
                added_of(1)
            if n == 26:
                pe.wait_ge(sem("att"), it * 2 + 2)
                pe.wait_ge(sem("state"), it * 16 + 16)
                for h in range(H):
                    hp, h2 = h // 2, h % 2
                    for t in range(NT):
                        o = pA[0][h2 * DV:(h2 + 1) * DV, hp * TB + t * P:hp * TB + (t + 1) * P]
                        pe.matmul(o, v[:, t, h * DV:(h + 1) * DV], att[:, t, h, :], start=True, stop=False,
                                  skip_group_check=True)
                        for c in (2 * t, 2 * t + 1):
                            i = pe.matmul(o[:, (c % 2) * CH:(c % 2 + 1) * CH], S[:, 1 + c, h * DV:(h + 1) * DV],
                                          qg[:, h, c * CH:(c + 1) * CH], start=False, stop=(c % 2 == 1),
                                          skip_group_check=True)
                i.then_inc(sem("o_mm"), 1)
            if n == 28:
                pe.wait_ge(sem("o_sq"), it + 1)
                pe.matmul(pA[1][:, :], headones[:, :], o_q, start=True, stop=True).then_inc(sem("ms_mm"), 1)
            if n == 30:
                pe.wait_ge(sem("og"), it + 1)
                wof = wo_g[:, :, :, :].rearrange("p b c n -> p (b c n)")
                for t in range(NT):
                    for c in range(DC):
                        i = pe.matmul(pA[0][:, t * D:(t + 1) * D], og[:, c * TB + t * P:c * TB + (t + 1) * P],
                                      wof[:, bass.ds((batch(it) * DC + c) * D, D)],
                                      start=(c == 0), stop=(c == DC - 1))
                i.then_inc(sem("wo_mm"), 1)

        def project(pe, wt, bank, hp, done):
            for h2 in range(2):
                h = 2 * hp + h2
                for c in range(DC):
                    i = pe.matmul(bank[:, h2 * TB:(h2 + 1) * TB], wt[:, c, h * DK:(h + 1) * DK], hA[:, c, :],
                                  start=(c == 0), stop=(c == DC - 1))
            i.then_inc(sem(done), 1)

        def attn_act(act, it, n):
            def turned(hp):
                act.wait_ge(sem("kgt_mm"), it * 2 + hp + 1)
                act.activation(kgt[:, :, 2 * hp:2 * hp + 2, :],
                               pA[hp][:, :].rearrange("p (t h n) -> p t h n", t=NT, h=2), ACT.Copy)\
                    .then_inc(sem("kgt"), 1)

            if n == 3:
                after(act, "k_mm", it * 2)
                modulate(act, it, "a", pA[0], col0, 1, 0, hA)
            if n == 5:
                act.wait_ge(sem("low_rank"), it + 1)
                act.activation(lr[:, :], pA[1][0:LR, 0:TB], ACT.Copy).then_inc(sem("lr"), 1)
            if n == 7:
                after(act, "wo_mm", it)
                for h in range(H):
                    if h % 2 == 0:
                        act.wait_ge(sem("z"), it * 2 + h // 2 + 1)
                    z = pA[h // 2][:, (h % 2) * TB:(h % 2 + 1) * TB]
                    act.activation(lz[:, h * TB:(h + 1) * TB], z, ACT.Abs, bias=w("bgk2")[:, h:h + 1])\
                        .then_inc(sem("z_read"), 1)
                    act.activation(rz[:, h * TB:(h + 1) * TB], z, ACT.Relu, bias=nbgk[:, h:h + 1], scale=-1.0)\
                        .then_inc(sem("z_read"), 1)
            if n == 7:
                act.wait_ge(sem("v_mm"), it + 1)
                act.activation(v[:, :, :].rearrange("p t n -> p (t n)"), pA[0][:, :], ACT.Copy)
                for half in range(2):
                    r = slice(half * CH, (half + 1) * CH)
                    i = act.activation(vh[r, :, half, :], pA[0][r, :].rearrange("p (t n) -> p t n", t=NT), ACT.Copy)
                i.then_inc(sem("v_s"), 1)
            if n == 8:
                act.wait_ge(sem("z_read"), it * 8 + 8)
                act.activation(lz[:, :], lz[:, :], ACT.Exp, scale=-1.0).then_inc(sem("z_exp"), 1)
                act.wait_ge(sem("z_exp"), it + 1)
                act.activation(lz[:, :], lz[:, :], ACT.Ln, bias=ones_s[:, 0:1]).then_inc(sem("z_ln"), 1)
            if n == 9:
                act.wait_ge(sem("g_mm"), it + 1)
                act.activation(sg[:, :], pA[1][:, :], ACT.Silu).then_inc(sem("sg"), 1)
            if n == 12:
                act.wait_ge(sem("cumsum"), it + 1)
                act.activation(flat(qg[:, :, :]), lz[:, :], ACT.Exp, scale=-1.0 / GN).then_inc(sem("eG"), 1)
                act.activation(flat(kin[:, :, :]), lz[:, :], ACT.Exp, scale=1.0 / GN).then_inc(sem("emG"), 1)
                act.wait_ge(sem("eG"), it + 1)
                act.activation(glast[:, :, :], qg[:, :, :].rearrange("p h (c t) -> p h c t", t=CH)[:, :, :, CH - 1],
                               ACT.Copy).then_inc(sem("glast"), 1)
            if n == 14:
                act.wait_ge(sem("to_end"), it + 1)
                act.activation(flat(kg[:, :, :]), rz[:, :], ACT.Exp, scale=1.0 / GN).then_inc(sem("eD"), 1)
            if n == 17:
                turned(0)
            if n == 22:
                turned(1)
            if n == 25:
                act.wait_ge(sem("o_mm"), it + 1)
                act.activation(o_s, pA[0][:, :], ACT.Copy).then_inc(sem("o_s"), 1)
                act.activation(o_q, pA[0][:, :], ACT.Square).then_inc(sem("o_sq"), 1)
            if n == 28:
                act.wait_ge(sem("ms_mm"), it + 1)
                act.activation(rms, pA[1][:, :], ACT.Ln, bias=epst[:, :], scale=1.0 / DV).then_inc(sem("ms_ln"), 1)
                act.wait_ge(sem("ms_ln"), it + 1)
                act.activation(rms, rms, ACT.Exp, scale=-0.5).then_inc(sem("rms"), 1)

        def attn_dve(dve, it, n):
            def pair(x, hp):
                return x[:, 2 * hp:2 * hp + 2, :].rearrange("p h t -> p (h t)")

            def queries(hp, bank):
                dve.wait_ge(sem("q_mm"), it * 2 + hp + 1)
                dve.scalar_tensor_tensor(pair(qg, hp), bank[:, :], DK ** -0.5, pair(qg, hp), ALU.mult, ALU.mult)\
                    .then_inc(sem("qg"), 1)

            def keys(hp, bank):
                dve.wait_ge(sem("k_mm"), it * 2 + hp + 1)
                dve.tensor_tensor(pair(kin, hp), bank[:, :], pair(kin, hp), ALU.mult)
                dve.tensor_tensor(pair(kg, hp), bank[:, :], pair(kg, hp), ALU.mult).then_inc(sem("kg"), 1)

            def states(hp):
                dve.wait_ge(sem("kv_mm"), it * 2 + hp + 1)
                for c in range(NCH):
                    for h2 in range(2):
                        h = 2 * hp + h2
                        if c > 0:
                            dve.wait_ge(sem("state"), it * 16 + hp * 8 + 2 * c + h2 - 1)
                        dve.scalar_tensor_tensor(
                            S[:, 2 + c, h * DV:(h + 1) * DV], S[:, 1 + c, h * DV:(h + 1) * DV], glast[:, h, c:c + 1],
                            pA[hp][:, (c * 2 + h2) * DV:(c * 2 + h2 + 1) * DV],
                            ALU.mult, ALU.add).then_inc(sem("state"), 1)

            def scored(hp):
                settled(dve)
                dve.wait_ge(sem(f"att_mm{hp}"), it + 1)
                dve.copy_predicated(att[:, :, 2 * hp:2 * hp + 2, :],
                                    causal[:, :].rearrange("p (t h n) -> p t h n", t=NT, h=2),
                                    pA[1 - hp][:, :].rearrange("p (t h n) -> p t h n", t=NT, h=2))\
                    .then_inc(sem("att"), 1)

            if n == 1:
                settled(dve)
                dve.wait_ge(sem("x_in"), (it + 1) * 16)
                ln_stats(dve, it, "a", lambda t: x_at(it, t))
            if n == 2:
                after(dve, "turn_a", it)
                ln_rows(dve, it, "a", lambda t: x_at(it, t), xnA)
            if n == 10:
                dve.wait_ge(sem("lz_sum"), it + 1)
                dve.tensor_tensor_scan(lz[:, :], chunkrun[:, :], lz[:, :], 0.0, ALU.mult, ALU.add)\
                    .then_inc(sem("cumsum"), 1)
                dve.wait_ge(sem("state"), it * 16)
                dve.wait_ge(sem("o_mm"), it)
                dve.tensor_copy(S[:, 1, :], flat(S[:, :, :])[:, bass.ds(later(it) * ((1 + NCH) * H * DV), H * DV)])\
                    .then_inc(sem("state0"), 1)
            if n == 16:
                dve.wait_ge(sem("glast"), it + 1)
                queries(0, pA[0])
            if n == 17:
                dve.wait_ge(sem("eD"), it + 1)
                keys(0, pA[1])
            if n == 18:
                scored(0)
            if n == 19:
                states(0)
            if n == 23:
                queries(1, pA[1])
            if n == 23:
                keys(1, pA[0])
            if n == 25:
                scored(1)
            if n == 25:
                states(1)
            if n == 28:
                dve.wait_ge(sem("sg"), it + 1)
                dve.wait_ge(sem("o_s"), it + 1)
                dve.tensor_tensor(o_s, o_s, sg[:, :], ALU.mult).then_inc(sem("o_n"), 1)

        def attn_pool(pool, it, n):
            if n == 0:
                ln_pool(pool, it, "a")
            if n == 9:
                pool.wait_ge(sem("z_ln"), it + 1)
                pool.tensor_tensor(lz[:, :], lz[:, :], rz[:, :], ALU.add).then_inc(sem("lz_sum"), 1)
            if n == 11:
                pool.wait_ge(sem("cumsum"), it + 1)
                lv = lz[:, :].rearrange("p (n t) -> p n t", t=CH)
                pool.tensor_tensor(rz[:, :].rearrange("p (n t) -> p n t", t=CH), lv,
                                   lv[:, :, CH - 1:CH].broadcast_to([P, H * NCH, CH]), ALU.subtract)\
                    .then_inc(sem("to_end"), 1)
            if n == 30:
                pool.wait_ge(sem("o_n"), it + 1)
                pool.wait_ge(sem("rms"), it + 1)
                pool.tensor_tensor(og, o_s, rms, ALU.mult).then_inc(sem("og"), 1)

        def front_pe(pe, it, n, back):
            if n == 0:
                after(pe, "ksum", it)
                turn(pe, it, "b", xnB, pB)
            if n == 4:
                pe.wait_ge(sem("hT_b"), (it + 1) * DC)
                for c in range(DC):
                    i = pe.matmul(pB[:, 0:TB], win2[:, c, :], hB[:, c, :], start=(c == 0), stop=(c == DC - 1))
                i.then_inc(sem("win_mm"), 1)
            if n == 8:
                pe.wait_ge(sem("facc"), (it + 1) * FJ)
                pe.wait_ge(sem("ffn_s"), it + 1)
                if back is not None:
                    pe.wait_ge(sem("x_scan"), back + 1)
                bof, wof = flat(bout_g[:, :, :]), flat(wout_g[:, :, :])
                for t in range(NT):
                    pe.matmul(pB[:, t * D:(t + 1) * D], ones_s[0:1, :], bof[:, bass.ds(batch(it) * D, D)],
                              start=True, stop=False)
                    i = pe.matmul(pB[:, t * D:(t + 1) * D], facc[:, t * P:(t + 1) * P],
                                  wof[:, bass.ds(batch(it) * D, D)], start=False, stop=True)
                i.then_inc(sem("wout_mm"), 1)
            if n == 10:
                turn(pe, it, "c", xnB, pB)
            for m, step in enumerate((12, 12, 14, 14)):
                if n == step:
                    pe.wait_ge(*((sem("hT_c"), (it + 1) * DC), (sem("x_cp"), it * 2 + 1), (sem("x_cp"), it * 2 + 2),
                                 (sem("sz"), it * 2 + 1))[m])
                    for k in range(2):
                        for c in range(DC):
                            col = (2 * m + k) * P
                            i = pe.matmul(pB[:, k * TB:(k + 1) * TB], inproj[:, c, col:col + P], hB[:, c, :],
                                          start=(c == 0), stop=(c == DC - 1))
                    i.then_inc(sem("in_mm"), 1)
            if n == 20:
                pe.wait_ge(sem("sz"), it * 2 + 2)
                if back is not None:
                    pe.wait_ge(sem("scores"), back + 1)
                pe.wait_ge(sem("xs"), it + 1)
                for lo, m, at in ((0, DR, 0), (DR, 2 * DS, TB)):
                    for k in range(DT):
                        i = pe.matmul(pB[0:m, at:at + TB], xproj[:, k, lo:lo + m], xs[:, k, :],
                                      start=(k == 0), stop=(k == DT - 1))
                i.then_inc(sem("dkq_mm"), 1)
            if n in (21, 22):
                m = 0 if n == 21 else 1
                pe.wait_ge(sem("dkq"), it * 2 + 2)
                if m == 1:
                    pe.wait_ge(sem("dt_sig"), it * DT + 2)
                for k in range(2):
                    i = pe.matmul(pB[:, k * TB:(k + 1) * TB], dthead[0:DR, (2 * m + k) * P:(2 * m + k + 1) * P],
                                  dtl[:, :], start=True, stop=True)
                i.then_inc(sem("dt_mm"), 1)
            if n == 22:
                pe.wait_ge(sem("dt_sig"), it * DT + DT)
                pe.wait_ge(sem("parts"), (it + 1) * 4)
                pe.matmul(pB[:, 0:TB], selk[:, :], k3[:, bass.ds((it % 2) * 2 * TB + TB, TB)],
                          start=True, stop=True).then_inc(sem("ksum_mm"), 1)
            if n == 28:
                spread(pe, it, 0)
            if n == 30:
                spread(pe, it, 1)

        def front_act(act, it, n):
            nt = DT * (DCV - 1)
            if n == 2:
                after(act, "score_mm", it - 2)
                modulate(act, it, "b", pB, col0, 4, 3, hB)
            if n == 4:
                act.wait_ge(sem("win_mm"), it + 1)
                act.activation(s_f[:, :], pB[:, 0:TB], ACT.Copy).then_inc(sem("ffn_s"), 1)
                act.wait_ge(sem("ffn_s"), it + 1)
            if n in (4, 6):
                for j in (range(4) if n == 4 else range(4, FJ)):
                    act.wait_ge(sem("facc"), it * FJ + j - 3)
                    act.activation(rel[:, j % 4, :], s_f[:, :], ACT.Relu, bias=b1s[:, j:j + 1],
                                   scale=w("w1")[:, j:j + 1]).then_inc(sem("relu"), 1)
            if n == 10:
                act.wait_ge(sem("win_mm"), it + 1)
                modulate(act, it, "c", pB, col1, 1, 0, hB)
            if n == 10:
                act.wait_ge(sem("conv"), it * 16)
                act.wait_ge(sem("tail"), it)
                act.activation(xraw[:, :, 0:DCV - 1],
                               tail[:, bass.ds(later(it) * nt, nt)].rearrange("p (k n) -> p k n", n=DCV - 1),
                               ACT.Copy).then_inc(sem("halo"), 1)
            for m, step in enumerate((12, 13)):
                if n == step:
                    act.wait_ge(sem("in_mm"), it * 4 + m + 1)
                    act.activation(xraw[:, 2 * m:2 * m + 2, DCV - 1:], pB[:, :].rearrange("p (k t) -> p k t", k=2),
                                   ACT.Copy).then_inc(sem("x_cp"), 1)
            for m, step in enumerate((15, 15)):
                if n == step:
                    after(act, "yz", it - 1)
                    act.wait_ge(sem("in_mm"), it * 4 + m + 3)
                    act.activation(sz[:, bass.ds((it % 2) * (DT * TB) + m * 2 * TB, 2 * TB)], pB[:, :], ACT.Silu)\
                        .then_inc(sem("sz"), 1)
            if n == 15:
                act.wait_ge(sem("x_cp"), it * 2 + 2)
                act.wait_ge(sem("halo"), it + 1)
                act.activation(tail[:, nt:2 * nt].rearrange("p (k n) -> p k n", n=DCV - 1), xraw[:, :, TB:],
                               ACT.Copy).then_inc(sem("tail"), 1)
            if n == 18:
                act.wait_ge(sem("conv"), it * 16 + 16)
                act.activation(xs[:, :, :], xs[:, :, :], ACT.Silu).then_inc(sem("xs"), 1)
            if n == 20:
                act.wait_ge(sem("dkq_mm"), it + 1)
                act.activation(dtl[:, :], pB[0:DR, 0:TB], ACT.Copy).then_inc(sem("dkq"), 1)
                kq = pB[0:32, TB:2 * TB]
                act.activation(kx[:, 0, :], kq, ACT.Copy)
                act.activation(kx[:, 1, :], kq, ACT.Square)
                after(act, "k_rows", (it - 1) * DS)
                after(act, "q_mm2", (it - 1) * (DS // 2))
                first = k3[0:32, bass.ds((it % 2) * 2 * TB, 2 * TB)]
                act.activation(first[:, 0:TB], kq, ACT.Copy)
                act.activation(first[:, TB:2 * TB], kq, ACT.Square).then_inc(sem("dkq"), 1)
            if n in (20, 21):
                m = 0 if n == 20 else 1
                if m == 0:
                    after(act, "inp", (it - 1) * DS)
                act.wait_ge(sem("dt_mm"), it * 2 + m + 1)
                for k in (2 * m, 2 * m + 1):
                    act.activation(dtv[:, bass.ds(((it % 2) * DT + k) * TB, TB)],
                                   pB[:, (k % 2) * TB:(k % 2 + 1) * TB], ACT.Sigmoid,
                                   bias=w("dtb")[:, k:k + 1]).then_inc(sem("dt_sig"), 1)
            if n == 23:
                act.wait_ge(sem("ksum_mm"), it + 1)
                act.activation(ksum[:, :], pB[:, 0:TB], ACT.Copy).then_inc(sem("ksum"), 1)
            if n == 25:
                act.wait_ge(sem("s_ksum"), it + 1)
                act.activation(tmp[:, :, :], tmp[:, :, :], ACT.Ln, bias=ones_s[:, 0:1]).then_inc(sem("den_ln"), 1)
                act.wait_ge(sem("den_ln"), it + 1)
                act.activation(tmp[:, :, :], tmp[:, :, :], ACT.Exp, scale=-1.0).then_inc(sem("den"), 1)
            if n == 31:
                q_rows(act, it, 0)
            if n == 31:
                decay(act, it, 0)

        def front_dve(dve, it, n, back):
            x_of = lambda t: x_at(it, t)
            if n == 0:
                dve.wait_ge(sem("wo_mm"), it + 1)
                dve.tensor_tensor(x_at(it, 0, NT), x_at(it, 0, NT), pA[0][:, :], ALU.add).then_inc(sem("x_attn"), 1)
                settled(dve)
                dve.wait_ge(sem("x_attn"), it + 1)
                ln_stats(dve, it, "b", x_of)
            if n == 1:
                after(dve, "turn_c", it)
                ln_rows(dve, it, "b", x_of, xnB)
            if n in (6, 7):
                for j in (range(4) if n == 6 else range(4, FJ)):
                    dve.wait_ge(sem("relu"), it * FJ + j + 1)
                    w2c = w("w2")[:, j:j + 1]
                    if j == 0:
                        dve.wait_ge(sem("wout_mm"), it)
                        dve.tensor_scalar(facc[:, :], rel[:, 0, :], w2c, w("b2"), ALU.mult, ALU.add)\
                            .then_inc(sem("facc"), 1)
                    else:
                        dve.wait_ge(sem("facc"), it * FJ + j)
                        dve.scalar_tensor_tensor(facc[:, :], rel[:, j % 4, :], w2c, facc[:, :], ALU.mult, ALU.add)\
                            .then_inc(sem("facc"), 1)
            if n == 9:
                dve.wait_ge(sem("wout_mm"), it + 1)
                dve.tensor_tensor(x_at(it, 0, NT), x_at(it, 0, NT), pB[:, :], ALU.add).then_inc(sem("x_ffn"), 1)
                settled(dve)
                dve.wait_ge(sem("x_ffn"), it + 1)
                ln_stats(dve, it, "c", x_of)
            if n == 10:
                dve.wait_ge(sem("turn_b"), it + 1)
                ln_rows(dve, it, "c", x_of, xnB)
            if n in (15, 17):
                half = 0 if n == 15 else 1
                ks = (2 * half, 2 * half + 1)
                if half == 0:
                    dve.wait_ge(sem("halo"), it + 1)
                    dve.wait_ge(sem("opened"), it)
                    dve.wait_ge(sem("u"), it)
                for j in range(DCV):
                    for k in ks:
                        done = it * 16 + half * 8 + 2 * j + k % 2
                        if j == 0:
                            dve.wait_ge(sem("x_cp"), it * 2 + k // 2 + 1)
                            dve.tensor_scalar(xs[:, k, :], xraw[:, k, 0:TB], w("convw")[:, k * DCV:k * DCV + 1],
                                              w("convb")[:, k:k + 1], ALU.mult, ALU.add).then_inc(sem("conv"), 1)
                        else:
                            dve.wait_ge(sem("conv"), done - 1)
                            dve.scalar_tensor_tensor(xs[:, k, :], xraw[:, k, j:j + TB],
                                                     w("convw")[:, k * DCV + j:k * DCV + j + 1], xs[:, k, :],
                                                     ALU.mult, ALU.add).then_inc(sem("conv"), 1)
            if n == 22:
                dve.wait_ge(sem("dkq"), it * 2 + 2)
                half = lambda r: k3[r, bass.ds((it % 2) * 2 * TB, 2 * TB)]
                dve.tensor_tensor(flat(kr[:, :, :]), flat(kx[:, :, :]), half(slice(0, 32)), ALU.subtract)\
                    .then_inc(sem("parts"), 1)
                dve.wait_ge(sem("parts"), it * 4 + 1)
                dve.tensor_copy(km[:, :, :], kr[:, :, :]).then_inc(sem("parts"), 1)
                dve.wait_ge(sem("parts"), it * 4 + 2)
                dve.tensor_copy(half(slice(32, 64)), flat(km[:, :, :])).then_inc(sem("parts"), 1)
                dve.tensor_tensor(half(slice(64, 96)), flat(kr[:, :, :]), flat(km[:, :, :]), ALU.subtract)\
                    .then_inc(sem("parts"), 1)
            if n == 28:
                dve.wait_ge(sem("den"), it + 1)
                d = turn2(dtv, it, DT * TB)
                dve.tensor_tensor(d, d, flat(tmp[:, :, :]), ALU.mult).then_inc(sem("dtv"), 1)
            if n == 29:
                dve.wait_ge(sem("dtv"), it + 1)
                dve.tensor_tensor(turn2(u, it, DT * TB), flat(xs[:, :, :]), turn2(dtv, it, DT * TB), ALU.mult)\
                    .then_inc(sem("u"), 1)
            if n == 31:
                scan_inputs(dve, it, 0)

        def front_pool(pool, it, n, back):
            if n == 0:
                ln_pool(pool, it, "b")
            if n == 9:
                ln_pool(pool, it, "c")
            if n == 24:
                settled(pool)
                pool.wait_ge(sem("ksum"), it + 1)
                if back is not None:
                    pool.wait_ge(sem("out_mm"), back + 1)
                pool.tensor_tensor(tmp[:, :, :], wide(turn2(dtv, it, DT * TB)),
                                  ksum[:, :].unsqueeze(1).broadcast_to([P, DT, TB]), ALU.mult)\
                    .then_inc(sem("s_ksum"), 1)

        def spread(pe, it, n):
            if n == 0:
                pe.wait_ge(sem("parts"), (it + 1) * 4)
            pe.wait_ge(sem("inp"), it * DS + n - 1)
            base = (it % 2) * 2 * TB
            pe.matmul(pK[n % 2][:, 0:TB], sel[:, n, :], k3[:, bass.ds(base + TB, TB)], start=True, stop=True)
            pe.matmul(pK[n % 2][:, TB:2 * TB], sel[:, n, :], k3[:, bass.ds(base, TB)], start=True, stop=True)\
                .then_inc(sem("k_rows"), 1)
            if n % 2 == 0:
                pe.wait_ge(sem("q_rows"), it * (DS // 2) + n // 2)
                pe.matmul(pQ[:, 0:TB], sel[:, DS + n, :], k3[:, bass.ds(base, TB)], start=True, stop=True)
                pe.matmul(pQ[:, TB:2 * TB], sel[:, DS + n + 1, :], k3[:, bass.ds(base, TB)], start=True, stop=True)\
                    .then_inc(sem("q_mm2"), 1)

        def scan_sum(pe, it, m):
            pe.wait_ge(sem("paired"), it * (DS // 2) + m + 1)
            for j in range(DT // 2):
                i = pe.matmul(pY[:, 2 * j:2 * j + 2, :], ident_s[:, :], st[:, (2 * m + 1) % 4, 2 * j:2 * j + 2, 1:],
                              start=False, stop=(m == DS // 2 - 1), skip_group_check=True)
            i.then_inc(sem("summed"), 1)

        def scan_pe(pe, it, n):
            m = n // 2
            if n % 2 == 0:
                if m + 2 < DS:
                    spread(pe, it, m + 2)
            elif m % 2 == 0 and m > 0:
                scan_sum(pe, it, m // 2 - 1)
            if n == 1:
                pe.wait_ge(sem("xs"), it + 1)
                pe.wait_ge(sem("yz"), it)
                for k in range(DT):
                    i = pe.matmul(pY[:, k, :], dskip[:, k, :], xs[:, k, :], start=(k % 2 == 0), stop=False,
                                  skip_group_check=True)
                i.then_inc(sem("opened"), 1)
            if n == 2 * DS - 1:
                scan_sum(pe, it, DS // 2 - 1)

        def q_rows(act, it, m):
            act.wait_ge(sem("q_mm2"), it * (DS // 2) + m + 1)
            act.wait_ge(sem("read_out"), it * DS + 2 * (m - 1))
            act.activation(qb[:, m % 2, :], pQ[:, :], ACT.Copy).then_inc(sem("q_rows"), 1)

        def decay(act, it, n):
            act.wait_ge(sem("rate"), it * DS + n + 1)
            act.activation(dec[:, n % 2, :, 1:], dec[:, n % 2, :, 1:], ACT.Identity, bias=ones_s[:, 0:1],
                           scale=-1.0).then_inc(sem("decay"), 1)
            act.wait_ge(sem("inp"), it * DS + n + 1)
            act.wait_ge(sem("saved"), (it - 1) * DS + n + 1)
            act.activation(st[:, n % 4, :, 0], last[:, bass.ds(later(it) * (DS * DT) + n * DT, DT)], ACT.Copy)\
                .then_inc(sem("carried"), 1)

        def scan_act(act, it, n):
            m = n // 2
            if n % 2 == 0:
                if m + 1 < DS:
                    decay(act, it, m + 1)
            elif m % 2 == 1 and m + 1 < DS:
                q_rows(act, it, (m + 1) // 2)

        def scan_inputs(dve, it, n):
            rows = pK[n % 2]
            if n == 0:
                dve.wait_ge(sem("dtv"), it + 1)
                dve.wait_ge(sem("u"), it + 1)
            dve.wait_ge(sem("k_rows"), it * DS + n + 1)
            dve.wait_ge(sem("scanned"), it * DS + n - 1)
            dve.tensor_tensor(dec[:, n % 2, :, 1:], wide(turn2(dtv, it, DT * TB)),
                              rows[:, 0:TB].unsqueeze(1).broadcast_to([P, DT, TB]), ALU.mult)\
                .then_inc(sem("rate"), 1)
            if n % 2 == 0:
                dve.wait_ge(sem("paired"), it * (DS // 2) + n // 2 - 1)
            else:
                dve.wait_ge(sem("summed"), it * (DS // 2) + (n - 3) // 2)
            dve.tensor_tensor(st[:, n % 4, :, 1:], wide(turn2(u, it, DT * TB)),
                              rows[:, TB:2 * TB].unsqueeze(1).broadcast_to([P, DT, TB]), ALU.mult)\
                .then_inc(sem("inp"), 1)

        def scan_dve(dve, it, n):
            if n % 2 == 0:
                if n // 2 + 1 < DS:
                    scan_inputs(dve, it, n // 2 + 1)
            else:
                run_state(dve, it, n // 2)

        def run_state(dve, it, n):
            dve.wait_ge(sem("decay"), it * DS + n + 1)
            dve.wait_ge(sem("carried"), it * DS + n + 1)
            dve.tensor_tensor_scan(st[:, n % 4].rearrange("p k t -> p (k t)"), dec[:, n % 2].rearrange("p k t -> p (k t)"), st[:, n % 4].rearrange("p k t -> p (k t)"), 0.0,
                                   ALU.mult, ALU.add).then_inc(sem("scanned"), 1)
            dve.wait_ge(sem("scanned"), it * DS + n + 1)
            dve.tensor_copy(last[:, (DS + n) * DT:(DS + n + 1) * DT], st[:, n % 4, :, TB])\
                .then_inc(sem("saved"), 1)

        def scan_pool(pool, it, n):
            if n % 2 == 1:
                read_state(pool, it, n // 2)

        def read_state(pool, it, n):
            pool.wait_ge(sem("saved"), it * DS + n + 1)
            pool.wait_ge(sem("q_rows"), it * (DS // 2) + n // 2 + 1)
            q = qb[:, (n // 2) % 2, (n % 2) * TB:(n % 2 + 1) * TB]
            pool.tensor_tensor(st[:, n % 4, :, 1:], st[:, n % 4, :, 1:], q.unsqueeze(1).broadcast_to([P, DT, TB]),
                               ALU.mult).then_inc(sem("read_out"), 1)
            if n % 2 == 1:
                pool.wait_ge(sem("read_out"), it * DS + n + 1)
                pool.tensor_tensor(st[:, n % 4, :, 1:], st[:, n % 4, :, 1:], st[:, (n - 1) % 4, :, 1:], ALU.add)\
                    .then_inc(sem("paired"), 1)

        def back_pe(pe, it, n, front):
            if n == 7:
                if front is not None:
                    pe.wait_ge(sem("ffn_s"), front + 1)
                else:
                    pe.wait_ge(sem("ksum"), NB + 1)
                pe.wait_ge(sem("yz"), it + 1)
                opf = oproj_g[:, :, :, :].rearrange("p b k n -> p (b k n)")
                for t in range(NT):
                    for k in range(DT):
                        i = pe.matmul(pB[:, t * D:(t + 1) * D], tmp[:, k, t * P:(t + 1) * P],
                                      opf[:, bass.ds((batch(it) * DT + k) * D, D)],
                                      start=(k == 0), stop=(k == DT - 1))
                i.then_inc(sem("out_mm"), 1)
            if n == 17:
                if front is not None:
                    pe.wait_ge(sem("sz"), front * 2 + 2)
                turn(pe, it, "d", xnC, pB)
            if n == 19:
                pe.wait_ge(sem("hT_d"), (it + 1) * DC)
                for t in range(NT):
                    for c in range(DC):
                        i = pe.matmul(pB[:, t * E:(t + 1) * E], hB[:, c, t * P:(t + 1) * P], gate[:, c, :],
                                      start=(c == 0), stop=(c == DC - 1))
                i.then_inc(sem("score_mm"), 1)

        def back_act(act, it, n, front):
            if n == 17:
                if front is not None:
                    act.wait_ge(sem("in_mm"), front * 4 + 4)
                modulate(act, it, "d", pB, col1, 4, 3, hB)
            if n == 19:
                act.wait_ge(sem("score_mm"), it + 1)
                act.activation(scores[:, bass.ds((it - 1) * (NT * E), NT * E)], pB[:, 0:NT * E], ACT.Copy)\
                    .then_inc(sem("scores"), 1)

        def back_dve(dve, it, n):
            if n == 1:
                dve.wait_ge(sem("summed"), (it + 1) * (DS // 2))
                dve.tensor_tensor(tmp[:, :, :], pY[:, :, :], wide(turn2(sz, it, DT * TB)), ALU.mult)\
                    .then_inc(sem("yz"), 1)
            if n == 8:
                dve.wait_ge(sem("out_mm"), it + 1)
                dve.wait_ge(sem("x_out"), it * 16)
                dve.tensor_tensor(flat(xo[:, :, :]), x_at(it, 0, NT), pB[:, :], ALU.add).then_inc(sem("x_scan"), 1)
                settled(dve)
                dve.wait_ge(sem("x_scan"), it + 1)
                ln_stats(dve, it, "d", lambda t: xo[:, t, :])
            if n == 9:
                dve.wait_ge(sem("rows_out"), it * 16)
                after(dve, "turn_d", it)
                ln_rows(dve, it, "d", lambda t: xo[:, t, :], xnC)

        def blocks_of(i, stages):
            return [i + d if s in stages else None for s, d in (("A", 2), ("F", 1), ("S", 0), ("C", -1))]

        def turn_pe(pe, i, stages):
            a, f, s, c = blocks_of(i, stages)
            for n in range(2 * DS):
                if s is not None:
                    scan_pe(pe, s, n)
                if c is not None:
                    back_pe(pe, c, n, f)
                if f is not None:
                    front_pe(pe, f, n, c)
                if a is not None:
                    attn_pe(pe, a, n)

        def turn_act(act, i, stages):
            a, f, s, c = blocks_of(i, stages)
            for n in range(2 * DS):
                if s is not None:
                    scan_act(act, s, n)
                if c is not None:
                    back_act(act, c, n, f)
                if f is not None:
                    front_act(act, f, n)
                if a is not None:
                    attn_act(act, a, n)

        def turn_dve(dve, i, stages):
            a, f, s, c = blocks_of(i, stages)
            for n in range(2 * DS):
                if s is not None:
                    scan_dve(dve, s, n)
                if c is not None:
                    back_dve(dve, c, n)
                if f is not None:
                    front_dve(dve, f, n, c)
                if a is not None:
                    attn_dve(dve, a, n)

        def turn_pool(pool, i, stages):
            a, f, s, c = blocks_of(i, stages)
            for n in range(2 * DS):
                if s is not None:
                    scan_pool(pool, s, n)
                if c is not None and n == 7:
                    ln_pool(pool, c, "d")
                if f is not None:
                    front_pool(pool, f, n, c)
                if a is not None:
                    attn_pool(pool, a, n)

        def pipeline(eng, a_turn):
            a_turn(eng, -1, "A")
            a_turn(eng, 0, "AF")
            a_turn(eng, 1, "AFS")
            with eng.Fori(2, NB - 1) as i:
                a_turn(eng, i, "AFSC")
            a_turn(eng, NB - 1, "FSC")
            a_turn(eng, NB, "SC")
            a_turn(eng, NB + 1, "C")

        with nc.Block() as block:
            @block.sync
            def _(sp):
                def load(it):
                    sp.dma_start(x_at(it, 0, NT).rearrange("p (t n) -> p t n", n=D),
                                 x_rows[bass.ds((it - 1) * TB, TB), :].rearrange("(t p) n -> p t n", p=P))\
                        .then_inc(sem("x_in"), 16)

                def store(it):
                    sp.wait_ge(sem("x_scan"), it + 1)
                    sp.dma_start(out_rows[bass.ds((it - 1) * TB, TB), :].rearrange("(t p) n -> p t n", p=P),
                                 xo[:, :, :]).then_inc(sem("x_out"), 16)
                    sp.wait_ge(sem("lnd_rows"), it + 1)
                    sp.dma_start(xn_d[bass.ds((it - 1) * TB, TB), :].rearrange("(t p) n -> p t n", p=P),
                                 xnC[:, :, :]).then_inc(sem("rows_out"), 16)

                load(1)
                for it in (2, 3):
                    sp.wait_ge(sem("x_in"), it * 16)
                    load(it)
                with sp.Fori(1, NB - XBUF + 2) as it:
                    sp.wait_ge(sem("x_in"), (it + XBUF - 1) * 16)
                    load(it + XBUF - 1)
                    store(it)
                for it in range(NB - XBUF + 2, NB + 1):
                    store(it)
                sp.wait_ge(sem("x_out"), (NB + 1) * 16)
                sp.wait_ge(sem("rows_out"), (NB + 1) * 16)

            @block.tensor
            def _(pe):
                pipeline(pe, turn_pe)

            @block.scalar
            def _(act):
                act.wait_ge(sem("tail0"), 2)
                pipeline(act, turn_act)

            @block.vector
            def _(dve):
                dve.memset(att[:, :, :, :], 0.0)
                dve.memset(vh[:, :, :, :], 0.0)
                dve.memset(S[:, 0, :], 0.0)
                for n in range(2):
                    dve.memset(dec[:, n, :, 0:1], 0.0)
                dve.memset(tail[:, 0:DT * (DCV - 1)], 0.0).then_inc(sem("tail0"), 1)
                dve.memset(last[:, 0:DS * DT], 0.0).then_inc(sem("tail0"), 1)
                dve.wait_ge(sem("tail0"), 2)
                pipeline(dve, turn_dve)

            @block.gpsimd
            def _(pool):
                pipeline(pool, turn_pool)


def experts(nc, sem, consts, w1_d, w2_d, out_rows, xn_d, scores, ones_s, ident_s, col1, gb1):
    with ExitStack() as ctx:
        def sb(name, shape, dt=F32):
            return ctx.enter_context(nc.sbuf_tensor(name, shape, dt))

        def ps(name, shape, dt=F32):
            return ctx.enter_context(nc.psum_tensor(name, shape, dt))

        def chain(eng, instruction, s):
            count[s] = count.get(s, 0) + 1
            instruction.then_inc(sem(s), 1)
            eng.wait_ge(sem(s), count[s])

        count = {}
        LT = NL * TT
        LOOKS = BITS // 2
        PARTS = 5
        WQ = 2 * DC * F // K
        samelist = sb("samelist", [P, P])
        segbefore = sb("segbefore", [P, P])
        iota = sb("iota", [P, P])
        token = sb("token", [P, 2, LT])
        bitsf = sb("bitsf", [P, 3 * LOOKS])
        bitsu = sb("bitsu", [P, 3 * LOOKS], U32)
        red = sb("red", [P, B * TT])
        prob = sb("prob", [P, B * TT, E])
        pl = sb("pl", [P, LT])
        seg = sb("seg", [P, SW])
        thr = sb("thr", [P, 1], U32)
        cand = sb("cand", [P, 3], U32)
        hit = sb("hit", [P, 3, SW])
        cnt = sb("cnt", [P, 3])
        passed = sb("passed", [P, 3])
        step = sb("step", [P, 1], U32)
        run = sb("run", [P, SW])
        offset = sb("offset", [P, 2])
        need = sb("need", [P, 1])
        posi = sb("posi", [P, LT], I32)
        loi = sb("loi", [P, LT], I32)
        lo = sb("lo", [P, LT])
        hi = sb("hi", [P, LT])
        rest = sb("rest", [P, LT])
        value = sb("value", [P, PARTS, LT], BF16)
        what = sb("what", [P, LT * PARTS * SL], BF16)
        entries = sb("entries", [P, 2, TT * PARTS * SL], BF16)
        onehot = sb("onehot", [P, 2, TT, P], BF16)
        gates = sb("gates", [P, NL * SL])
        ids = sb("ids", [P, NL * SL], U32)
        w_in = sb("w_in", [P, 2, DC * F])
        w_up = sb("w_up", [P, 2, 2, DC * F], F32R)
        w_rest = sb("w_rest", [P, 2, 2, DC * F], F32R)
        xg = sb("xg", [P, 2, SL, D])
        hg = sb("hg", [P, DC, K])
        hg_up = sb("hg_up", [P, DC, K], F32R)
        hg_rest = sb("hg_rest", [P, DC, K], F32R)
        h1 = sb("h1", [P, 4, K])
        masked = sb("masked", [P, WQ, K])
        h1_up = sb("h1_up", [P, FT, K], F32R)
        h1_rest = sb("h1_rest", [P, FT, K], F32R)
        ys = sb("ys", [P, 2, SL, D])
        pc = ps("pc", [P, 2, 512])
        pt = ps("pt", [P, 2, 512])
        ph = ps("ph", [P, 2, 512])
        po = ps("po", [P, 2, 512])

        def flat(x):
            return x.rearrange("p a b -> p (a b)")

        def by_tile(x, j):
            return x.rearrange("p (n j) -> p j n", j=ST)[:, j, :]

        ITEMS = NL // 4

        FIRST, PER_LIST = WQ + DC, FT + DC + WQ // 2

        def splits(i, n, ahead):
            no_weights = WQ // 2 if n == 3 and not ahead else 0
            return FIRST + (i - 1) * 4 * PER_LIST + n * PER_LIST - no_weights

        def ring(n, more):
            return (FIRST + n * PER_LIST + more) % 4

        def every_turn(eng, a_turn):
            with eng.Fori(1, ITEMS) as i:
                a_turn(eng, i, True)
            a_turn(eng, ITEMS, False)

        with nc.Block() as block:
            @block.sync
            def _(sp):
                def load(e):
                    for n, w_d in enumerate((w1_d, w2_d)):
                        sp.dma_start(w_in[:, n].rearrange("p (c f) -> p c f", c=w_d.shape[1] // P),
                                     w_d[bass.ds(e, 1)].rearrange("e (c p) f -> p (e c) f", p=P))\
                            .then_inc(sem("w_in"), 16)

                for name, dst in (("bitsf", bitsf[:, :]), ("samelist", samelist[:, :]),
                                  ("segbefore", segbefore[:, :]), ("iota", iota[:, :]),
                                  ("token", token[:, :, :].rearrange("p a n -> p (a n)"))):
                    a, n = CONST_AT[name]
                    sp.dma_start(dst, consts[:, a:a + n]).then_inc(sem("const2_in"), 16)
                load(0)
                with sp.Fori(1, E) as e:
                    sp.wait_ge(sem("w_split"), e * WQ)
                    load(e)

            @block.vector
            def _(dve):
                def do(instruction):
                    chain(dve, instruction, "sel_step")

                sc = scores[:, :].rearrange("p (t e) -> p t e", e=E)
                do(dve.tensor_reduce(red[:, :], sc, AX_X, ALU.max))
                do(dve.tensor_tensor(sc, sc, red[:, :].unsqueeze(2).broadcast_to([P, B * TT, E]), ALU.subtract))
                dve.wait_ge(sem("const2_in"), 80)
                dve.tensor_copy(bitsu[:, :], bitsf[:, :])
                do(dve.memset(thr[:, :], 0))
                dve.wait_ge(sem("prob_exp"), 1)
                do(dve.tensor_reduce(red[:, :], prob[:, :, :], AX_X, ALU.add))
                do(dve.reciprocal(red[:, :], red[:, :]))
                for b in range(B):
                    i = dve.tensor_tensor(
                        pl[:, :].rearrange("p (e b t) -> p b e t", b=B, t=TT)[:, b],
                        prob[:, b * TT:(b + 1) * TT, :].rearrange("p t e -> p e t"),
                        red[:, b * TT:(b + 1) * TT].unsqueeze(1).broadcast_to([P, E, TT]), ALU.mult)
                i.then_inc(sem("selected"), 1)
                dve.wait_ge(sem("seg_mm"), 1)
                do(dve.tensor_copy(seg[:, :].rearrange("p (j n) -> p j n", j=ST), pt[:, :, 0:P]))
                def look(i, q):
                    dve.tensor_tensor(cand[:, :], thr[:, :].broadcast_to([P, 3]), bitsu[:, bass.ds(i * 3, 3)],
                                      ALU.bitwise_or).then_inc(sem("t_look"), 1)
                    dve.wait_ge(sem("t_look"), i * 5 + 1)
                    for j in range(3):
                        last = dve.tensor_scalar(hit[:, j, :], seg[:, :], cand[:, j:j + 1].bitcast(F32), None, ALU.is_ge)
                    last.then_inc(sem("t_look"), 1)
                    dve.wait_ge(sem("t_look"), i * 5 + 2)
                    dve.tensor_reduce(cnt[:, :], hit[:, :, :], AX_X, ALU.add).then_inc(sem("t_cnt"), 1)
                    if q is not None:
                        whole, to = (x[:, bass.ds(q * K, K)] for x in (flat(w_in[:, :, :]), flat(masked[:, :, :])))
                        dve.tensor_scalar(to.bitcast(I32), whole.bitcast(I32), UPPER, None, ALU.bitwise_and)\
                            .then_inc(sem("masked"), 1)
                        dve.wait_ge(sem("masked"), q + 1)
                        dve.tensor_tensor(flat(w_rest[:, 0])[:, bass.ds(q * K, K)], whole, to, ALU.subtract)\
                            .then_inc(sem("w_split"), 1)
                    dve.wait_ge(sem("t_all"), i + 1)
                    dve.tensor_scalar(passed[:, :], pc[:, 0, 0:3], float(K), bitsf[:, bass.ds(i * 3, 1)],
                                      ALU.is_ge, ALU.mult).then_inc(sem("t_look"), 1)
                    dve.wait_ge(sem("t_look"), i * 5 + 3)
                    with nc.allow_low_precision(reason="at most 3 at two bits: exact"):
                        dve.tensor_reduce(step[:, :], passed[:, :], AX_X, ALU.add).then_inc(sem("t_look"), 1)
                    dve.wait_ge(sem("t_look"), i * 5 + 4)
                    dve.tensor_tensor(thr[:, :], thr[:, :], step[:, :], ALU.bitwise_or).then_inc(sem("t_look"), 1)
                    dve.wait_ge(sem("t_look"), i * 5 + 5)

                with dve.Fori(0, LOOKS - WQ) as i:
                    look(i, None)
                dve.wait_ge(sem("w_in"), 32)
                with dve.Fori(LOOKS - WQ, LOOKS) as i:
                    look(i, i - (LOOKS - WQ))
                above, equal, marked = (hit[:, j, :] for j in range(3))
                tf = thr[:, :].bitcast(F32)
                dve.tensor_scalar(above, seg[:, :], tf, None, ALU.is_gt)
                do(dve.tensor_scalar(equal, seg[:, :], tf, None, ALU.is_equal))
                dve.tensor_reduce(cnt[:, 0:2], hit[:, 0:2, :], AX_X, ALU.add).then_inc(sem("selected"), 1)

                def counted(marks, column, n):
                    dve.tensor_tensor_scan(run[:, :], ones_s[:, 0:1].broadcast_to([P, SW]), marks, 0.0,
                                           ALU.mult, ALU.add)
                    dve.wait_ge(sem("prefix"), n)
                    do(dve.tensor_copy(offset[:, 0:1], pc[:, 1, column:column + 1]))

                counted(equal, 1, 1)
                do(dve.tensor_scalar(need[:, :], pc[:, 0, 0:1], -1.0, float(K), ALU.mult, ALU.add))
                do(dve.tensor_scalar(run[:, :], run[:, :], offset[:, 0:1], need[:, :], ALU.add, ALU.is_le))
                do(dve.tensor_tensor(marked, run[:, :], equal, ALU.mult))
                do(dve.tensor_tensor(marked, marked, above, ALU.add))
                dve.tensor_reduce(cnt[:, 2:3], marked, AX_X, ALU.add).then_inc(sem("selected"), 1)
                counted(marked, 2, 2)
                dve.scalar_tensor_tensor(run[:, :], run[:, :], offset[:, 0:1], marked, ALU.add, ALU.mult)\
                    .then_inc(sem("selected"), 1)
                do(dve.tensor_copy(value[:, 2, :], pl[:, :]))
                do(dve.tensor_tensor(rest[:, :], pl[:, :], value[:, 2, :], ALU.subtract))
                do(dve.tensor_copy(value[:, 3, :], rest[:, :]))
                do(dve.tensor_tensor(value[:, 4, :], rest[:, :], value[:, 3, :], ALU.subtract))
                dve.tensor_copy(value[:, 0:2, :], token[:, :, :])
                dve.wait_ge(sem("rank_mm"), 1)
                do(dve.tensor_scalar(posi[:, :].rearrange("p (n j) -> p j n", j=ST), pt[:, :, 0:P], -1.0, None,
                                     ALU.add))
                do(dve.tensor_scalar(loi[:, :], posi[:, :], P - 1, None, ALU.bitwise_and))
                do(dve.tensor_copy(lo[:, :], loi[:, :]))
                do(dve.tensor_scalar(loi[:, :], posi[:, :], 7, None, ALU.arith_shift_right))
                do(dve.tensor_copy(hi[:, :], loi[:, :]))
                wv = what[:, :].rearrange("p (n a c) -> p n a c", a=PARTS, c=SL)
                for a in range(PARTS):
                    for c in range(SL):
                        i = dve.scalar_tensor_tensor(wv[:, :, a, c], hi[:, :], float(c), value[:, a, :],
                                                     ALU.is_equal, ALU.mult)
                i.then_inc(sem("what"), 1)
                dve.wait_ge(sem("what"), 1)

                def place(k, m):
                    if not (isinstance(k, int) and k < 2):
                        dve.wait_ge(sem("slot_mm"), k - 1)
                    dve.tensor_copy(entries[:, m % 2], what[:, bass.ds(k * TT * PARTS * SL, TT * PARTS * SL)])
                    dve.tensor_tensor(onehot[:, m % 2], iota[:, :].unsqueeze(1).broadcast_to([P, TT, P]),
                                      lo[:, bass.ds(k * TT, TT)].unsqueeze(2).broadcast_to([P, TT, P]), ALU.is_equal)\
                        .then_inc(sem("onehot"), 1)

                def slots_of(k, m):
                    sums = pc[:, m % 2, 0:PARTS * SL].rearrange("p (a c) -> p c a", c=SL)
                    dve.wait_ge(sem("slot_mm"), k + 1)
                    with nc.allow_low_precision(reason="whole numbers below 2 ** 24: exact"):
                        dve.tensor_reduce(ids[:, bass.ds(k * SL, SL)], sums[:, :, 0:2], AX_X, ALU.add)
                    dve.tensor_reduce(gates[:, bass.ds(k * SL, SL)], sums[:, :, 2:PARTS], AX_X, ALU.add)\
                        .then_inc(sem("ids"), 1)

                def split(whole, rest, done, count, slot):
                    to = masked[:, slot, :]
                    if not (isinstance(count, int) and count <= 4):
                        dve.wait_ge(sem("upper"), count - 4)
                    dve.tensor_scalar(to.bitcast(I32), whole.bitcast(I32), UPPER, None, ALU.bitwise_and)\
                        .then_inc(sem("masked"), 1)
                    dve.wait_ge(sem("masked"), count)
                    dve.tensor_tensor(rest, whole, to, ALU.subtract).then_inc(sem(done), 1)

                h = DC * F // 4

                def split_weights(slot, q, count, at_ring):
                    n, at = q // 4, (q % 4) * h
                    split(w_in[:, n, at:at + h], w_rest[:, slot, n, at:at + h], "w_split", count, at_ring)

                place(0, 0)
                for m in range(4):
                    if m < 3:
                        place(m + 1, m + 1)
                    slots_of(m, m)
                for c in range(DC):
                    dve.wait_ge(sem("hg"), PER_TURN["hg"] + c + 1)
                    split(hg[:, c, :], hg_rest[:, c, :], "hg_split", WQ + c + 1, (WQ + c) % 4)

                def a_turn(dve, i, ahead):
                    for n in range(4):
                        b = n % 2
                        last_list = n == 3 and not ahead
                        for f in range(FT):
                            dve.wait_ge(sem("gelu"), i * 4 * FT + n * FT + f + 1)
                            if f == 0:
                                dve.wait_ge(sem("down_mm"), i * 4 * SL + n * SL)
                            split(h1[:, f % 4, :], h1_rest[:, f, :], "h1_split", splits(i, n, ahead) + f + 1,
                                  ring(n, f))
                        if not last_list:
                            for c in range(DC):
                                dve.wait_ge(sem("hg"), (i * 4 + n + 1) * DC + c + 1)
                                split(hg[:, c, :], hg_rest[:, c, :], "hg_split", splits(i, n, ahead) + FT + c + 1,
                                      ring(n, FT + c))
                        for c in range(SL):
                            dve.wait_ge(sem("down_mm"), i * 4 * SL + n * SL + c + 1)
                            if c == 0:
                                dve.wait_ge(sem("ys_free"), (i - 1) * 4 + n + 1)
                            dve.scalar_tensor_tensor(
                                ys[:, b, c, :], po[:, c % 2, 0:D],
                                gates[:, bass.ds((i - 1) * 4 * SL + n * SL + c, 1)],
                                gb1[:, b * D:(b + 1) * D], ALU.mult, ALU.mult).then_inc(sem("scaled"), 1)
                            if ahead or n < 2:
                                if n % 2 == 0 and c == 0:
                                    dve.wait_ge(sem("w_in"), (i - 1) * 64 + 64 + n // 2 * 32)
                                for q in ((0, 1), (2,), (3,), ())[c]:
                                    split_weights(1 - n // 2, n % 2 * (WQ // 2) + q,
                                                  splits(i, n, ahead) + FT + DC + q + 1, ring(n, FT + DC + q))
                            if n % 2 == 1 and ahead and c < 2:
                                place(i * 4 + n - 1 + c, c)
                        if n % 2 == 1 and ahead:
                            for c in range(2):
                                slots_of(i * 4 + n - 1 + c, c)

                every_turn(dve, a_turn)

            @block.scalar
            def _(act):
                act.wait_ge(sem("sel_step"), 2)
                act.activation(prob[:, :, :].rearrange("p t e -> p (t e)"), scores[:, :], ACT.Exp)\
                    .then_inc(sem("prob_exp"), 1)

                def put(to, count, at_ring):
                    act.wait_ge(sem("masked"), count)
                    act.activation(to, masked[:, at_ring, :], ACT.Copy).then_inc(sem("upper"), 1)

                def put_weights(slot, q, count, at_ring):
                    n, at = q // 4, (q % 4) * K
                    put(w_up[:, slot, n, at:at + K], count, at_ring)

                def modulated(k_count, b):
                    for c in range(DC):
                        act.wait_ge(sem("gt_mm"), k_count + c + 1)
                        sc, sh = ((what * DC + c) * B + b for what in (4, 3))
                        act.activation(hg[:, c, :], pt[:, c, :], ACT.Identity, bias=col1[:, sh:sh + 1],
                                       scale=col1[:, sc:sc + 1]).then_inc(sem("hg"), 1)

                def a_turn(act, i, ahead):
                    for n in range(4):
                        for f in range(FT):
                            act.wait_ge(sem("up_mm"), i * 4 * FT + n * FT + f + 1)
                            act.wait_ge(sem("h1_split"), i * 4 * FT + n * FT + f - 3)
                            act.activation(h1[:, f % 4, :], ph[:, f % 2, :], ACT.Gelu).then_inc(sem("gelu"), 1)
                            if f > 0:
                                put(h1_up[:, f - 1, :], splits(i, n, ahead) + f, ring(n, f - 1))
                        put(h1_up[:, FT - 1, :], splits(i, n, ahead) + FT, ring(n, FT - 1))
                        if ahead or n < 3:
                            modulated((i * 4 + n + 1) * DC, (n + 1) % 2)
                            for c in range(DC):
                                put(hg_up[:, c, :], splits(i, n, ahead) + FT + c + 1, ring(n, FT + c))
                        if ahead or n < 2:
                            for q in range(WQ // 2):
                                put_weights(1 - n // 2, n % 2 * (WQ // 2) + q, splits(i, n, ahead) + FT + DC + q + 1,
                                            ring(n, FT + DC + q))

                with act.Fori(0, WQ) as q:
                    act.wait_ge(sem("masked"), q + 1)
                    act.activation(flat(w_up[:, 0])[:, bass.ds(q * K, K)], flat(masked[:, :, :])[:, bass.ds(q * K, K)],
                                   ACT.Copy).then_inc(sem("upper"), 1)
                modulated(PER_TURN["gt_mm"], 0)
                for c in range(DC):
                    put(hg_up[:, c, :], WQ + c + 1, (WQ + c) % 4)
                every_turn(act, a_turn)

            @block.tensor
            def _(pe):
                pe.wait_ge(sem("selected"), 1)
                for j in range(ST):
                    m = pe.transpose(pt[:, j, 0:P], by_tile(pl[:, :], j), ident_s[:, :])
                m.then_inc(sem("seg_mm"), 1)
                with pe.Fori(0, LOOKS) as i:
                    pe.wait_ge(sem("t_cnt"), i + 1)
                    pe.matmul(pc[:, 0, 0:3], samelist[:, :], cnt[:, :], start=True, stop=True).then_inc(sem("t_all"), 1)
                pe.wait_ge(sem("selected"), 2)
                pe.wait_ge(sem("t_look"), LOOKS * 5)
                pe.matmul(pc[:, 0, 0:1], samelist[:, :], cnt[:, 0:1], start=True, stop=True)
                pe.matmul(pc[:, 1, 1:2], segbefore[:, :], cnt[:, 1:2], start=True, stop=True).then_inc(sem("prefix"), 1)
                pe.wait_ge(sem("selected"), 3)
                pe.matmul(pc[:, 1, 2:3], segbefore[:, :], cnt[:, 2:3], start=True, stop=True).then_inc(sem("prefix"), 1)
                pe.wait_ge(sem("selected"), 4)
                for j in range(ST):
                    m = pe.transpose(pt[:, j, 0:P], run[:, j * P:(j + 1) * P], ident_s[:, :])
                m.then_inc(sem("rank_mm"), 1)
                pe.wait_ge(sem("what"), 1)

                def slots_of(k, m):
                    pe.wait_ge(sem("onehot"), k + 1)
                    if not (isinstance(k, int) and k < 2):
                        pe.wait_ge(sem("ids"), k - 1)
                    for t in range(TT):
                        last = pe.matmul(pc[:, m % 2, 0:PARTS * SL], onehot[:, m % 2, t, :],
                                         entries[:, m % 2, t * PARTS * SL:(t + 1) * PARTS * SL], start=(t == 0), stop=(t == TT - 1))
                    last.then_inc(sem("slot_mm"), 1)

                def turned(gathered, b):
                    pe.wait_ge(sem(f"rows_in{b}"), gathered * SL * 16)
                    for c in range(DC):
                        for s in range(SL):
                            m = pe.transpose(pt[:, c, s * P:(s + 1) * P], xg[:, b, s, c * P:(c + 1) * P], ident_s[:, :])
                        m.then_inc(sem("gt_mm"), 1)

                for m in range(4):
                    slots_of(m, m)
                turned(1, 0)

                upper, rest = (lambda x, y: x), (lambda x, y: y)

                def in_parts(to, chunks, stationary, moving):
                    terms = [(c, parts) for c in range(chunks) for parts in ((upper, upper), (upper, rest), (rest, upper))]
                    for n, (c, (p0, p1)) in enumerate(terms):
                        m = pe.matmul(to, stationary(c, p0), moving(c, p1),
                                      start=(n == 0), stop=(n == len(terms) - 1))
                    return m

                def a_turn(pe, i, ahead):
                    for n in range(4):
                        e2, b = n // 2, n % 2
                        pe.wait_ge(sem("hg_split"), (i * 4 + n + 1) * DC)
                        if b == 0:
                            pe.wait_ge(sem("w_split"), (i - 1) * 2 * WQ + (e2 + 1) * WQ)
                        pe.wait_ge(sem("upper"), splits(i, n, ahead))
                        for f in range(FT):
                            pe.wait_ge(sem("gelu"), i * 4 * FT + n * FT + f - 1)
                            m = in_parts(ph[:, f % 2, :], DC, lambda c, part: part(w_up, w_rest)[
                                :, e2, 0, c * F + f * P:c * F + (f + 1) * P],
                                lambda c, part: part(hg_up, hg_rest)[:, c, :])
                            m.then_inc(sem("up_mm"), 1)
                        if ahead or n < 3:
                            turned((i - 1) * 2 + (n + 1) // 2 + 1, (n + 1) % 2)
                        pe.wait_ge(sem("h1_split"), i * 4 * FT + (n + 1) * FT)
                        pe.wait_ge(sem("upper"), splits(i, n, ahead) + FT)
                        for s in range(SL):
                            pe.wait_ge(sem("scaled"), i * 4 * SL + n * SL + s - 1)
                            m = in_parts(po[:, s % 2, 0:D], FT,
                                         lambda f, part: part(h1_up, h1_rest)[:, f, s * P:(s + 1) * P],
                                         lambda f, part: part(w_up, w_rest)[:, e2, 1, f * D:(f + 1) * D])
                            m.then_inc(sem("down_mm"), 1)
                        if ahead and n % 2 == 1:
                            for c in range(2):
                                slots_of(i * 4 + n - 1 + c, c)

                every_turn(pe, a_turn)

            @block.gpsimd
            def _(pool):
                def gather(k):
                    b = k % 2
                    pool.wait_ge(sem("ids"), k + 1)
                    for s in range(SL):
                        pool.indirect_dma_start(
                            xg[:, b, s, :], None, xn_d[:, :],
                            bass.IndirectOffsetOnAxis(ap=ids[:, k * SL + s:k * SL + s + 1], axis=0))\
                            .then_inc(sem(f"rows_in{b}"), 16)

                def scatter(k):
                    b = k % 2
                    pool.wait_ge(sem("scaled"), PER_TURN["scaled"] + (k + 1) * SL)
                    for s in range(SL):
                        pool.indirect_dma_start(
                            out_rows, bass.IndirectOffsetOnAxis(ap=ids[:, k * SL + s:k * SL + s + 1], axis=0),
                            ys[:, b, s, :], None, compute_op=ALU.add).then_inc(sem(f"added{b}"), 16)

                gather(0)
                gather(1)
                for k in range(NL):
                    if k >= 2:
                        pool.wait_ge(sem(f"added{k % 2}"), k // 2 * SL * 16)
                    pool.sem_inc(sem("ys_free"), 1)
                    if k + 2 < NL:
                        pool.wait_ge(sem("gt_mm"), PER_TURN["gt_mm"] + (k + 1) * DC)
                        gather(k + 2)
                    scatter(k)
                for b in range(B):
                    pool.wait_ge(sem(f"added{b}"), E * SL * 16)


def rows_of_chunks(a):
    n = a.shape[1]
    c = -(-a.shape[0] // P)
    full = np.zeros((c * P, n), np.float32)
    full[:a.shape[0]] = a
    return full.reshape(c, P, n).transpose(1, 0, 2).reshape(P, c * n)


def kernel(**inputs):
    import concourse.bacc as _bacc
    from concourse.bass_utils import run_bass_kernel_spmd as _run

    a = {k: np.asarray(v) for k, v in inputs.items()}
    col = lambda x: x.reshape(-1, P).T
    two = lambda x: np.concatenate([x, x], axis=-1)

    def pair(x):
        return np.concatenate([x[:, 0::2], x[:, 1::2]], axis=0)

    wt = {
        "wq": rows_of_chunks(a["L0_attn_Wq"]), "wk": rows_of_chunks(a["L0_attn_Wk"]),
        "wv": rows_of_chunks(a["L0_attn_Wv"]), "wg": rows_of_chunks(a["L0_attn_Wg"]),
        "wgk1": rows_of_chunks(a["L0_attn_Wgk1"]), "wgk2": rows_of_chunks(a["L0_attn_Wgk2"]),
        "win2": rows_of_chunks(two(a["L0_ffn_Win"])), "inproj": rows_of_chunks(a["L1_attn_in_proj_w"].T),
        "xproj": rows_of_chunks(a["L1_attn_x_proj_w"].T), "dthead": rows_of_chunks(a["L1_attn_dt_head_w"].T),
        "gate": rows_of_chunks(a["L1_ffn_gate_w"].T), "bgk2": col(a["L0_attn_bgk2"]),
        "bin": two(a["L0_ffn_bin_"])[:, None], "w1": pair(a["L0_ffn_W1"]), "b1": pair(a["L0_ffn_b1"]),
        "w2": pair(a["L0_ffn_W2"]),
        "b2": np.concatenate([a["L0_ffn_b2"], np.zeros(FM, np.float32)])[:, None],
        "convw": a["L1_attn_conv_w"].reshape(DT, P, DCV).transpose(1, 0, 2).reshape(P, DT * DCV),
        "convb": col(a["L1_attn_conv_b"]), "dtb": col(a["L1_attn_dt_head_b"]), "dskip": col(a["L1_attn_D"]),
        "gnw": two(a["L0_attn_gnw"])[:, None],
    }
    fd = {
        "wo": rows_of_chunks(a["L0_attn_Wo"]),
        "wout2": np.concatenate([a["L0_ffn_Wout"], a["L0_ffn_Wout"]], axis=0),
        "bout": rows_of_chunks(a["L0_ffn_bout"][None, :]),
        "outproj": rows_of_chunks(a["L1_attn_out_proj_w"].T),
        "c0": rows_of_chunks(a["L0_c"].T), "c1": rows_of_chunks(a["L1_c"].T),
    }
    cs = shape_constants()
    packed = lambda sizes, parts: np.ascontiguousarray(np.concatenate([parts[n] for n, _ in sizes], axis=1))
    arrays = {
        "x_in": a["L0_attn_x"], "consts": packed(CONST_SIZES, cs), "weights": packed(WEIGHT_SIZES, wt),
        "folds": packed(FOLD_SIZES, fd), "wmod0": a["L0_wmod"], "wmod1": a["L1_wmod"],
        "w1_d": a["L1_ffn_w1"], "w2_d": a["L1_ffn_w2"],
    }
    nc = _bacc.Bacc("TRN2", target_bir_lowering=False, num_devices=1)
    args = [nc.dram_tensor(n, v.shape, mybir.dt.from_np(v.dtype), kind="ExternalInput").ap() for n, v in arrays.items()]
    args.append(nc.dram_tensor("y_out", (B, T, D), F32, kind="ExternalOutput").ap())
    build(nc, *args)
    r = _run(nc, [arrays], core_ids=[0])
    return r.results[0]["y_out"]
```
